# Optimizing a Trainium2 kernel written in Bass

```python
import numpy as np
import jax
import jax.numpy as jnp

def _softmax(x, axis=-1):
    return jax.nn.softmax(x, axis=axis)

def _gelu(x):
    return jax.nn.gelu(x, approximate=True)

def _silu(x):
    return jax.nn.silu(x)

def _sigmoid(x):
    return jax.nn.sigmoid(x)

def _layernorm(x, axis=-1, eps=1e-05):
    m = jnp.mean(x, axis=axis, keepdims=True)
    v = jnp.var(x, axis=axis, keepdims=True)
    return (x - m) / jnp.sqrt(v + eps)

def _scatter_add(tgt, idx, src, axis=0):
    return tgt.at[idx].add(src)

def _segment_sum(src, seg, n):
    return jax.ops.segment_sum(src, seg, n)
kernel_name = 'mk_flamingo_gated_d2_seqx_r8_4e25d2'

def setup_inputs(seed: int=0):
    np.random.seed(seed)
    _w = jnp.asarray

    def _rec_inputs():
        import jax
        import jax.numpy as jnp
        _rk = jax.random.key(seed)
        x = -0.0002928 + 1 * jax.random.normal(jax.random.fold_in(_rk, 1), (64, 64, 128), jnp.float32)
        _lenS = 64 - jax.random.randint(jax.random.fold_in(_rk, 7), (64,), 0, max(1, 64 // 4) + 1, jnp.int32)
        _lenS2 = 64 - jax.random.randint(jax.random.fold_in(_rk, 8), (64,), 0, max(1, 64 // 4) + 1, jnp.int32)
        _ctx_1024P = jax.random.normal(jax.random.fold_in(_rk, 11), (64, 16, 128), jnp.float32)
        _ctx_1024c = jax.random.dirichlet(jax.random.fold_in(_rk, 511), 0.3 * jnp.ones((16,), jnp.float32), (64, 64))
        _ctx_1024t = jnp.einsum('bsk,bkd->bsd', _ctx_1024c, _ctx_1024P)
        _ctx_1024t = _ctx_1024t * jax.lax.rsqrt(jnp.mean(jnp.square(_ctx_1024t)) + 1e-12) * 0.953939
        ctx_1024 = -1.39393e-06 + 0.999914 * (_ctx_1024t + 0.3 * jax.random.normal(jax.random.fold_in(_rk, 611), (64, 64, 128), jnp.float32))
        _validS = jnp.arange(64)[None, :] < _lenS[:, None]
        _validS2 = jnp.arange(64)[None, :] < _lenS2[:, None]
        _causal = jnp.tril(jnp.ones((64, 64), dtype=bool))
        mask_BxSxS2_ff0 = jnp.where(jnp.ones((64, 64, 64), dtype=bool), 0.0, -1000000000.0).astype(jnp.float32)
        _g = jax.random.normal(jax.random.fold_in(_rk, 9001), (2, 2), jnp.float32)
        _g = jnp.sign(_g) * jnp.maximum(jnp.abs(_g), 1.0) + (_g == 0) * 1.0
        g_xattn = _g[0]
        g_ffn = _g[1]
        return (x, ctx_1024, mask_BxSxS2_ff0, g_xattn, g_ffn)
    x, ctx_1024, mask_BxSxS2_ff0, g_xattn, g_ffn = _rec_inputs()

    def _L0_xattn_setup():
        import jax, jax.numpy as jnp
        import numpy as np
        import math
        D = 128
        H = 16
        HD = D // H

        def _split_heads(x, B, L):
            return x.reshape(B, L, H, HD).transpose(0, 2, 1, 3)
        key = jax.random.key(seed)
        ks = jax.random.split(key, 12)
        B, L = (2, 256)
        s = 1.0 / math.sqrt(D)
        inp = {'q': jax.random.normal(ks[0], (B, L, D), jnp.float32), 'k': jax.random.normal(ks[1], (B, L, D), jnp.float32), 'v': jax.random.normal(ks[2], (B, L, D), jnp.float32), 'Wq': jax.random.normal(ks[3], (D, D), jnp.float32) * s, 'bq': jnp.zeros((D,), jnp.float32), 'Wk': jax.random.normal(ks[4], (D, D), jnp.float32) * s, 'bk': jnp.zeros((D,), jnp.float32), 'Wv': jax.random.normal(ks[5], (D, D), jnp.float32) * s, 'bv': jnp.zeros((D,), jnp.float32), 'Wo': jax.random.normal(ks[6], (D, D), jnp.float32) * s, 'bo': jnp.zeros((D,), jnp.float32), 'P': jax.random.normal(ks[7], (H, H), jnp.float32)}
        return inp
    _L0_xattn_all = _L0_xattn_setup()
    _L0_xattn_in = {k: v for k, v in _L0_xattn_all.items() if k in ('Wq', 'bq', 'Wk', 'bk', 'Wv', 'bv', 'Wo', 'bo', 'P')}
    del _L0_xattn_all

    def _L0_ffn_setup():
        import jax, jax.numpy as jnp
        import numpy as np
        B, S, D, F_DIM, E, TOPK = (2, 128, 128, 512, 8, 2)
        key = jax.random.key(seed)
        k0, k1, k2, k3 = jax.random.split(key, 4)
        hidden_states = jax.random.normal(k0, (B, S, D), dtype=jnp.float32)
        router_w = jax.random.normal(k1, (E, D), dtype=jnp.float32) * 0.02
        w1 = jax.random.normal(k2, (E, F_DIM, D), dtype=jnp.float32) * 0.02
        w2 = jax.random.normal(k3, (E, D, F_DIM), dtype=jnp.float32) * 0.02
        expert_scale = jnp.ones((E,), dtype=jnp.float32)
        return {'hidden_states': hidden_states, 'router_w': router_w, 'w1': w1, 'w2': w2, 'expert_scale': expert_scale}
    _L0_ffn_all = _L0_ffn_setup()
    _L0_ffn_in = {k: v for k, v in _L0_ffn_all.items() if k in ('router_w', 'w1', 'w2', 'expert_scale')}
    del _L0_ffn_all

    def _L1_xattn_setup():
        import jax, jax.numpy as jnp
        import numpy as np
        DIM = 128
        CTX_DIM = 128
        HEADS = 16
        DIM_HEAD = 64
        INNER = HEADS * DIM_HEAD
        FF_INNER = 4 * DIM
        EPS = 1e-05

        def layer_norm(x, g, b):
            mu = jnp.mean(x, axis=-1, keepdims=True)
            var = jnp.var(x, axis=-1, keepdims=True)
            return (x - mu) * jax.lax.rsqrt(var + EPS) * g + b
        key = jax.random.key(seed)
        ks = jax.random.split(key, 10)
        b, n, j = (2, 256, 256)
        x = jax.random.normal(ks[0], (b, n, DIM), dtype=jnp.float32)
        context = jax.random.normal(ks[1], (b, j, CTX_DIM), dtype=jnp.float32)
        mask = jnp.zeros((b, n, j), dtype=jnp.float32)
        s = 0.02
        Wq = jax.random.normal(ks[2], (DIM, INNER), dtype=jnp.float32) * s
        Wkv = jax.random.normal(ks[3], (CTX_DIM, 2 * DIM_HEAD), dtype=jnp.float32) * s
        Wout = jax.random.normal(ks[4], (INNER, DIM), dtype=jnp.float32) * s
        W1 = jax.random.normal(ks[5], (DIM, 2 * FF_INNER), dtype=jnp.float32) * s
        W2 = jax.random.normal(ks[6], (FF_INNER, DIM), dtype=jnp.float32) * s
        ln_g = jnp.ones((DIM,), jnp.float32)
        ln_b = jnp.zeros((DIM,), jnp.float32)
        cln_g = jnp.ones((CTX_DIM,), jnp.float32)
        cln_b = jnp.zeros((CTX_DIM,), jnp.float32)
        return {'x': x, 'context': context, 'mask': mask, 'ln_g': ln_g, 'ln_b': ln_b, 'cln_g': cln_g, 'cln_b': cln_b, 'Wq': Wq, 'Wkv': Wkv, 'Wout': Wout, 'W1': W1, 'W2': W2}
    _L1_xattn_all = _L1_xattn_setup()
    _L1_xattn_in = {k: v for k, v in _L1_xattn_all.items() if k in ('ln_g', 'ln_b', 'cln_g', 'cln_b', 'Wq', 'Wkv', 'Wout', 'W1', 'W2')}
    del _L1_xattn_all

    def _L1_ffn_setup():
        import jax, jax.numpy as jnp
        import numpy as np
        D_MODEL = 128
        D_FF = 352
        N_EXPERTS = 8
        key = jax.random.key(seed)
        k_in, k1, k2, k3 = jax.random.split(key, 4)
        scale = 0.02
        inputs = jax.random.normal(k_in, (4, N_EXPERTS * 256, D_MODEL), dtype=jnp.float32)
        w1 = jax.random.normal(k1, (N_EXPERTS, D_MODEL, D_FF), dtype=jnp.float32) * scale
        w3 = jax.random.normal(k3, (N_EXPERTS, D_MODEL, D_FF), dtype=jnp.float32) * scale
        w2 = jax.random.normal(k2, (N_EXPERTS, D_FF, D_MODEL), dtype=jnp.float32) * scale
        return {'inputs': inputs, 'w1': w1, 'w3': w3, 'w2': w2}
    _L1_ffn_all = _L1_ffn_setup()
    _L1_ffn_in = {k: v for k, v in _L1_ffn_all.items() if k in ('w1', 'w3', 'w2')}
    del _L1_ffn_all
    return {'x': x, 'ctx_1024': ctx_1024, 'mask_BxSxS2_ff0': mask_BxSxS2_ff0, 'g_xattn': g_xattn, 'g_ffn': g_ffn, 'L0_xattn_Wq': _L0_xattn_in['Wq'], 'L0_xattn_bq': _L0_xattn_in['bq'], 'L0_xattn_Wk': _L0_xattn_in['Wk'], 'L0_xattn_bk': _L0_xattn_in['bk'], 'L0_xattn_Wv': _L0_xattn_in['Wv'], 'L0_xattn_bv': _L0_xattn_in['bv'], 'L0_xattn_Wo': _L0_xattn_in['Wo'], 'L0_xattn_bo': _L0_xattn_in['bo'], 'L0_xattn_P': _L0_xattn_in['P'], 'L0_ffn_router_w': _L0_ffn_in['router_w'], 'L0_ffn_w1': _L0_ffn_in['w1'], 'L0_ffn_w2': _L0_ffn_in['w2'], 'L0_ffn_expert_scale': _L0_ffn_in['expert_scale'], 'L1_xattn_ln_g': _L1_xattn_in['ln_g'], 'L1_xattn_ln_b': _L1_xattn_in['ln_b'], 'L1_xattn_cln_g': _L1_xattn_in['cln_g'], 'L1_xattn_cln_b': _L1_xattn_in['cln_b'], 'L1_xattn_Wq': _L1_xattn_in['Wq'], 'L1_xattn_Wkv': _L1_xattn_in['Wkv'], 'L1_xattn_Wout': _L1_xattn_in['Wout'], 'L1_xattn_W1': _L1_xattn_in['W1'], 'L1_xattn_W2': _L1_xattn_in['W2'], 'L1_ffn_w1': _L1_ffn_in['w1'], 'L1_ffn_w3': _L1_ffn_in['w3'], 'L1_ffn_w2': _L1_ffn_in['w2']}

def reference(x, ctx_1024, mask_BxSxS2_ff0, g_xattn, g_ffn, L0_xattn_Wq, L0_xattn_bq, L0_xattn_Wk, L0_xattn_bk, L0_xattn_Wv, L0_xattn_bv, L0_xattn_Wo, L0_xattn_bo, L0_xattn_P, L0_ffn_router_w, L0_ffn_w1, L0_ffn_w2, L0_ffn_expert_scale, L1_xattn_ln_g, L1_xattn_ln_b, L1_xattn_cln_g, L1_xattn_cln_b, L1_xattn_Wq, L1_xattn_Wkv, L1_xattn_Wout, L1_xattn_W1, L1_xattn_W2, L1_ffn_w1, L1_ffn_w3, L1_ffn_w2):
    import jax
    import jax.numpy as jnp

    def _L0_xattn_ref(q, k, v, Wq, bq, Wk, bk, Wv, bv, Wo, bo, P):
        import jax, jax.numpy as jnp
        import numpy as np
        import math
        D = 128
        H = 16
        HD = D // H

        def _split_heads(x, B, L):
            return x.reshape(B, L, H, HD).transpose(0, 2, 1, 3)
        B, L, _ = q.shape
        qh = _split_heads(q @ Wq.T + bq, B, L)
        kh = _split_heads(k @ Wk.T + bk, B, L)
        vh = _split_heads(v @ Wv.T + bv, B, L)
        logits = jnp.einsum('bhld,bhmd->bhlm', qh, kh) / math.sqrt(HD)
        logits = jnp.einsum('bhlm,hg->bglm', logits, P)
        attn = jax.nn.softmax(logits, axis=-1)
        out = jnp.einsum('bhlm,bhmd->bhld', attn, vh)
        out = out.transpose(0, 2, 1, 3).reshape(B, L, D)
        return out @ Wo.T + bo

    def _L0_ffn_ref(hidden_states, router_w, w1, w2, expert_scale):
        import jax, jax.numpy as jnp
        import numpy as np
        B, S, D, F_DIM, E, TOPK = (2, 128, 128, 512, 8, 2)
        b, s, d = hidden_states.shape
        xf = hidden_states.reshape(-1, d)
        logits = xf @ router_w.T
        probs = jax.nn.softmax(logits, axis=-1)
        top_w, top_idx = jax.lax.top_k(probs, TOPK)
        top_w = jax.nn.softmax(top_w, axis=-1)
        combine = jnp.sum(jax.nn.one_hot(top_idx, E, dtype=xf.dtype) * top_w[..., None], axis=1)
        h = jax.nn.silu(jnp.einsum('td,efd->tef', xf, w1))
        y = jnp.einsum('tef,edf->ted', h, w2)
        y = y * expert_scale[None, :, None]
        out = jnp.einsum('te,ted->td', combine, y)
        return out.reshape(b, s, d)

    def _L1_xattn_ref(x, context, mask, ln_g, ln_b, cln_g, cln_b, Wq, Wkv, Wout, W1, W2):
        import jax, jax.numpy as jnp
        import numpy as np
        DIM = 128
        CTX_DIM = 128
        HEADS = 16
        DIM_HEAD = 64
        INNER = HEADS * DIM_HEAD
        FF_INNER = 4 * DIM
        EPS = 1e-05

        def layer_norm(x, g, b):
            mu = jnp.mean(x, axis=-1, keepdims=True)
            var = jnp.var(x, axis=-1, keepdims=True)
            return (x - mu) * jax.lax.rsqrt(var + EPS) * g + b
        scale = DIM_HEAD ** (-0.5)
        xn = layer_norm(x, ln_g, ln_b)
        cn = layer_norm(context, cln_g, cln_b)
        b, n, _ = xn.shape
        q = (xn @ Wq).reshape(b, n, HEADS, DIM_HEAD).transpose(0, 2, 1, 3) * scale
        kv = cn @ Wkv
        k, v = jnp.split(kv, 2, axis=-1)
        sim = jnp.einsum('bhid,bjd->bhij', q, k) + mask[:, None, :, :]
        attn = jax.nn.softmax(sim, axis=-1)
        out = jnp.einsum('bhij,bjd->bhid', attn, v)
        out = out.transpose(0, 2, 1, 3).reshape(b, n, INNER) @ Wout
        h = xn @ W1
        val, gate = jnp.split(h, 2, axis=-1)
        out = out + jax.nn.silu(gate) * val @ W2
        return out

    def _L1_ffn_ref(inputs, w1, w3, w2):
        import jax, jax.numpy as jnp
        import numpy as np
        D_MODEL = 128
        D_FF = 352
        N_EXPERTS = 8
        B, T, D = inputs.shape
        E = w1.shape[0]
        C = T // E
        x = inputs.reshape(B, E, C, D)
        gate = jnp.einsum('becd,edf->becf', x, w1)
        up = jnp.einsum('becd,edf->becf', x, w3)
        h = jax.nn.silu(gate) * up
        out = jnp.einsum('becf,efd->becd', h, w2)
        return out.reshape(B, T, D)
    x = x + jnp.tanh(g_xattn[0]) * _L0_xattn_ref(_layernorm(x, axis=-1), ctx_1024, ctx_1024, L0_xattn_Wq, L0_xattn_bq, L0_xattn_Wk, L0_xattn_bk, L0_xattn_Wv, L0_xattn_bv, L0_xattn_Wo, L0_xattn_bo, L0_xattn_P)
    x = x + jnp.tanh(g_ffn[0]) * _L0_ffn_ref(_layernorm(x, axis=-1), L0_ffn_router_w, L0_ffn_w1, L0_ffn_w2, L0_ffn_expert_scale)
    x = x + jnp.tanh(g_xattn[1]) * _L1_xattn_ref(_layernorm(x, axis=-1), ctx_1024, mask_BxSxS2_ff0, L1_xattn_ln_g, L1_xattn_ln_b, L1_xattn_cln_g, L1_xattn_cln_b, L1_xattn_Wq, L1_xattn_Wkv, L1_xattn_Wout, L1_xattn_W1, L1_xattn_W2)
    x = x + jnp.tanh(g_ffn[1]) * _L1_ffn_ref(_layernorm(x, axis=-1), L1_ffn_w1, L1_ffn_w3, L1_ffn_w2)
    return x

_drawn_inputs = setup_inputs


def setup_inputs(seed=0):
    import zlib

    import numpy as np

    out = dict(_drawn_inputs(seed))
    spreads = {'g_ffn': (-1.0, 0.6),
     'L0_xattn_bq': (0.0, 0.1),
     'L0_xattn_bk': (0.0, 2.0),
     'L0_xattn_bv': (0.0, 0.1),
     'L0_xattn_bo': (0.0, 0.1),
     'L0_ffn_expert_scale': (1.0, 0.6),
     'L1_xattn_ln_g': (1.0, 0.6),
     'L1_xattn_ln_b': (0.0, 0.8),
     'L1_xattn_cln_g': (1.0, 0.6),
     'L1_xattn_cln_b': (0.0, 2.0)}
    factors = {'L0_ffn_router_w': 2.906,
     'L1_xattn_Wq': 64.0,
     'L1_xattn_W1': 6.134,
     'L1_xattn_W2': 6.153,
     'L1_ffn_w1': 8.0,
     'L1_ffn_w3': 8.0,
     'L1_ffn_w2': 8.0,
     'L1_xattn_Wkv': 2.992,
     'L1_xattn_Wout': 2.839}
    for name, (base, spread) in spreads.items():
        noise = np.random.default_rng([zlib.crc32(name.encode()), seed]).standard_normal(out[name].shape)
        drawn = base * np.exp(spread * noise) if base else spread * noise
        out[name] = jnp.asarray(drawn.astype(out[name].dtype))
    for name, factor in factors.items():
        out[name] = (out[name] * factor).astype(out[name].dtype)
    return out
```

```python
from contextlib import ExitStack

import concourse.bass as bass
from concourse import mybir

F32 = mybir.dt.float32
ALU = mybir.AluOpType
ACT = mybir.ActivationFunctionType
AX = mybir.AxisListType

D = 128
SEQ = 64
NSEQ = 64
TOK = 128
T = NSEQ * SEQ // TOK
H = 16
HP = H // 2
HD0 = D // H
HD1 = 64
E0 = 8
F0 = 512
FC0 = F0 // 128
GT = 4
G = T // GT
E1 = 8
F1 = 352
F1C = [(0, 128), (128, 128), (256, 96)]
CT = SEQ // E1
MLP = 512
MC = MLP // 128
EPS = 1e-5
VW = 2 * (HD0 + 1)


def known(n):
    return isinstance(n, int)


def after(eng, sem, n):
    if not known(n) or n > 0:
        eng.wait_ge(sem, n)


def live(t, n=T):
    return not known(t) or 0 <= t < n


def pipelined(eng, step, lead, trail, n=T):
    lo = 4
    hi = n - lead - (n - lead) % 2
    for s in range(-lead, lo):
        step(s, s % 2)
    with eng.Fori(0, (hi - lo) // 2) as i:
        for u in range(2):
            step(i * 2 + (lo + u), u)
    for s in range(hi, n + trail):
        step(s, s % 2)


def build(nc, x, ctx_in, mask, g_xattn, g_ffn, wqT0, bq0, wkT0, bk0, wvT0, bv0, woT0, bo0, P0,
          routerT, w1T0, w2T0, escale, ln_g, ln_b, cln_g, cln_b, wq1, wkv1, wout1, w1m, w2m,
          w1e, w3e, w2e, out):
    with ExitStack() as ctx:
        def sb(name, *shape):
            return ctx.enter_context(nc.sbuf_tensor(name, [128, *shape], F32))

        def sem(name):
            return ctx.enter_context(nc.semaphore(name))

        X = sb("X", T, D)
        MK = sb("MK", T, SEQ)
        ident = sb("ident", 128)
        minus_half = sb("minus_half", GT)
        eps = sb("eps", GT)
        gates = sb("gates", 4)
        rawg = sb("rawg", 4)
        spare = sb("spare", 1)

        wq0_sb = sb("wq0_sb", D)
        wk0_sb = sb("wk0_sb", D)
        wv0_sb = sb("wv0_sb", D)
        wo0_sb = sb("wo0_sb", D)
        bias0 = sb("bias0", 3)
        bk_scaled = sb("bk_scaled", 1)
        Pc = sb("Pc", H)
        gbo = sb("gbo", D)
        router_sb = sb("router_sb", E0)
        escale_sb = sb("escale_sb", E0)
        tri = sb("tri", E0, E0)
        lnv = sb("lnv", 4)
        wkv_sb = sb("wkv_sb", 256)
        wq1_sb = sb("wq1_sb", H * HD1)
        wout_sb = sb("wout_sb", HP, D)
        w1m_sb = sb("w1m_sb", 2 * MLP)
        w2m_sb = sb("w2m_sb", MC, D)

        w1_sb = sb("w1_sb", E0, F0)
        w2_sb = sb("w2_sb", E0, FC0, D)
        w1e_sb = sb("w1e_sb", E1, F1)
        w3e_sb = sb("w3e_sb", E1, F1)
        w2e_sb = sb("w2e_sb", E1, len(F1C), D)
        cxb = [sb(f"cxb{u}", D) for u in range(2)]

        SIZES = {"ac": 13 * 1024 + 512, "bd": 7 * 1024 + 256}
        arenas = {k: sb(f"arena_{k}", n) for k, n in SIZES.items()}
        at = {}

        def part(which, *shape):
            n = 1
            for d in shape:
                n *= d
            lo = at.get(which, 0)
            at[which] = lo + n
            assert at[which] <= SIZES[which], (which, at)
            a = arenas[which][:, lo:lo + n]
            if len(shape) == 1:
                return a
            names = "abcd"[:len(shape)]
            return a.rearrange(f"p ({' '.join(names)}) -> p {' '.join(names)}",
                               **dict(zip(names[1:], shape[1:])))

        xn = [part("ac", D) for _ in range(2)]
        xcT = [part("ac", 4, 128) for _ in range(2)]
        qT = [part("ac", TOK) for _ in range(2)]
        kT = [part("ac", TOK) for _ in range(2)]
        KE = [part("ac", H, TOK) for _ in range(2)]
        VB = [part("ac", 2, HP, VW) for _ in range(2)]
        Ea = [part("ac", H, SEQ) for _ in range(2)]
        ETa = [part("ac", HP, TOK) for _ in range(2)]
        On = [part("ac", H, HD0) for _ in range(2)]
        OTa = [part("ac", TOK) for _ in range(2)]
        stat = [part("ac", 16) for _ in range(2)]
        mx = [part("ac", H) for _ in range(2)]
        rs = [part("ac", H) for _ in range(2)]
        yn = part("bd", GT, D)
        yT = [part("bd", GT * TOK) for _ in range(2)]
        Th = [part("bd", GT * TOK) for _ in range(2)]
        U = [part("bd", GT * TOK) for _ in range(4)]
        bst = part("bd", GT, 6)
        bmv = part("bd", GT, 2)
        brs = part("bd", GT)
        lg = part("bd", GT, E0)
        lmx = part("bd", GT)
        lsum = part("bd", GT)
        pr = part("bd", GT, E0)
        top = part("bd", GT, 8)
        c12 = part("bd", 3, GT)
        cmpg = part("bd", GT, E0, E0)
        cmpe = part("bd", GT, E0, E0)
        rank = part("bd", GT, E0)
        coef = [part("bd", GT, E0) for _ in range(2)]
        c2 = part("bd", GT, E0)
        at["ac"] = 0
        xn2 = [part("ac", 2, D) for _ in range(2)]
        xcT2 = [part("ac", 4, 128) for _ in range(2)]
        QT = [part("ac", HP, TOK) for _ in range(2)]
        KB = [part("ac", 2, 2, SEQ) for _ in range(2)]
        VC = [part("ac", 2, 2, HD1) for _ in range(2)]
        Ec = [part("ac", H, SEQ) for _ in range(2)]
        ETc = [part("ac", HP, TOK) for _ in range(2)]
        OTc = [part("ac", HP, TOK) for _ in range(2)]
        tg = [part("ac", MC, TOK) for _ in range(2)]
        Uc = [part("ac", MC, TOK) for _ in range(2)]
        cst = [part("ac", 40) for _ in range(2)]
        cmx = [part("ac", H) for _ in range(2)]
        csum = [part("ac", H) for _ in range(2)]
        cinv = [part("ac", H) for _ in range(2)]
        at["bd"] = 0
        zn = [part("bd", D) for _ in range(2)]
        dst_ = [part("bd", 16) for _ in range(2)]
        ZT = part("bd", T * TOK)
        Td = [part("bd", 512) for _ in range(2)]
        Ud = [part("bd", 512) for _ in range(3)]
        at["ac"] = 0
        RT = part("ac", T * TOK)
        PS = ctx.enter_context(nc.psum_tensor("PS", [128, 8, 512], F32))

        small_loaded = sem("small_loaded")
        x_loaded = [sem(f"x_loaded{i}") for i in range(4)]
        w0_loaded = sem("w0_loaded")
        ctx_loaded = [sem(f"ctx_loaded{u}") for u in range(2)]
        w1l_loaded = sem("w1l_loaded")
        wd_loaded = sem("wd_loaded")
        ident_zero = sem("ident_zero")
        ident_ready = sem("ident_ready")
        half_ready = sem("half_ready")
        gates_ready = sem("gates_ready")
        const_ready = sem("const_ready")
        vb_zero = sem("vb_zero")
        a_st = sem("a_st"); a_mv = sem("a_mv"); a_eps = sem("a_eps"); a_rstd = sem("a_rstd"); a_xn = sem("a_xn"); a_xb = sem("a_xb")
        a_tin = sem("a_tin"); a_xc = sem("a_xc"); a_qkv = sem("a_qkv"); a_k = sem("a_k"); a_q = sem("a_q"); a_v = sem("a_v")
        a_ked = sem("a_ked"); a_kep = sem("a_kep"); a_s = sem("a_s"); a_mx = sem("a_mx"); a_sub = sem("a_sub"); a_exp = sem("a_exp")
        a_te = sem("a_te"); a_et = sem("a_et"); a_av = sem("a_av"); a_rc = sem("a_rc"); a_on = sem("a_on"); a_to = sem("a_to")
        a_ot = sem("a_ot"); a_pr = sem("a_pr"); a_res = sem("a_res")
        b_ch = sem("b_ch"); b_mv = sem("b_mv"); b_eps = sem("b_eps"); b_rstd = sem("b_rstd"); b_yn = sem("b_yn"); b_ty = sem("b_ty"); b_yT = sem("b_yT")
        b_lg = sem("b_lg"); b_lmx = sem("b_lmx"); b_ex = sem("b_ex"); b_dp = sem("b_dp"); b_ex2 = sem("b_ex2"); b_coef = sem("b_coef")
        b_h = sem("b_h"); b_t = sem("b_t"); b_u = sem("b_u"); b_yu = sem("b_yu"); b_acc = sem("b_acc")
        c_ch = sem("c_ch"); c_ch2 = sem("c_ch2"); c_add = sem("c_add"); c_mv = sem("c_mv"); c_eps = sem("c_eps"); c_rstd = sem("c_rstd"); c_xn = sem("c_xn"); c_tin = sem("c_tin"); c_xc = sem("c_xc")
        c_kv = sem("c_kv"); c_kve = sem("c_kve"); c_q = sem("c_q"); c_qe = sem("c_qe"); c_s = sem("c_s"); c_mx = sem("c_mx")
        c_sub = sem("c_sub"); c_exp = sem("c_exp"); c_sum = sem("c_sum"); c_inv = sem("c_inv"); c_nrm = sem("c_nrm"); c_te = sem("c_te"); c_et = sem("c_et")
        c_o = sem("c_o"); c_ot = sem("c_ot"); c_h = sem("c_h"); c_t = sem("c_t"); c_g = sem("c_g"); c_u = sem("c_u"); c_out = sem("c_out"); c_res = sem("c_res")
        kb_zero = sem("kb_zero")
        d_st = sem("d_st"); d_mv = sem("d_mv"); d_eps = sem("d_eps"); d_rstd = sem("d_rstd"); d_zn = sem("d_zn"); d_tz = sem("d_tz"); d_zt = sem("d_zt")
        d_h = sem("d_h"); d_t = sem("d_t"); d_g = sem("d_g"); d_u = sem("d_u"); d_yu = sem("d_yu"); d_r = sem("d_r"); d_tr = sem("d_tr"); d_x = sem("d_x")
        stored = sem("stored")

        block = ctx.enter_context(nc.Block())

        x_t = x.rearrange("(t b) s d -> (b s) t d", b=2)
        c_t_in = ctx_in.rearrange("(t b) s d -> (b s) t d", b=2)
        out_t = out.rearrange("(t b) s d -> (b s) t d", b=2)
        LC = T // 4
        N_SMALL = 19

        @block.sync
        def _(sp):
            def load_x(i):
                sl = slice(i * LC, (i + 1) * LC)
                sp.dma_start(X[:, sl, :], x_t[:, sl, :]).then_inc(x_loaded[i], 16)

            load_x(0)
            smalls = ((wq0_sb[:, :], wqT0), (wk0_sb[:, :], wkT0), (wv0_sb[:, :], wvT0), (wo0_sb[:, :], woT0),
                      (bias0[:, 0:1], bq0.unsqueeze(1)), (bias0[:, 1:2], bk0.unsqueeze(1)),
                      (bias0[:, 2:3], bv0.unsqueeze(1)),
                      (gbo[:, :], bo0.unsqueeze(0).broadcast_to([128, D])),
                      (rawg[:, 0:2], g_xattn.unsqueeze(0).broadcast_to([128, 2])),
                      (rawg[:, 2:4], g_ffn.unsqueeze(0).broadcast_to([128, 2])),
                      (escale_sb[:, :], escale.unsqueeze(0).broadcast_to([128, E0])),
                      (router_sb[:, :], routerT),
                      (lnv[:, 0:1], ln_g.unsqueeze(1)), (lnv[:, 1:2], ln_b.unsqueeze(1)),
                      (lnv[:, 2:3], cln_g.unsqueeze(1)), (lnv[:, 3:4], cln_b.unsqueeze(1)),
                      (wkv_sb[:, :], wkv1), (Pc[:, :], P0), (w2m_sb[:, :, :], w2m.rearrange("(c p) d -> p c d", p=128)))
            assert len(smalls) == N_SMALL
            for dst, src in smalls:
                sp.dma_start(dst, src).then_inc(small_loaded, 16)

            def load_ctx(t, u, sem_free, free):
                after(sp, sem_free, free)
                sp.dma_start(cxb[u][:, :], c_t_in[:, bass.ts(t, 1), :].squeeze(1)).then_inc(ctx_loaded[u], 16)

            load_ctx(0, 0, a_tin, 0)
            load_ctx(1, 1, a_tin, 0)
            for i in range(1, 4):
                load_x(i)
            sp.dma_start(w1_sb[:, :, :], w1T0).then_inc(w0_loaded, 16)
            sp.dma_start(w2_sb[:, :, :, :], w2T0).then_inc(w0_loaded, 16)
            with sp.Fori(1, T // 2) as i:
                for u in range(2):
                    load_ctx(i * 2 + u, u, a_tin, i * 2 + (u - 1))
            sp.dma_start(MK[:, :, :], mask.rearrange("(t b) s m -> (b s) t m", b=2)).then_inc(w1l_loaded, 16)
            sp.dma_start(wq1_sb[:, :], wq1).then_inc(w1l_loaded, 16)
            sp.dma_start(wout_sb[:, :, :], wout1.rearrange("(t p) d -> p t d", p=128)).then_inc(w1l_loaded, 16)
            sp.dma_start(w1m_sb[:, :], w1m).then_inc(w1l_loaded, 16)
            sp.dma_start(w1e_sb[:, :, :], w1e).then_inc(wd_loaded, 16)
            sp.dma_start(w3e_sb[:, :, :], w3e).then_inc(wd_loaded, 16)
            for c, (f, n) in enumerate(F1C):
                sp.dma_start(w2e_sb[0:n, :, c, :], w2e[:, f:f + n, :].rearrange("e f d -> f e d")).then_inc(wd_loaded, 16)
            load_ctx(0, 0, a_tin, T)
            load_ctx(1, 1, a_tin, T)
            with sp.Fori(1, T // 2) as i:
                for u in range(2):
                    load_ctx(i * 2 + u, u, c_mv, i * 4 + (2 * u - 2))
            for g in range(G):
                sp.wait_ge(d_x, g + 1)
                sl = slice(g * GT, (g + 1) * GT)
                sp.dma_start(out_t[:, sl, :], X[:, sl, :]).then_inc(stored, 16)
            sp.wait_ge(stored, 16 * G)

        @block.gpsimd
        def _(pool):
            pool.memset(ident[:, :], 0.0).then_inc(ident_zero, 1)
            pool.memset(minus_half[:, :], -0.5).then_inc(half_ready, 1)
            pool.memset(eps[:, :], EPS).then_inc(half_ready, 1)
            pool.memset(tri[:, :, :], 0.0).then_inc(ident_zero, 1)
            pool.wait_ge(ident_zero, 2)
            pool.affine_select(out=ident[:, :], in_=ident[:, :], compare_op=ALU.not_equal, fill=1.0, base=0,
                               pattern=[[-1, 128]], channel_multiplier=1).then_inc(ident_ready, 1)
            pool.affine_select(out=tri[:, :, :], in_=tri[:, :, :], compare_op=ALU.is_ge, fill=1.0, base=0,
                               pattern=[[-1, E0], [1, E0]], channel_multiplier=0).then_inc(ident_ready, 1)
            pool.wait_ge(half_ready, 2)
            pool.wait_ge(const_ready, 2)

            def rstd(t, u):
                if live(t):
                    pool.wait_ge(a_mv, t + 1)
                    pool.tensor_tensor(stat[u][:, 8:9], stat[u][:, 7:8], eps[:, 0:1], ALU.add).then_inc(a_eps, 1)
                    pool.wait_ge(a_eps, t + 1)
                    pool.tensor_tensor(stat[u][:, 9:10], stat[u][:, 8:9], minus_half[:, 0:1], ALU.pow).then_inc(a_rstd, 1)

            def scale_k(t, u):
                if live(t):
                    pool.wait_ge(a_k, t + 1)
                    pool.tensor_tensor(KE[u][:, HP:H, :], kT[u].unsqueeze(1).to_broadcast([128, HP, TOK]),
                                       Pc[:, HP:H].unsqueeze(2).to_broadcast([128, HP, TOK]), ALU.mult).then_inc(a_kep, 1)

            def add_bias(t):
                if live(t):
                    pool.wait_ge(a_xn, t + 1)
                    pool.tensor_tensor(X[:, bass.ts(t, 1), :].squeeze(1), X[:, bass.ts(t, 1), :].squeeze(1), gbo[:, :], ALU.add).then_inc(a_xb, 1)

            def step(s, u):
                scale_k(s + 1, 1 - u)
                rstd(s + 2, u)
                add_bias(s)

            pipelined(pool, step, 2, 0)

            def group_rstd(g):
                if live(g, G):
                    after(pool, b_mv, g + 1)
                    pool.tensor_tensor(brs, bmv[:, :, 1], eps[:, :], ALU.add).then_inc(b_eps, 1)
                    after(pool, b_eps, g + 1)
                    pool.tensor_tensor(brs, brs, minus_half[:, :], ALU.pow).then_inc(b_rstd, 1)

            with pool.Fori(0, G) as g:
                group_rstd(g)


            def rstd_c(t, u, k):
                if live(t):
                    pool.wait_ge(c_mv, t * 2 + (k + 1))
                    a = 12 if k == 0 else 28
                    n = 2 if k == 0 else 1
                    pool.tensor_tensor(cst[u][:, a + 4:a + 4 + n], cst[u][:, a + 1:a + 2 * n:2], eps[:, 0:n], ALU.add).then_inc(c_eps, 1)
                    pool.wait_ge(c_eps, t * 2 + (k + 1))
                    pool.tensor_tensor(cst[u][:, a + 6:a + 6 + n], cst[u][:, a + 4:a + 4 + n], minus_half[:, 0:n], ALU.pow).then_inc(c_rstd, 1)

            def divide(t, u):
                if live(t):
                    pool.wait_ge(c_inv, t + 1)
                    pool.tensor_tensor(Ec[u], Ec[u], cinv[u].unsqueeze(2).to_broadcast([128, H, SEQ]), ALU.mult).then_inc(c_nrm, 1)

            def step_c(s, u):
                rstd_c(s + 2, u, 0)
                rstd_c(s + 2, u, 1)
                divide(s, u)

            pipelined(pool, step_c, 2, 0)

            def rstd_d(t, u):
                pool.wait_ge(d_mv, t + 1)
                pool.tensor_tensor(dst_[u][:, 8:9], dst_[u][:, 7:8], eps[:, 0:1], ALU.add).then_inc(d_eps, 1)
                pool.wait_ge(d_eps, t + 1)
                pool.tensor_tensor(dst_[u][:, 9:10], dst_[u][:, 8:9], minus_half[:, 0:1], ALU.pow).then_inc(d_rstd, 1)

            with pool.Fori(0, T // 2) as i:
                for u in range(2):
                    rstd_d(i * 2 + u, u)

        @block.scalar
        def _(act):
            act.wait_ge(small_loaded, 16 * N_SMALL)
            act.activation(gates[:, :], rawg[:, :], ACT.Tanh).then_inc(gates_ready, 1)
            act.wait_ge(const_ready, 1)

            def out_t_copy(t, u):
                if live(t):
                    act.wait_ge(a_to, t + 1)
                    act.activation(OTa[u], PS[:, 7, 0:128], ACT.Identity, bias=bias0[:, 2:3]).then_inc(a_ot, 1)

            def in_copy(t, u):
                if live(t):
                    act.wait_ge(a_tin, t + 1)
                    after(act, a_qkv, t - 1)
                    act.copy(xcT[u][:, 0:2, :], PS[:, 0, 0:256].rearrange("p (a b) -> p a b", a=2)).then_inc(a_xc, 1)
                    act.copy(xcT[u][:, 2:4, :].rearrange("p b (k m) -> p b k m", k=2),
                             PS[:, 0, 128:256].rearrange("p (b m) -> p b m", b=2).unsqueeze(2).to_broadcast([128, 2, 2, SEQ])).then_inc(a_xc, 1)

            def e_t_copy(t, u):
                if live(t):
                    act.wait_ge(a_te, t + 1)
                    act.copy(ETa[u], PS[:, 4:6, :].rearrange("p a (b c) -> p (a b) c", b=4)).then_inc(a_et, 1)

            def qkv_copy(t, u):
                if live(t):
                    act.wait_ge(a_qkv, t + 1)
                    after(act, a_ked, t - 1)
                    after(act, a_kep, t - 1)
                    act.activation(kT[u], PS[:, 1, 128:256], ACT.Identity, bias=bk_scaled[:, 0:1], scale=HD0 ** -0.5).then_inc(a_k, 1)
                    act.activation(qT[u], PS[:, 1, 0:128], ACT.Identity, bias=bias0[:, 0:1]).then_inc(a_q, 1)
                    after(act, a_av, t - 1)
                    v = PS[:, 1, 256:512].rearrange("p (b t k d) -> p b t k d", b=2, t=HP, k=2)
                    vb = VB[u].rearrange("p b t (k d) -> p b t k d", k=2)
                    for k in range(2):
                        act.copy(vb[64 * k:64 * k + 64, :, :, k, 0:HD0], v[64 * k:64 * k + 64, :, :, k, :]).then_inc(a_v, 1)

            def exps(t, u):
                if live(t):
                    act.wait_ge(a_sub, t + 1)
                    act.activation(Ea[u], Ea[u], ACT.Exp).then_inc(a_exp, 1)

            def step(s, u):
                out_t_copy(s - 2, u)
                in_copy(s + 1, 1 - u)
                e_t_copy(s - 1, 1 - u)
                qkv_copy(s + 1, 1 - u)
                exps(s, u)

            act.wait_ge(vb_zero, 6)
            pipelined(act, step, 1, 2)

            def yT_copy(g, u):
                if live(g, G):
                    act.wait_ge(b_ty, g + 1)
                    act.copy(yT[u], PS[:, 6, :]).then_inc(b_yT, 1)

            def router_exp(g):
                if live(g, G):
                    act.wait_ge(b_lmx, g + 1)
                    act.activation(pr, lg, ACT.Exp).then_inc(b_ex, 1)

            def second_exp(g):
                if live(g, G):
                    act.wait_ge(b_dp, g + 1)
                    act.activation(c12[:, 1, :], c12[:, 0, :], ACT.Exp).then_inc(b_ex2, 1)

            def group_b(g, u):
                for e in range(E0):
                    for c in range(FC0):
                        j = e * FC0 + c
                        act.wait_ge(b_h, g * (E0 * FC0) + (j + 1))
                        after(act, b_u, g * (E0 * FC0) + (j - 1))
                        act.activation(Th[j % 2], PS[:, j % 4, :], ACT.Tanh, scale=0.5).then_inc(b_t, 1)
                        if j == 11:
                            yT_copy(g + 1, 1 - u)
                        if j == 17:
                            router_exp(g + 1)
                        if j == 20:
                            second_exp(g + 1)

            yT_copy(0, 0)
            router_exp(0)
            second_exp(0)
            group_b(0, 0)
            with act.Fori(0, (G - 2) // 2) as i:
                group_b(i * 2 + 1, 1)
                group_b(i * 2 + 2, 0)
            group_b(G - 1, 1)

            def in_copy_c(t, u):
                if live(t):
                    act.wait_ge(c_tin, t + 1)
                    after(act, c_h, t - 1)
                    act.activation(xcT2[u][:, 0, :], PS[:, 0, 0:128], ACT.Identity, bias=lnv[:, 1:2], scale=lnv[:, 0:1]).then_inc(c_xc, 1)
                    act.activation(xcT2[u][:, 1, :], PS[:, 0, 128:256], ACT.Identity, bias=lnv[:, 3:4], scale=lnv[:, 2:3]).then_inc(c_xc, 1)
                    act.activation(xcT2[u][:, 2:4, :].rearrange("p b (k m) -> p b k m", k=2),
                                   PS[:, 0, 128:256].rearrange("p (b m) -> p b m", b=2).unsqueeze(2).to_broadcast([128, 2, 2, SEQ]),
                                   ACT.Identity, bias=lnv[:, 3:4], scale=lnv[:, 2:3]).then_inc(c_xc, 1)

            def kv_copy(t, u):
                if live(t):
                    act.wait_ge(c_kv, t + 1)
                    after(act, c_o, t - 1)
                    for k in range(2):
                        q = slice(64 * k, 64 * k + 64)
                        act.mul(KB[u][q, :, k, :], PS[q, 1, 0:128].rearrange("p (b m) -> p b m", b=2), HD1 ** -0.5).then_inc(c_kve, 1)
                        act.copy(VC[u][q, :, k, :], PS[q, 1, 128:384].rearrange("p (b k d) -> p b k d", b=2, k=2)[:, :, k, :]).then_inc(c_kve, 1)

            def q_copy(t, u):
                if live(t):
                    act.wait_ge(c_q, t + 1)
                    act.copy(QT[u], PS[:, 2:4, :].rearrange("p a (b c) -> p (a b) c", b=4)).then_inc(c_qe, 1)

            def exps_c(t, u):
                if live(t):
                    act.wait_ge(c_sub, t + 1)
                    act.activation(Ec[u], Ec[u], ACT.Exp).then_inc(c_exp, 1)

            def e_t_copy_c(t, u):
                if live(t):
                    act.wait_ge(c_te, t + 1)
                    act.copy(ETc[u], PS[:, 6:8, :].rearrange("p a (b c) -> p (a b) c", b=4)).then_inc(c_et, 1)

            def tanh_c(t, u):
                if live(t):
                    act.wait_ge(c_h, t + 1)
                    act.activation(tg[u], PS[:, 3, :].rearrange("p (a b) -> p a b", a=MC), ACT.Tanh, scale=0.5).then_inc(c_t, 1)

            def o_t_copy(t, u):
                if live(t):
                    act.wait_ge(c_o, t + 1)
                    act.copy(OTc[u].rearrange("p t (b l) -> p b t l", b=2),
                             PS[:, 6:8, :].rearrange("p b (t l) -> p b t l", t=HP)).then_inc(c_ot, 1)

            def step_c(s, u):
                e_t_copy_c(s - 1, 1 - u)
                in_copy_c(s + 1, 1 - u)
                exps_c(s, u)
                tanh_c(s, u)
                o_t_copy(s - 1, 1 - u)
                kv_copy(s + 1, 1 - u)
                q_copy(s + 1, 1 - u)

            act.wait_ge(kb_zero, 4)
            pipelined(act, step_c, 1, 1)

            act.wait_ge(c_res, T)
            with act.Fori(0, T // 2) as i:
                for u in range(2):
                    t = i * 2 + u
                    act.wait_ge(d_tz, t + 1)
                    act.copy(ZT[:, bass.ts(t, 128)], PS[:, 6 + u, 0:128]).then_inc(d_zt, 1)
            for j in range(E1 * 3):
                n = F1C[j % 3][1]
                act.wait_ge(d_h, j + 1)
                after(act, d_u, j - 1)
                act.activation(Td[j % 2][0:n, :], PS[0:n, 2 * (j % 2), :], ACT.Tanh, scale=0.5).then_inc(d_t, 1)

        @block.vector
        def _(dve):
            for p in range(2):
                dve.memset(VB[p], 0.0).then_inc(vb_zero, 1)
            dve.wait_ge(vb_zero, 2)
            for p in range(2):
                dve.memset(VB[p][0:64, :, :, HD0:HD0 + 1], 1.0).then_inc(vb_zero, 1)
                dve.memset(VB[p][64:128, :, :, VW - 1:VW], 1.0).then_inc(vb_zero, 1)
            dve.wait_ge(small_loaded, 16 * N_SMALL)
            dve.tensor_scalar(bk_scaled[:, :], bias0[:, 1:2], HD0 ** -0.5, None, ALU.mult).then_inc(const_ready, 1)
            dve.wait_ge(gates_ready, 1)
            dve.tensor_scalar(gbo[:, :], gbo[:, :], gates[:, 0:1], None, ALU.mult).then_inc(const_ready, 1)
            dve.tensor_scalar(w2m_sb[:, :, :], w2m_sb[:, :, :], 0.5, None, ALU.mult).then_inc(const_ready, 1)
            dve.tensor_scalar(escale_sb[:, :], escale_sb[:, :], gates[:, 2:3], 0.5, ALU.mult, ALU.mult).then_inc(const_ready, 1)
            dve.tensor_scalar(gates[:, 3:4], gates[:, 3:4], 0.5, None, ALU.mult).then_inc(const_ready, 1)
            dve.wait_ge(const_ready, 5)

            def xtile(t):
                return X[:, bass.ts(t, 1), :].squeeze(1)

            def stats(t, u):
                if live(t):
                    dve.bn_stats(stat[u][:, 0:6], xtile(t)).then_inc(a_st, 1)
                    dve.wait_ge(a_st, t + 1)
                    dve.memset(spare[:, 0:1], 0.0)
                    dve.bn_aggr(stat[u][:, 6:8], stat[u][:, 0:6]).then_inc(a_mv, 1)

            def normalise(t, u):
                if live(t):
                    dve.wait_ge(a_rstd, t + 1)
                    after(dve, a_tin, t - 1)
                    dve.tensor_scalar(xn[u], xtile(t), stat[u][:, 6:7], stat[u][:, 9:10], ALU.subtract, ALU.mult).then_inc(a_xn, 1)

            def softmax(t, u):
                if live(t):
                    S = PS[:, 2:4, :].rearrange("p a (g m) -> p (a g) m", g=8)
                    dve.wait_ge(a_s, t + 1)
                    dve.reduce_max(mx[u], S, AX.X).then_inc(a_mx, 1)
                    dve.wait_ge(a_mx, t + 1)
                    after(dve, a_te, t - 1)
                    dve.tensor_tensor(Ea[u], S, mx[u].unsqueeze(2).to_broadcast([128, H, SEQ]), ALU.subtract).then_inc(a_sub, 1)

            def scale_k(t, u):
                if live(t):
                    dve.wait_ge(a_k, t + 1)
                    for g in range(HP):
                        m = dve.tensor_scalar(KE[u][:, g, :], kT[u], Pc[:, g:g + 1], None, ALU.mult)
                    m.then_inc(a_ked, 1)

            def normalise_out(t, u):
                if live(t):
                    O = PS[:, 6, 0:HP * VW].rearrange("p (g d) -> p g d", g=H)
                    dve.wait_ge(a_av, t + 1)
                    dve.reciprocal(rs[u], O[:, :, HD0]).then_inc(a_rc, 1)
                    dve.wait_ge(a_rc, t + 1)
                    after(dve, a_to, t - 1)
                    dve.tensor_tensor(On[u], O[:, :, 0:HD0], rs[u].unsqueeze(2).to_broadcast([128, H, HD0]), ALU.mult).then_inc(a_on, 1)

            def residual(t):
                if live(t):
                    dve.wait_ge(a_pr, t + 1)
                    dve.wait_ge(a_xb, t + 1)
                    dve.scalar_tensor_tensor(xtile(t), PS[:, 7, 128:256], gates[:, 0:1], xtile(t), ALU.mult, ALU.add).then_inc(a_res, 1)

            def step(s, u):
                normalise(s + 1, 1 - u)
                softmax(s, u)
                residual(s - 2)
                scale_k(s + 1, 1 - u)
                normalise_out(s - 1, 1 - u)
                if known(s) and s == 0:
                    for q in x_loaded[1:]:
                        dve.wait_ge(q, 16)
                stats(s + 2, u)

            dve.wait_ge(x_loaded[0], 16)
            pipelined(dve, step, 2, 2)
            dve.wait_ge(a_res, T)
            for p in range(2):
                dve.memset(KB[p], 0.0).then_inc(kb_zero, 1)
                dve.memset(VC[p], 0.0).then_inc(kb_zero, 1)

            NB = E0 * FC0
            CH = 17
            chain = [0]
            v4 = [128, GT, E0]
            v5 = [128, GT, E0, E0]

            def link(ins, g):
                chain[0] += 1
                ins.then_inc(b_ch, 1)
                dve.wait_ge(b_ch, g * CH + chain[0])

            def group_stats(g):
                if live(g, G):
                    chain[0] = 0
                    for k in range(GT):
                        m = dve.bn_stats(bst[:, k, :], xtile(g * GT + k))
                    chain[0] += 1
                    m.then_inc(b_ch, 1)
                    dve.wait_ge(b_ch, g * CH + chain[0])
                    dve.memset(spare[:, 0:1], 0.0)
                    for k in range(GT):
                        m = dve.bn_aggr(bmv[:, k, :], bst[:, k, :])
                    m.then_inc(b_mv, 1)

            def group_normalise(g):
                if live(g, G):
                    dve.wait_ge(b_rstd, g + 1)
                    for k in range(GT):
                        m = dve.tensor_scalar(yn[:, k, :], xtile(g * GT + k), bmv[:, k, 0:1], brs[:, k:k + 1], ALU.subtract, ALU.mult)
                    m.then_inc(b_yn, 1)

            def route_shift(g):
                if live(g, G):
                    L = PS[:, 7, 0:GT * E0].rearrange("p (k e) -> p k e", k=GT)
                    dve.wait_ge(b_lg, g + 1)
                    link(dve.reduce_max(lmx, L, AX.X), g)
                    dve.tensor_tensor(lg, L, lmx.unsqueeze(2).to_broadcast(v4), ALU.subtract).then_inc(b_lmx, 1)

            def route_probs(g):
                if live(g, G):
                    dve.wait_ge(b_ex, g + 1)
                    link(dve.reduce_sum(lsum, pr, AX.X), g)
                    link(dve.reciprocal(lsum, lsum), g)
                    link(dve.tensor_tensor(pr, pr, lsum.unsqueeze(2).to_broadcast(v4), ALU.mult), g)

            def route_top(g):
                if live(g, G):
                    for k in range(GT):
                        m = dve.max(top[:, k, :], pr[:, k, :])
                    link(m, g)
                    dve.tensor_tensor(c12[:, 0, :], top[:, :, 1], top[:, :, 0], ALU.subtract).then_inc(b_dp, 1)

            def route_compare(g):
                if live(g, G):
                    for k in range(GT):
                        v3 = [128, E0, E0]
                        dve.tensor_tensor(cmpg[:, k], pr[:, k, :].unsqueeze(1).to_broadcast(v3), pr[:, k, :].unsqueeze(2).to_broadcast(v3), ALU.is_gt)
                        m = dve.tensor_tensor(cmpe[:, k], pr[:, k, :].unsqueeze(1).to_broadcast(v3), pr[:, k, :].unsqueeze(2).to_broadcast(v3), ALU.is_equal)
                    link(m, g)

            def route_ties(g):
                if live(g, G):
                    link(dve.tensor_tensor(cmpe, cmpe, tri[:, :, :].unsqueeze(1).to_broadcast(v5), ALU.mult), g)
                    link(dve.tensor_tensor(cmpg, cmpg, cmpe, ALU.add), g)

            def route_rank(g):
                if live(g, G):
                    link(dve.reduce_sum(rank, cmpg, AX.X), g)
                    dve.wait_ge(b_ex2, g + 1)
                    link(dve.tensor_scalar(c12[:, 2, :], c12[:, 1, :], 1.0, None, ALU.add), g)
                    link(dve.reciprocal(c12[:, 0, :], c12[:, 2, :]), g)
                    link(dve.tensor_tensor(c12[:, 2, :], c12[:, 1, :], c12[:, 0, :], ALU.mult), g)

            def route_weights(g, u):
                if live(g, G):
                    w = [c12[:, i, :].unsqueeze(2).to_broadcast(v4) for i in (0, 2)]
                    link(dve.scalar_tensor_tensor(coef[u], rank, 0.0, w[0], ALU.is_equal, ALU.mult), g)
                    link(dve.scalar_tensor_tensor(c2, rank, 1.0, w[1], ALU.is_equal, ALU.mult), g)
                    link(dve.tensor_tensor(coef[u], coef[u], c2, ALU.add), g)
                    link(dve.tensor_tensor(coef[u], coef[u], escale_sb[:, :].unsqueeze(1).to_broadcast(v4), ALU.mult), g)
                    assert chain[0] == CH, chain[0]

            def combine(g, e, u):
                dve.wait_ge(b_yu, (g * E0 + (e + 1)) * FC0)
                after(dve, b_acc, g * E0 + e)
                for k in range(GT):
                    m = dve.scalar_tensor_tensor(xtile(g * GT + k), PS[:, 4 + e % 2, k * D:(k + 1) * D], coef[u][:, k, e:e + 1],
                                                 xtile(g * GT + k), ALU.mult, ALU.add)
                m.then_inc(b_acc, 1)

            def group_b(g, u):
                for j in range(NB):
                    e, c = j // FC0, j % FC0
                    dve.wait_ge(b_t, g * NB + (j + 1))
                    after(dve, b_yu, g * NB + (j - 3))
                    dve.scalar_tensor_tensor(U[j % 4], Th[j % 2], 1.0, PS[:, j % 4, :], ALU.add, ALU.mult).then_inc(b_u, 1)
                    if e and c == 2:
                        combine(g, e - 1, u)
                    if j == 5:
                        group_stats(g + 1)
                    if j == 7:
                        group_normalise(g + 1)
                    if j == 16:
                        route_shift(g + 1)
                    if j == 19:
                        route_probs(g + 1)
                    if j == 20:
                        route_top(g + 1)
                    if j == 21:
                        route_compare(g + 1)
                    if j == 23:
                        route_ties(g + 1)
                    if j == 24:
                        route_rank(g + 1)
                    if j == 25:
                        route_weights(g + 1, 1 - u)
                combine(g, E0 - 1, u)

            group_stats(0)
            group_normalise(0)
            route_shift(0)
            route_probs(0)
            route_top(0)
            route_compare(0)
            route_ties(0)
            route_rank(0)
            route_weights(0, 0)
            group_b(0, 0)
            with dve.Fori(0, (G - 2) // 2) as i:
                group_b(i * 2 + 1, 1)
                group_b(i * 2 + 2, 0)
            group_b(G - 1, 1)
            dve.wait_ge(b_acc, G * E0)

            def stats_c(t, u):
                if live(t):
                    s = cst[u]
                    dve.wait_ge(ctx_loaded[u], t * 8 + (8 * T + 16 - 8 * u))
                    dve.bn_stats(s[:, 0:6], xtile(t)).then_inc(c_ch, 1)
                    dve.bn_stats(s[:, 6:12], cxb[u][:, :]).then_inc(c_ch, 1)
                    dve.wait_ge(c_ch, t * 2 + 2)
                    dve.memset(spare[:, 0:1], 0.0)
                    dve.bn_aggr(s[:, 12:14], s[:, 0:6])
                    dve.bn_aggr(s[:, 14:16], s[:, 6:12]).then_inc(c_mv, 1)

            def normalise_c(t, u):
                if live(t):
                    s = cst[u]
                    dve.wait_ge(c_rstd, t * 2 + 1)
                    after(dve, c_tin, t - 1)
                    dve.tensor_scalar(xn2[u][:, 0, :], xtile(t), s[:, 12:13], s[:, 18:19], ALU.subtract, ALU.mult).then_inc(c_ch2, 1)
                    dve.tensor_scalar(xn2[u][:, 1, :], cxb[u][:, :], s[:, 14:15], s[:, 19:20], ALU.subtract, ALU.mult)
                    dve.wait_ge(c_ch2, t * 2 + 1)
                    dve.bn_stats(s[:, 20:26], xn2[u][:, 0, :]).then_inc(c_ch2, 1)
                    dve.wait_ge(c_ch2, t * 2 + 2)
                    dve.memset(spare[:, 0:1], 0.0)
                    dve.bn_aggr(s[:, 28:30], s[:, 20:26]).then_inc(c_mv, 1)

            def normalise_again(t, u):
                if live(t):
                    s = cst[u]
                    dve.wait_ge(c_rstd, t * 2 + 2)
                    dve.tensor_scalar(xn2[u][:, 0, :], xn2[u][:, 0, :], s[:, 28:29], s[:, 34:35], ALU.subtract, ALU.mult).then_inc(c_xn, 1)

            def softmax_c(t, u):
                if live(t):
                    S = PS[:, 4:6, :].rearrange("p a (g m) -> p (a g) m", g=8)
                    dve.wait_ge(c_s, t + 1)
                    after(dve, c_te, t - 1)
                    dve.tensor_tensor(Ec[u], S, MK[:, bass.ts(t, 1), :].to_broadcast([128, H, SEQ]), ALU.add).then_inc(c_add, 1)
                    dve.wait_ge(c_add, t + 1)
                    dve.reduce_max(cmx[u], Ec[u], AX.X).then_inc(c_mx, 1)
                    dve.wait_ge(c_mx, t + 1)
                    dve.tensor_tensor(Ec[u], Ec[u], cmx[u].unsqueeze(2).to_broadcast([128, H, SEQ]), ALU.subtract).then_inc(c_sub, 1)

            def sums_c(t, u):
                if live(t):
                    dve.wait_ge(c_exp, t + 1)
                    dve.reduce_sum(csum[u], Ec[u], AX.X).then_inc(c_sum, 1)
                    dve.wait_ge(c_sum, t + 1)
                    dve.reciprocal(cinv[u], csum[u]).then_inc(c_inv, 1)

            def mlp_c(t, u):
                if live(t):
                    dve.wait_ge(c_t, t + 1)
                    dve.scalar_tensor_tensor(tg[u].rearrange("p a b -> p (a b)"), tg[u].rearrange("p a b -> p (a b)"), 1.0, PS[:, 3, :],
                                             ALU.add, ALU.mult).then_inc(c_g, 1)
                    dve.wait_ge(c_g, t + 1)
                    after(dve, c_out, t - 1)
                    dve.tensor_tensor(Uc[u].rearrange("p a b -> p (a b)"), tg[u].rearrange("p a b -> p (a b)"), PS[:, 2, :], ALU.mult).then_inc(c_u, 1)

            def residual_c(t):
                if live(t):
                    dve.wait_ge(c_out, t + 1)
                    dve.scalar_tensor_tensor(xtile(t), PS[:, 0, 256:384], gates[:, 1:2], xtile(t), ALU.mult, ALU.add).then_inc(c_res, 1)

            def step_c(s, u):
                residual_c(s - 2)
                normalise_again(s + 1, 1 - u)
                softmax_c(s, u)
                mlp_c(s, u)
                sums_c(s, u)
                stats_c(s + 2, u)
                normalise_c(s + 2, u)

            pipelined(dve, step_c, 2, 2)

            dve.wait_ge(c_res, T)
            dve.wait_ge(c_tin, T)

            def stats_d(t, u):
                if live(t):
                    dve.bn_stats(dst_[u][:, 0:6], xtile(t)).then_inc(d_st, 1)
                    dve.wait_ge(d_st, t + 1)
                    dve.memset(spare[:, 0:1], 0.0)
                    dve.bn_aggr(dst_[u][:, 6:8], dst_[u][:, 0:6]).then_inc(d_mv, 1)

            def normalise_d(t, u):
                if live(t):
                    dve.wait_ge(d_rstd, t + 1)
                    after(dve, d_tz, t - 1)
                    dve.tensor_scalar(zn[u], xtile(t), dst_[u][:, 6:7], dst_[u][:, 9:10], ALU.subtract, ALU.mult).then_inc(d_zn, 1)

            def step_d(s, u):
                stats_d(s + 1, 1 - u)
                normalise_d(s, u)

            pipelined(dve, step_d, 1, 1)

            ZR = RT.rearrange("p (b s) -> p b s", s=SEQ)

            def expert_out(e):
                dve.wait_ge(d_yu, 3 * (e + 1))
                dve.tensor_scalar(ZR[:, :, e * CT:(e + 1) * CT], PS[:, 4 + e % 2, :].rearrange("p (b s) -> p b s", s=CT),
                                  gates[:, 3:4], None, ALU.mult).then_inc(d_r, 1)

            for j in range(E1 * 3):
                n = F1C[j % 3][1]
                dve.wait_ge(d_t, j + 1)
                dve.scalar_tensor_tensor(Td[j % 2][0:n, :], Td[j % 2][0:n, :], 1.0, PS[0:n, 2 * (j % 2), :], ALU.add, ALU.mult).then_inc(d_g, 1)
                dve.wait_ge(d_g, j + 1)
                after(dve, d_yu, j - 2)
                dve.tensor_tensor(Ud[j % 3][0:n, :], Td[j % 2][0:n, :], PS[0:n, 2 * (j % 2) + 1, :], ALU.mult).then_inc(d_u, 1)
                if j % 3 == 1 and j >= 3:
                    expert_out(j // 3 - 1)
            expert_out(E1 - 1)
            for g in range(G):
                dve.wait_ge(d_tr, g + 1)
                dve.tensor_tensor(X[:, g * GT:(g + 1) * GT, :], PS[:, 6 + g % 2, :].rearrange("p (k d) -> p k d", k=GT),
                                  X[:, g * GT:(g + 1) * GT, :], ALU.add).then_inc(d_x, 1)

        @block.tensor
        def _(pe):
            def scores(t, u):
                if live(t):
                    pe.wait_ge(a_q, t + 1)
                    pe.wait_ge(a_ked, t + 1)
                    pe.wait_ge(a_kep, t + 1)
                    after(pe, a_sub, t)
                    for h in range(2):
                        for b in range(2):
                            m = pe.matmul(PS[64 * b:64 * b + 64, 2 + h, :].rearrange("p (g m) -> p g m", m=SEQ),
                                          qT[u][:, 64 * b:64 * b + 64],
                                          KE[u][:, 8 * h:8 * h + 8, 64 * b:64 * b + 64], start=True, stop=True)
                    m.then_inc(a_s, 1)

            def turn_out(t, u):
                if live(t):
                    pe.wait_ge(a_on, t + 1)
                    after(pe, a_res, t)
                    pe.transpose(PS[:, 7, 0:128], On[u].rearrange("p g d -> p (g d)"), ident[:, :]).then_inc(a_to, 1)

            def turn_in(t, u):
                if live(t):
                    pe.wait_ge(a_xn, t + 1)
                    after(pe, a_xc, t * 2)
                    pe.wait_ge(ctx_loaded[u], t * 8 + (16 - 8 * u))
                    pe.transpose(PS[:, 0, 0:128], xn[u], ident[:, :])
                    pe.transpose(PS[:, 0, 128:256], cxb[u][:, :], ident[:, :]).then_inc(a_tin, 1)

            def turn_e(t, u):
                if live(t):
                    pe.wait_ge(a_exp, t + 1)
                    after(pe, a_et, t)
                    for k in range(HP):
                        m = pe.transpose(PS[:, 4 + k // 4, 128 * (k % 4):128 * (k % 4) + 128],
                                         Ea[u][:, 2 * k:2 * k + 2, :].rearrange("p g m -> p (g m)"), ident[:, :])
                    m.then_inc(a_te, 1)

            def project(t, u):
                if live(t):
                    pe.wait_ge(a_xc, t * 2 + 2)
                    after(pe, a_v, t * 2)
                    pe.matmul(PS[:, 1, 128:256], wk0_sb[:, :], xcT[u][:, 1, :], start=True, stop=True)
                    pe.matmul(PS[:, 1, 0:128], wq0_sb[:, :], xcT[u][:, 0, :], start=True, stop=True)
                    for b in range(2):
                        m = pe.matmul(PS[:, 1, 256 + 128 * b:384 + 128 * b], xcT[u][:, 2 + b, :], wv0_sb[:, :], start=True, stop=True)
                    m.then_inc(a_qkv, 1)

            def project_out(t, u):
                if live(t):
                    pe.wait_ge(a_ot, t + 1)
                    pe.matmul(PS[:, 7, 128:256], OTa[u], wo0_sb[:, :], start=True, stop=True).then_inc(a_pr, 1)

            def values(t, u):
                if live(t):
                    pe.wait_ge(a_et, t + 1)
                    pe.wait_ge(a_v, t * 2 + 2)
                    after(pe, a_on, t)
                    for k in range(HP):
                        for b in range(2):
                            m = pe.matmul(PS[64 * b:64 * b + 64, 6, VW * k:VW * k + VW], ETa[u][:, k, 64 * b:64 * b + 64],
                                          VB[u][:, b, k, :], start=True, stop=True)
                    m.then_inc(a_av, 1)

            def step(s, u):
                scores(s, u)
                turn_out(s - 2, u)
                turn_in(s + 1, 1 - u)
                turn_e(s - 1, 1 - u)
                project(s + 1, 1 - u)
                project_out(s - 2, u)
                values(s - 1, 1 - u)

            pe.wait_ge(small_loaded, 16 * N_SMALL)
            pe.wait_ge(ident_ready, 2)
            pipelined(pe, step, 1, 2)

            NB = E0 * FC0

            def turn_y(g):
                if live(g, G):
                    pe.wait_ge(b_yn, g + 1)
                    after(pe, b_yT, g)
                    for k in range(GT):
                        m = pe.transpose(PS[:, 6, 128 * k:128 * k + 128], yn[:, k, :], ident[:, :])
                    m.then_inc(b_ty, 1)

            def router(g, u):
                if live(g, G):
                    pe.wait_ge(b_yT, g + 1)
                    after(pe, b_lmx, g)
                    for k in range(GT):
                        m = pe.matmul(PS[:, 7, E0 * k:E0 * k + E0], yT[u][:, 128 * k:128 * k + 128], router_sb[:, :], start=True, stop=True)
                    m.then_inc(b_lg, 1)

            def up(g, j, u):
                e, c = j // FC0, j % FC0
                after(pe, b_u, g * NB + (j - 3))
                pe.matmul(PS[:, j % 4, :], w1_sb[:, e, 128 * c:128 * c + 128], yT[u], start=True, stop=True).then_inc(b_h, 1)

            def down(g, j):
                e, c = j // FC0, j % FC0
                pe.wait_ge(b_u, g * NB + (j + 1))
                if c == 0:
                    after(pe, b_acc, g * E0 + (e - 1))
                for k in range(GT):
                    m = pe.matmul(PS[:, 4 + e % 2, D * k:D * k + D], U[j % 4][:, 128 * k:128 * k + 128], w2_sb[:, e, c, :],
                                  start=(c == 0 and k == 0), stop=(c == FC0 - 1), skip_group_check=True)
                m.then_inc(b_yu, 1)

            def group_b(g, u, last=False):
                for j in range(NB):
                    if j == 11:
                        turn_y(g + 1)
                    if j == 15:
                        router(g + 1, 1 - u)
                    if j + 2 < NB:
                        up(g, j + 2, u)
                    elif not last:
                        up(g + 1, j + 2 - NB, 1 - u)
                    down(g, j)

            pe.wait_ge(w0_loaded, 32)
            turn_y(0)
            router(0, 0)
            up(0, 0, 0)
            up(0, 1, 0)
            group_b(0, 0)
            with pe.Fori(0, (G - 2) // 2) as i:
                group_b(i * 2 + 1, 1)
                group_b(i * 2 + 2, 0)
            group_b(G - 1, 1, last=True)

            def turn_in_c(t, u):
                if live(t):
                    pe.wait_ge(c_xn, t + 1)
                    after(pe, c_xc, t * 3)
                    after(pe, c_res, t - 2)
                    pe.transpose(PS[:, 0, 0:128], xn2[u][:, 0, :], ident[:, :])
                    pe.transpose(PS[:, 0, 128:256], xn2[u][:, 1, :], ident[:, :]).then_inc(c_tin, 1)

            def keys_values(t, u):
                if live(t):
                    pe.wait_ge(c_xc, t * 3 + 3)
                    after(pe, c_kve, t * 4)
                    pe.matmul(PS[:, 1, 0:128], wkv_sb[:, 0:128], xcT2[u][:, 1, :], start=True, stop=True)
                    for b in range(2):
                        m = pe.matmul(PS[:, 1, 128 + 128 * b:256 + 128 * b], xcT2[u][:, 2 + b, :], wkv_sb[:, 128:256], start=True, stop=True)
                    m.then_inc(c_kv, 1)

            def queries(t, u):
                if live(t):
                    after(pe, c_u, t)
                    for k in range(HP):
                        m = pe.matmul(PS[:, 2 + k // 4, 128 * (k % 4):128 * (k % 4) + 128], wq1_sb[:, 128 * k:128 * k + 128],
                                      xcT2[u][:, 0, :], start=True, stop=True)
                    m.then_inc(c_q, 1)

            def scores_c(t, u):
                if live(t):
                    pe.wait_ge(c_qe, t + 1)
                    pe.wait_ge(c_kve, t * 4 + 4)
                    after(pe, c_sub, t)
                    for k in range(HP):
                        for b in range(2):
                            m = pe.matmul(PS[64 * b:64 * b + 64, 4 + k // 4, 128 * (k % 4):128 * (k % 4) + 128],
                                          QT[u][:, k, 64 * b:64 * b + 64], KB[u][:, b, :, :].rearrange("p k m -> p (k m)"),
                                          start=True, stop=True)
                    m.then_inc(c_s, 1)

            def turn_e_c(t, u):
                if live(t):
                    pe.wait_ge(c_nrm, t + 1)
                    after(pe, c_ot, t)
                    for k in range(HP):
                        m = pe.transpose(PS[:, 6 + k // 4, 128 * (k % 4):128 * (k % 4) + 128],
                                         Ec[u][:, 2 * k:2 * k + 2, :].rearrange("p g m -> p (g m)"), ident[:, :])
                    m.then_inc(c_te, 1)

            def mlp_up(t, u):
                if live(t):
                    pe.wait_ge(c_qe, t + 1)
                    for k in range(2 * MC):
                        m = pe.matmul(PS[:, 2 + k // 4, 128 * (k % 4):128 * (k % 4) + 128], w1m_sb[:, 128 * k:128 * k + 128],
                                      xcT2[u][:, 0, :], start=True, stop=True)
                    m.then_inc(c_h, 1)

            def values_c(t, u):
                if live(t):
                    pe.wait_ge(c_et, t + 1)
                    for b in range(2):
                        m = pe.matmul(PS[:, 6 + b, :].rearrange("p (t l) -> p t l", t=HP), VC[u][:, b, :, :].rearrange("p k d -> p (k d)"),
                                      ETc[u][:, :, 64 * b:64 * b + 64], start=True, stop=True)
                    m.then_inc(c_o, 1)

            def project_c(t, u):
                if live(t):
                    pe.wait_ge(c_ot, t + 1)
                    pe.wait_ge(c_u, t + 1)
                    after(pe, c_res, t)
                    for k in range(MC):
                        pe.matmul(PS[:, 0, 256:384], Uc[u][:, k, :], w2m_sb[:, k, :], start=(k == 0), stop=False)
                    for k in range(HP):
                        m = pe.matmul(PS[:, 0, 256:384], OTc[u][:, k, :], wout_sb[:, k, :], start=False, stop=(k == HP - 1))
                    m.then_inc(c_out, 1)

            def step_c(s, u):
                scores_c(s, u)
                turn_e_c(s - 1, 1 - u)
                turn_in_c(s + 1, 1 - u)
                mlp_up(s, u)
                values_c(s - 1, 1 - u)
                keys_values(s + 1, 1 - u)
                queries(s + 1, 1 - u)
                project_c(s - 1, 1 - u)

            pe.wait_ge(w1l_loaded, 64)
            pe.wait_ge(b_acc, G * E0)
            pe.wait_ge(const_ready, 5)
            pipelined(pe, step_c, 1, 1)

            def turn_z(t, u):
                if live(t):
                    pe.wait_ge(d_zn, t + 1)
                    after(pe, d_zt, t - 1)
                    pe.transpose(PS[:, 6 + u, 0:128], zn[u], ident[:, :]).then_inc(d_tz, 1)

            pe.wait_ge(c_ot, T)
            pipelined(pe, turn_z, 0, 1)
            Z = ZT.rearrange("p (b s) -> p b s", s=SEQ)

            def up_d(j):
                e, (f, n) = j // 3, F1C[j % 3]
                after(pe, d_u, j - 1)
                z = Z[:, :, e * CT:(e + 1) * CT]
                for i, w in enumerate((w1e_sb, w3e_sb)):
                    m = pe.matmul(PS[0:n, 2 * (j % 2) + i, :].rearrange("p (b s) -> p b s", s=CT), w[:, e, f:f + n], z, start=True, stop=True)
                m.then_inc(d_h, 1)

            def down_d(j):
                e, c = j // 3, j % 3
                n = F1C[c][1]
                pe.wait_ge(d_u, j + 1)
                if c == 0:
                    after(pe, d_r, e - 1)
                pe.matmul(PS[:, 4 + e % 2, :], w2e_sb[0:n, e, c, :], Ud[j % 3][0:n, :], start=(c == 0), stop=(c == 2)).then_inc(d_yu, 1)

            pe.wait_ge(wd_loaded, 80)
            pe.wait_ge(d_zt, T)
            up_d(0)
            for j in range(E1 * 3):
                if j + 1 < E1 * 3:
                    up_d(j + 1)
                down_d(j)
            pe.wait_ge(d_r, E1)
            for g in range(G):
                after(pe, d_x, g - 1)
                for k in range(GT):
                    t = g * GT + k
                    m = pe.transpose(PS[:, 6 + g % 2, 128 * k:128 * k + 128], RT[:, 128 * t:128 * t + 128], ident[:, :])
                m.then_inc(d_tr, 1)


def kernel(**inputs):
    import numpy as np
    import concourse.bacc as bacc
    from concourse.bass_utils import run_bass_kernel_spmd

    a = {k: np.asarray(v) for k, v in inputs.items()}
    wk, wv = np.split(a["L1_xattn_Wkv"], 2, axis=1)
    laid = [
        ("x", a["x"]), ("ctx_in", a["ctx_1024"]), ("mask", a["mask_BxSxS2_ff0"]), ("g_xattn", a["g_xattn"]), ("g_ffn", a["g_ffn"]),
        ("wqT0", a["L0_xattn_Wq"].T), ("bq0", a["L0_xattn_bq"]), ("wkT0", a["L0_xattn_Wk"].T), ("bk0", a["L0_xattn_bk"]),
        ("wvT0", a["L0_xattn_Wv"].T), ("bv0", a["L0_xattn_bv"]), ("woT0", a["L0_xattn_Wo"].T), ("bo0", a["L0_xattn_bo"]),
        ("P0", np.repeat(a["L0_xattn_P"], HD0, axis=0)), ("routerT", a["L0_ffn_router_w"].T),
        ("w1T0", a["L0_ffn_w1"].transpose(2, 0, 1)),
        ("w2T0", a["L0_ffn_w2"].reshape(E0, D, FC0, 128).transpose(3, 0, 2, 1)),
        ("escale", a["L0_ffn_expert_scale"]),
        ("ln_g", a["L1_xattn_ln_g"]), ("ln_b", a["L1_xattn_ln_b"]), ("cln_g", a["L1_xattn_cln_g"]), ("cln_b", a["L1_xattn_cln_b"]),
        ("wq1", a["L1_xattn_Wq"]), ("wkv1", np.concatenate([wk, wk, wv, wv], axis=1)), ("wout1", a["L1_xattn_Wout"]),
        ("w1m", a["L1_xattn_W1"]), ("w2m", a["L1_xattn_W2"]),
        ("w1e", a["L1_ffn_w1"].transpose(1, 0, 2)), ("w3e", a["L1_ffn_w3"].transpose(1, 0, 2)), ("w2e", a["L1_ffn_w2"]),
    ]
    nc = bacc.Bacc("TRN2", target_bir_lowering=False, num_devices=1)
    arrays, args = {}, []
    for name, v in laid:
        v = np.ascontiguousarray(v)
        arrays[name] = v
        args.append(nc.dram_tensor(name, v.shape, mybir.dt.from_np(v.dtype), kind="ExternalInput").ap())
    args.append(nc.dram_tensor("out", a["x"].shape, F32, kind="ExternalOutput").ap())
    build(nc, *args)
    r = run_bass_kernel_spmd(nc, [arrays], core_ids=[0])
    return r.results[0]["out"]
```

```python
from contextlib import ExitStack

import concourse.bass as bass
from concourse import mybir

F32 = mybir.dt.float32
ALU = mybir.AluOpType
ACT = mybir.ActivationFunctionType
AX = mybir.AxisListType

D = 128
SEQ = 64
NSEQ = 64
TOK = 128
T = NSEQ * SEQ // TOK
H = 16
HP = H // 2
HD0 = D // H
HD1 = 64
E0 = 8
F0 = 512
FC0 = F0 // 128
REG = NSEQ * SEQ + 128
NS = (2 * NSEQ * SEQ + E0 * 127) // 128 + 1
SPARE = NS - 2 * NSEQ * SEQ // 128
ROWS = E0 * REG + SPARE * 128
GT = 4
G = T // GT
E1 = 8
F1 = 352
F1C = [(0, 128), (128, 128), (256, 96)]
CT = SEQ // E1
MLP = 512
MC = MLP // 128
EPS = 1e-5
assert NS % 2 == 0
KA = 5
OUT1 = 3
LINKS = 7
W_LINKS = 19
VW = 2 * (HD0 + 1)


def known(n):
    return isinstance(n, int)


def after(eng, sem, n):
    if not known(n) or n > 0:
        eng.wait_ge(sem, n)


def live(t, n=T):
    return not known(t) or 0 <= t < n


def pipelined(eng, step, lead, trail, n=T, lo=4):
    hi = n - lead - (n - lead) % 2
    for s in range(-lead, lo):
        step(s, s % 2)
    with eng.Fori(0, (hi - lo) // 2) as i:
        for u in range(2):
            step(i * 2 + (lo + u), u)
    for s in range(hi, n + trail):
        step(s, s % 2)


def build(nc, x, ctx_in, mask, g_xattn, g_ffn, wqT0, bq0, wkT0, bk0, wvT0, bv0, woT0, bo0, P0,
          routerT, w1T0, w2T0, escale, ln_g, ln_b, cln_g, cln_b, wq1, wkv1, wout1, w1m, w2m,
          w1e, w3e, w2e, shape_consts, out, y_rows, o_rows):
    with ExitStack() as ctx:
        def sb(name, *shape, dtype=F32):
            return ctx.enter_context(nc.sbuf_tensor(name, [128, *shape], dtype))

        def sem(name):
            return ctx.enter_context(nc.semaphore(name))

        X = sb("X", T, D)
        MK = sb("MK", T, SEQ)
        ident = sb("ident", 128)
        minus_half = sb("minus_half", GT)
        eps = sb("eps", GT)
        gates = sb("gates", 4)
        rawg = sb("rawg", 4)
        spare = sb("spare", 3)

        wq0_sb = sb("wq0_sb", D)
        wk0_sb = sb("wk0_sb", D)
        wv0_sb = sb("wv0_sb", D)
        wo0_sb = sb("wo0_sb", D)
        bias0 = sb("bias0", 3)
        bk_scaled = sb("bk_scaled", 1)
        Pc = sb("Pc", H)
        gbo = sb("gbo", D)
        router_sb = sb("router_sb", E0)
        escale_sb = sb("escale_sb", E0)
        tri = sb("tri", E0, E0)
        lnv = sb("lnv", 4)
        wkv_sb = sb("wkv_sb", 256)
        wq1_sb = sb("wq1_sb", H * HD1)
        wout_sb = sb("wout_sb", HP, D)
        w1m_sb = sb("w1m_sb", 2 * MLP)
        w2m_sb = sb("w2m_sb", MC, D)

        w1_sb = sb("w1_sb", E0, F0)
        w2_sb = sb("w2_sb", E0, FC0, D)
        w1e_sb = sb("w1e_sb", E1, F1)
        w3e_sb = sb("w3e_sb", E1, F1)
        w2e_sb = sb("w2e_sb", E1, len(F1C), D)
        consts = sb("consts", E0 + T + NS)
        wide = sb("wide", 129)
        PR = sb("PR", T, E0)
        RK = sb("RK", T, E0)
        POS = sb("POS", T, 2)
        MR = sb("MR", T, 2)
        CF = sb("CF", 2, T)
        rows_used = sb("rows_used", E0)
        pool_spare = sb("pool_spare", 1)
        zeros = sb("zeros", D)
        BF = mybir.dt.bfloat16
        before_bf = sb("before_bf", 128, dtype=BF)
        ones_bf = sb("ones_bf", 128, dtype=BF)
        ohb = sb("ohb", 2, E0, dtype=BF)
        ixs = [sb(f"ixs{u}", 2, dtype=mybir.dt.uint32) for u in range(2)]
        ixp = sb("ixp", E0, dtype=mybir.dt.uint32)
        emap = sb("emap", NS, dtype=mybir.dt.int32)
        rmap = sb("rmap", NS, dtype=mybir.dt.int32)
        cxb = [sb(f"cxb{u}", D) for u in range(2)]

        SIZES = {"ac": 13 * 1024 + 512, "bd": 7 * 1024 + 256}
        arenas = {k: sb(f"arena_{k}", n) for k, n in SIZES.items()}
        at = {}

        def part(which, *shape):
            n = 1
            for d in shape:
                n *= d
            lo = at.get(which, 0)
            at[which] = lo + n
            assert at[which] <= SIZES[which], (which, at)
            a = arenas[which][:, lo:lo + n]
            if len(shape) == 1:
                return a
            names = "abcd"[:len(shape)]
            return a.rearrange(f"p ({' '.join(names)}) -> p {' '.join(names)}",
                               **dict(zip(names[1:], shape[1:])))

        xn = [part("ac", D) for _ in range(2)]
        xcT = [part("ac", 4, 128) for _ in range(2)]
        qT = [part("ac", TOK) for _ in range(2)]
        kT = [part("ac", TOK) for _ in range(2)]
        KE = [part("ac", H, TOK) for _ in range(2)]
        VB = [part("ac", 2, HP, VW) for _ in range(2)]
        Ea = [part("ac", H, SEQ) for _ in range(2)]
        ETa = [part("ac", HP, TOK) for _ in range(2)]
        On = [part("ac", H, HD0) for _ in range(2)]
        OTa = [part("ac", TOK) for _ in range(2)]
        stat = [part("ac", 16) for _ in range(2)]
        mx = [part("ac", H) for _ in range(2)]
        rs = [part("ac", H) for _ in range(2)]
        ystat = [part("bd", 16) for _ in range(2)]
        yn = [part("bd", D) for _ in range(2)]
        yt = [part("bd", TOK) for _ in range(2)]
        yst = [part("bd", D) for _ in range(2)]
        lmx = part("bd", 2)
        lsum = part("bd", 2)
        lg = part("bd", 2, E0)
        ex = part("bd", 2, E0)
        dif = part("bd", 2, E0, E0)
        tie = part("bd", 2, E0, E0)
        slot = part("bd", 2, E0)
        picked = part("bd", 2, 2, E0)
        cnt = part("bd", E0)
        cmpj = part("bd", E0, T)
        ntl = part("bd", E0)
        before = part("bd", E0, E0)
        ends = part("bd", E0)
        hop = part("bd", E0)
        past = part("bd", NS, E0)
        mapf = part("bd", 2, NS)
        at["bd"] = 0
        ST = [part("bd", D) for _ in range(2)]
        yTs = [part("bd", TOK) for _ in range(2)]
        Th = [part("bd", F0) for _ in range(2)]
        U = [part("bd", F0) for _ in range(2)]
        UT = [part("bd", FC0, TOK) for _ in range(2)]
        OT = [part("bd", D) for _ in range(2)]
        shift = part("bd", E0)
        pick = part("bd", T, E0)
        p12 = part("bd", 2, T)
        cw = part("bd", 3, T)
        Gt = [part("bd", 2, D) for _ in range(2)]
        at["ac"] = 0
        xn2 = [part("ac", 2, D) for _ in range(2)]
        xcT2 = [part("ac", 4, 128) for _ in range(2)]
        QT = [part("ac", HP, TOK) for _ in range(2)]
        KB = [part("ac", 2, 2, SEQ) for _ in range(2)]
        VC = [part("ac", 2, 2, HD1) for _ in range(2)]
        Ec = [part("ac", H, SEQ) for _ in range(2)]
        ETc = [part("ac", HP, TOK) for _ in range(2)]
        OTc = [part("ac", HP, TOK) for _ in range(2)]
        tg = [part("ac", MC, TOK) for _ in range(2)]
        Uc = [part("ac", MC, TOK) for _ in range(2)]
        cst = [part("ac", 40) for _ in range(2)]
        cmx = [part("ac", H) for _ in range(2)]
        csum = [part("ac", H) for _ in range(2)]
        cinv = [part("ac", H) for _ in range(2)]
        at["bd"] = 0
        zn = [part("bd", D) for _ in range(2)]
        dst_ = [part("bd", 16) for _ in range(2)]
        ZT = part("bd", T * TOK)
        Td = [part("bd", 512) for _ in range(2)]
        Ud = [part("bd", 512) for _ in range(3)]
        at["ac"] = 0
        RT = part("ac", T * TOK)
        PS = ctx.enter_context(nc.psum_tensor("PS", [128, 8, 512], F32))

        small_loaded = sem("small_loaded")
        x_loaded = [sem(f"x_loaded{i}") for i in range(4)]
        w0_loaded = sem("w0_loaded")
        ctx_loaded = [sem(f"ctx_loaded{u}") for u in range(2)]
        w1l_loaded = sem("w1l_loaded")
        wd_loaded = sem("wd_loaded")
        ident_zero = sem("ident_zero")
        ident_ready = sem("ident_ready")
        half_ready = sem("half_ready")
        gates_ready = sem("gates_ready")
        const_ready = sem("const_ready")
        vb_zero = sem("vb_zero")
        a_st = sem("a_st"); a_mv = sem("a_mv"); a_eps = sem("a_eps"); a_rstd = sem("a_rstd"); a_xn = sem("a_xn"); a_xb = sem("a_xb")
        a_tin = sem("a_tin"); a_xc = sem("a_xc"); a_qk = sem("a_qk"); a_qkv = sem("a_qkv"); a_k = sem("a_k"); a_q = sem("a_q"); a_v = sem("a_v")
        a_ked = sem("a_ked"); a_kep = sem("a_kep"); a_kea = sem("a_kea"); a_s = sem("a_s"); a_mx = sem("a_mx"); a_sub = sem("a_sub"); a_exp = sem("a_exp")
        a_te = sem("a_te"); a_et = sem("a_et"); a_av = sem("a_av"); a_rc = sem("a_rc"); a_on = sem("a_on"); a_to = sem("a_to")
        a_ot = sem("a_ot"); a_pr = sem("a_pr"); a_res = sem("a_res")
        y_st = sem("y_st"); y_mv = sem("y_mv"); y_eps = sem("y_eps"); y_rstd = sem("y_rstd"); y_saved = sem("y_saved")
        y_n = sem("y_n"); y_tin = sem("y_tin"); y_t = sem("y_t"); r_logits = sem("r_logits"); r_rank = sem("r_rank"); r_max = sem("r_max"); r_slot = sem("r_slot")
        r_shift = sem("r_shift"); r_exp = sem("r_exp"); r_two = sem("r_two"); r_count = sem("r_count"); r_counted = sem("r_counted"); r_pos = sem("r_pos")
        yst_ready = sem("yst_ready"); ix_ready = sem("ix_ready"); pad_ix = sem("pad_ix")
        scattered = [sem(f"scattered{u}") for u in range(2)]
        padded = [sem(f"padded{e}") for e in range(E0)]; trash_zero = sem("trash_zero"); zeros_ready = sem("zeros_ready")
        consts_loaded = sem("consts_loaded"); route_const = sem("route_const")
        m_link = sem("m_link"); map_ready = sem("map_ready"); w_link = sem("w_link"); w_dif = sem("w_dif"); w_exp = sem("w_exp")
        st_loaded = [sem(f"st_loaded{u}") for u in range(2)]
        o_stored = [sem(f"o_stored{u}") for u in range(2)]
        b_ty = sem("b_ty"); b_yT = sem("b_yT"); b_h = sem("b_h"); b_t = sem("b_t"); b_u = sem("b_u"); b_tu = sem("b_tu"); b_uT = sem("b_uT")
        b_y = sem("b_y"); b_o = sem("b_o")
        g_ix = sem("g_ix"); g_sum = sem("g_sum"); g_add = sem("g_add")
        gathered = [sem(f"gathered{u}") for u in range(2)]
        c_ch = sem("c_ch"); c_ch2 = sem("c_ch2"); c_add = sem("c_add"); c_mv = sem("c_mv"); c_eps = sem("c_eps"); c_rstd = sem("c_rstd"); c_xn = sem("c_xn"); c_tin = sem("c_tin"); c_xc = sem("c_xc")
        c_kv = sem("c_kv"); c_kve = sem("c_kve"); c_q = sem("c_q"); c_qe = sem("c_qe"); c_s = sem("c_s"); c_mx = sem("c_mx")
        c_sub = sem("c_sub"); c_exp = sem("c_exp"); c_sum = sem("c_sum"); c_inv = sem("c_inv"); c_nrm = sem("c_nrm"); c_te = sem("c_te"); c_et = sem("c_et")
        c_o = sem("c_o"); c_ot = sem("c_ot"); c_h = sem("c_h"); c_t = sem("c_t"); c_g = sem("c_g"); c_u = sem("c_u"); c_out = sem("c_out"); c_res = sem("c_res")
        kb_zero = sem("kb_zero")
        d_st = sem("d_st"); d_mv = sem("d_mv"); d_eps = sem("d_eps"); d_rstd = sem("d_rstd"); d_zn = sem("d_zn"); d_tz = sem("d_tz"); d_zt = sem("d_zt")
        d_h = sem("d_h"); d_t = sem("d_t"); d_g = sem("d_g"); d_u = sem("d_u"); d_yu = sem("d_yu"); d_r = sem("d_r"); d_tr = sem("d_tr"); d_x = sem("d_x")
        stored = sem("stored")

        block = ctx.enter_context(nc.Block())

        x_t = x.rearrange("(t b) s d -> (b s) t d", b=2)
        c_t_in = ctx_in.rearrange("(t b) s d -> (b s) t d", b=2)
        out_t = out.rearrange("(t b) s d -> (b s) t d", b=2)
        LC = T // 4
        N_SMALL = 19

        @block.sync
        def _(sp):
            def load_x(i):
                sl = slice(i * LC, (i + 1) * LC)
                sp.dma_start(X[:, sl, :], x_t[:, sl, :]).then_inc(x_loaded[i], 16)

            load_x(0)
            smalls = ((wq0_sb[:, :], wqT0), (wk0_sb[:, :], wkT0), (wv0_sb[:, :], wvT0), (wo0_sb[:, :], woT0),
                      (bias0[:, 0:1], bq0.unsqueeze(1)), (bias0[:, 1:2], bk0.unsqueeze(1)),
                      (bias0[:, 2:3], bv0.unsqueeze(1)),
                      (gbo[:, :], bo0.unsqueeze(0).broadcast_to([128, D])),
                      (rawg[:, 0:2], g_xattn.unsqueeze(0).broadcast_to([128, 2])),
                      (rawg[:, 2:4], g_ffn.unsqueeze(0).broadcast_to([128, 2])),
                      (escale_sb[:, :], escale.unsqueeze(0).broadcast_to([128, E0])),
                      (router_sb[:, :], routerT),
                      (lnv[:, 0:1], ln_g.unsqueeze(1)), (lnv[:, 1:2], ln_b.unsqueeze(1)),
                      (lnv[:, 2:3], cln_g.unsqueeze(1)), (lnv[:, 3:4], cln_b.unsqueeze(1)),
                      (wkv_sb[:, :], wkv1), (Pc[:, :], P0), (w2m_sb[:, :, :], w2m.rearrange("(c p) d -> p c d", p=128)))
            assert len(smalls) == N_SMALL
            for dst, src in smalls:
                sp.dma_start(dst, src).then_inc(small_loaded, 16)

            def load_ctx(t, u, sem_free, free):
                after(sp, sem_free, free)
                sp.dma_start(cxb[u][:, :], c_t_in[:, bass.ts(t, 1), :].squeeze(1)).then_inc(ctx_loaded[u], 16)

            sp.dma_start(consts[:, :], shape_consts[0:1, 0:E0 + T + NS].broadcast_to([128, E0 + T + NS])).then_inc(consts_loaded, 16)
            sp.dma_start(wide[:, :], shape_consts[1:129, :]).then_inc(consts_loaded, 16)
            load_ctx(0, 0, a_tin, 0)
            load_ctx(1, 1, a_tin, 0)
            for i in range(1, 4):
                load_x(i)
            sp.dma_start(w1_sb[:, :, :], w1T0).then_inc(w0_loaded, 16)
            sp.dma_start(w2_sb[:, :, :, :], w2T0).then_inc(w0_loaded, 16)
            with sp.Fori(1, T // 2) as i:
                for u in range(2):
                    load_ctx(i * 2 + u, u, a_tin, i * 2 + (u - 1))
            sp.dma_start(MK[:, :, :], mask.rearrange("(t b) s m -> (b s) t m", b=2)).then_inc(w1l_loaded, 16)
            sp.dma_start(wq1_sb[:, :], wq1).then_inc(w1l_loaded, 16)
            sp.dma_start(wout_sb[:, :, :], wout1.rearrange("(t p) d -> p t d", p=128)).then_inc(w1l_loaded, 16)
            sp.dma_start(w1m_sb[:, :], w1m).then_inc(w1l_loaded, 16)
            sp.dma_start(w1e_sb[:, :, :], w1e).then_inc(wd_loaded, 16)
            sp.dma_start(w3e_sb[:, :, :], w3e).then_inc(wd_loaded, 16)
            for c, (f, n) in enumerate(F1C):
                sp.dma_start(w2e_sb[0:n, :, c, :], w2e[:, f:f + n, :].rearrange("e f d -> f e d")).then_inc(wd_loaded, 16)
            def load_slot(i, u):
                if live(i, NS):
                    after(sp, b_ty, i - 1)
                    if known(i) and i < E0:
                        sp.wait_ge(padded[i], 16)
                    row = sp.value_load(rmap[0:1, bass.ds(i, 1)], min_val=0, max_val=ROWS - 128)
                    sp.dma_start(ST[u], y_rows[bass.ds(row, 128), :]).then_inc(st_loaded[u], 16)

            def store_slot(i, u):
                if live(i, NS):
                    sp.wait_ge(b_o, i + 1)
                    sp.dma_start(o_rows[bass.ts(i, 128), :], OT[u]).then_inc(o_stored[u], 16)

            def step_b(s, u):
                load_slot(s + 3, 1 - u)
                store_slot(s - 3, 1 - u)

            sp.wait_ge(map_ready, 2)
            sp.wait_ge(trash_zero, 16)
            for u in range(2):
                sp.wait_ge(scattered[u], 16 * T)
            pipelined(sp, step_b, 3, 3, n=NS, lo=6)
            load_ctx(0, 0, a_tin, T)
            load_ctx(1, 1, a_tin, T)
            with sp.Fori(1, T // 2) as i:
                for u in range(2):
                    load_ctx(i * 2 + u, u, c_mv, i * 4 + (2 * u - 2))
            for g in range(G):
                sp.wait_ge(d_x, g + 1)
                sl = slice(g * GT, (g + 1) * GT)
                sp.dma_start(out_t[:, sl, :], X[:, sl, :]).then_inc(stored, 16)
            sp.wait_ge(stored, 16 * G)

        @block.gpsimd
        def _(pool):
            pool.memset(ident[:, :], 0.0).then_inc(ident_zero, 1)
            pool.memset(minus_half[:, :], -0.5).then_inc(half_ready, 1)
            pool.memset(eps[:, :], EPS).then_inc(half_ready, 1)
            pool.memset(tri[:, :, :], 0.0).then_inc(ident_zero, 1)
            pool.wait_ge(ident_zero, 2)
            pool.affine_select(out=ident[:, :], in_=ident[:, :], compare_op=ALU.not_equal, fill=1.0, base=0,
                               pattern=[[-1, 128]], channel_multiplier=1).then_inc(ident_ready, 1)
            pool.affine_select(out=tri[:, :, :], in_=tri[:, :, :], compare_op=ALU.is_ge, fill=1.0, base=0,
                               pattern=[[-1, E0], [1, E0]], channel_multiplier=0).then_inc(ident_ready, 1)
            pool.memset(zeros[:, :], 0.0).then_inc(zeros_ready, 1)
            pool.wait_ge(zeros_ready, 1)
            pool.dma_start(y_rows[E0 * REG:ROWS, :].rearrange("(k p) d -> p k d", p=128),
                           zeros[:, :].unsqueeze(1).to_broadcast([128, SPARE, D])).then_inc(trash_zero, 16)
            pool.wait_ge(half_ready, 2)
            pool.wait_ge(const_ready, 2)

            def rstd(t, u):
                if live(t):
                    pool.wait_ge(a_mv, t + 1)
                    pool.tensor_tensor(stat[u][:, 8:9], stat[u][:, 7:8], eps[:, 0:1], ALU.add).then_inc(a_eps, 1)
                    pool.wait_ge(a_eps, t + 1)
                    pool.tensor_tensor(stat[u][:, 9:10], stat[u][:, 8:9], minus_half[:, 0:1], ALU.pow).then_inc(a_rstd, 1)

            def scale_k(t, u):
                if live(t):
                    pool.wait_ge(a_k, t + 1)
                    pool.tensor_tensor(KE[u][:, HP:H, :], kT[u].unsqueeze(1).to_broadcast([128, HP, TOK]),
                                       Pc[:, HP:H].unsqueeze(2).to_broadcast([128, HP, TOK]), ALU.mult).then_inc(a_kep, 1)

            def add_bias(t):
                if live(t):
                    pool.wait_ge(a_xn, t + 1)
                    pool.tensor_tensor(X[:, bass.ts(t, 1), :].squeeze(1), X[:, bass.ts(t, 1), :].squeeze(1), gbo[:, :], ALU.add).then_inc(a_xb, 1)

            def rstd_y(t, u):
                if live(t):
                    pool.wait_ge(y_mv, t + 1)
                    pool.tensor_tensor(ystat[u][:, 8:9], ystat[u][:, 7:8], eps[:, 0:1], ALU.add).then_inc(y_eps, 1)
                    pool.wait_ge(y_eps, t + 1)
                    pool.tensor_tensor(ystat[u][:, 7:8], ystat[u][:, 8:9], minus_half[:, 0:1], ALU.pow).then_inc(y_rstd, 1)
                    pool.wait_ge(y_rstd, t + 1)
                    pool.tensor_copy(MR[:, bass.ts(t, 1), :].squeeze(1), ystat[u][:, 6:8]).then_inc(y_saved, 1)

            def scatter(t, u):
                if live(t):
                    pool.wait_ge(r_pos, t + 1)
                    after(pool, scattered[u], t * 16 - 16 * u)
                    pool.tensor_copy(ixs[u][:, :], POS[:, bass.ts(t, 1), :].squeeze(1)).then_inc(ix_ready, 1)
                    pool.wait_ge(ix_ready, t + 1)
                    pool.wait_ge(yst_ready, t + 1)
                    pool.tensor_tensor(pool_spare[:, :], eps[:, 0:1], eps[:, 0:1], ALU.add)
                    for r in range(2):
                        pool.indirect_dma_start(y_rows, bass.IndirectOffsetOnAxis(ap=ixs[u][:, r:r + 1], axis=0), yst[u], None).then_inc(scattered[u], 16)

            def step(s, u):
                scatter(s - 9, 1 - u)
                scale_k(s + 1, 1 - u)
                add_bias(s)
                rstd(s + 3, 1 - u)
                rstd_y(s - 2, u)

            pipelined(pool, step, 3, 10, lo=10)

            pool.wait_ge(pad_ix, 1)
            for e in range(E0):
                pool.indirect_dma_start(y_rows, bass.IndirectOffsetOnAxis(ap=ixp[:, e:e + 1], axis=0), zeros[:, :], None).then_inc(padded[e], 16)


            def rstd_c(t, u, k):
                if live(t):
                    pool.wait_ge(c_mv, t * 2 + (k + 1))
                    a = 12 if k == 0 else 28
                    n = 2 if k == 0 else 1
                    pool.tensor_tensor(cst[u][:, a + 4:a + 4 + n], cst[u][:, a + 1:a + 2 * n:2], eps[:, 0:n], ALU.add).then_inc(c_eps, 1)
                    pool.wait_ge(c_eps, t * 2 + (k + 1))
                    pool.tensor_tensor(cst[u][:, a + 6:a + 6 + n], cst[u][:, a + 4:a + 4 + n], minus_half[:, 0:n], ALU.pow).then_inc(c_rstd, 1)

            def divide(t, u):
                if live(t):
                    pool.wait_ge(c_inv, t + 1)
                    pool.tensor_tensor(Ec[u], Ec[u], cinv[u].unsqueeze(2).to_broadcast([128, H, SEQ]), ALU.mult).then_inc(c_nrm, 1)

            def gather(t, u):
                if live(t):
                    after(pool, gathered[u], t * 16 - 16 * u)
                    pool.tensor_copy(ixs[u][:, :], POS[:, bass.ts(t, 1), :].squeeze(1)).then_inc(g_ix, 1)
                    pool.wait_ge(g_ix, t + 1)
                    after(pool, g_sum, t - 1)
                    pool.tensor_tensor(pool_spare[:, :], eps[:, 0:1], eps[:, 0:1], ALU.add)
                    for r in range(2):
                        pool.indirect_dma_start(Gt[u][:, r, :], None, o_rows, bass.IndirectOffsetOnAxis(ap=ixs[u][:, r:r + 1], axis=0)).then_inc(gathered[u], 16)

            def step_c(s, u):
                divide(s, u)
                rstd_c(s + 2, u, 0)
                rstd_c(s + 2, u, 1)
                gather(s + 4, u)

            for u in range(2):
                pool.wait_ge(scattered[u], 16 * T)
                pool.wait_ge(w_link, W_LINKS)
                pool.wait_ge(o_stored[u], 8 * NS)
            pipelined(pool, step_c, 4, 0)

            def rstd_d(t, u):
                pool.wait_ge(d_mv, t + 1)
                pool.tensor_tensor(dst_[u][:, 8:9], dst_[u][:, 7:8], eps[:, 0:1], ALU.add).then_inc(d_eps, 1)
                pool.wait_ge(d_eps, t + 1)
                pool.tensor_tensor(dst_[u][:, 9:10], dst_[u][:, 8:9], minus_half[:, 0:1], ALU.pow).then_inc(d_rstd, 1)

            with pool.Fori(0, T // 2) as i:
                for u in range(2):
                    rstd_d(i * 2 + u, u)

        @block.scalar
        def _(act):
            act.wait_ge(small_loaded, 16 * N_SMALL)
            act.activation(gates[:, :], rawg[:, :], ACT.Tanh).then_inc(gates_ready, 1)
            act.wait_ge(const_ready, 1)

            def out_t_copy(t, u):
                if live(t):
                    act.wait_ge(a_to, t + 1)
                    act.activation(OTa[u], PS[:, 7, 0:128], ACT.Identity, bias=bias0[:, 2:3]).then_inc(a_ot, 1)

            def in_copy(t, u):
                if live(t):
                    act.wait_ge(a_tin, t + 1)
                    after(act, a_qkv, t - 1)
                    act.copy(xcT[u][:, 0:2, :], PS[:, 0, 0:256].rearrange("p (a b) -> p a b", a=2)).then_inc(a_xc, 1)
                    act.copy(xcT[u][:, 2:4, :].rearrange("p b (k m) -> p b k m", k=2),
                             PS[:, 0, 128:256].rearrange("p (b m) -> p b m", b=2).unsqueeze(2).to_broadcast([128, 2, 2, SEQ])).then_inc(a_xc, 1)

            def e_t_copy(t, u):
                if live(t):
                    act.wait_ge(a_te, t + 1)
                    act.copy(ETa[u], PS[:, 4:6, :].rearrange("p a (b c) -> p (a b) c", b=4)).then_inc(a_et, 1)

            def qk_copy(t, u):
                if live(t):
                    act.wait_ge(a_qk, t + 1)
                    after(act, a_ked, t - 1)
                    after(act, a_kep, t - 1)
                    after(act, a_kea, t - 1)
                    act.activation(kT[u], PS[:, 1, 128:256], ACT.Identity, bias=bk_scaled[:, 0:1], scale=HD0 ** -0.5).then_inc(a_k, 1)
                    act.activation(qT[u], PS[:, 1, 0:128], ACT.Identity, bias=bias0[:, 0:1]).then_inc(a_q, 1)

            def scale_k(t, u):
                if live(t):
                    act.wait_ge(a_k, t + 1)
                    for g in range(HP - KA, HP):
                        m = act.activation(KE[u][:, g, :], kT[u], ACT.Identity, scale=Pc[:, g:g + 1])
                    m.then_inc(a_kea, 1)

            def v_copy(t, u):
                if live(t):
                    act.wait_ge(a_qkv, t + 1)
                    after(act, a_av, t - 1)
                    v = PS[:, 1, 256:512].rearrange("p (b t k d) -> p b t k d", b=2, t=HP, k=2)
                    vb = VB[u].rearrange("p b t (k d) -> p b t k d", k=2)
                    for k in range(2):
                        act.copy(vb[64 * k:64 * k + 64, :, :, k, 0:HD0], v[64 * k:64 * k + 64, :, :, k, :]).then_inc(a_v, 1)

            def exps(t, u):
                if live(t):
                    act.wait_ge(a_sub, t + 1)
                    act.activation(Ea[u], Ea[u], ACT.Exp).then_inc(a_exp, 1)

            def y_copy(t, u):
                if live(t):
                    act.wait_ge(y_tin, t + 1)
                    after(act, r_logits, t - 1)
                    act.copy(yt[u], PS[:, 0, 256:384]).then_inc(y_t, 1)

            def router_exp(t):
                if live(t):
                    act.wait_ge(r_shift, t + 2)
                    after(act, r_rank, t * LINKS - (2 * LINKS - 6))
                    act.activation(ex, lg, ACT.Exp).then_inc(r_exp, 2)

            def step(s, u):
                if u == 1:
                    router_exp(s - 7)
                v_copy(s, u)
                out_t_copy(s - 2, u)
                qk_copy(s + 1, 1 - u)
                e_t_copy(s - 1, 1 - u)
                scale_k(s + 1, 1 - u)
                in_copy(s + 2, u)
                y_copy(s - 4, u)
                exps(s, u)

            act.wait_ge(vb_zero, 6)
            pipelined(act, step, 2, 10, lo=10)

            def tanh_b(i, u):
                if live(i, NS):
                    act.wait_ge(b_h, i + 1)
                    after(act, b_u, i - 1)
                    act.activation(Th[u], PS[:, 1 + u, :], ACT.Tanh, scale=0.5).then_inc(b_t, 1)

            def u_t_copy(i, u):
                if live(i, NS):
                    act.wait_ge(b_tu, i + 1)
                    after(act, b_y, i - 1)
                    act.copy(UT[u], PS[:, 3 + u, :].rearrange("p (c t) -> p c t", c=FC0)).then_inc(b_uT, 1)

            def step_b(s, u):
                u_t_copy(s - 2, u)
                tanh_b(s, u)
                if known(s) and s == 1:
                    act.wait_ge(w_dif, 1)
                    act.activation(cw[:, 1, :], cw[:, 0, :], ACT.Exp).then_inc(w_exp, 1)

            act.wait_ge(map_ready, 2)
            pipelined(act, step_b, 0, 2, n=NS)

            def in_copy_c(t, u):
                if live(t):
                    act.wait_ge(c_tin, t + 1)
                    after(act, c_h, t - 1)
                    act.activation(xcT2[u][:, 0, :], PS[:, 0, 0:128], ACT.Identity, bias=lnv[:, 1:2], scale=lnv[:, 0:1]).then_inc(c_xc, 1)
                    act.activation(xcT2[u][:, 1, :], PS[:, 0, 128:256], ACT.Identity, bias=lnv[:, 3:4], scale=lnv[:, 2:3]).then_inc(c_xc, 1)
                    act.activation(xcT2[u][:, 2:4, :].rearrange("p b (k m) -> p b k m", k=2),
                                   PS[:, 0, 128:256].rearrange("p (b m) -> p b m", b=2).unsqueeze(2).to_broadcast([128, 2, 2, SEQ]),
                                   ACT.Identity, bias=lnv[:, 3:4], scale=lnv[:, 2:3]).then_inc(c_xc, 1)

            def kv_copy(t, u):
                if live(t):
                    act.wait_ge(c_kv, t + 1)
                    after(act, c_o, t - 1)
                    for k in range(2):
                        q = slice(64 * k, 64 * k + 64)
                        act.mul(KB[u][q, :, k, :], PS[q, 1, 0:128].rearrange("p (b m) -> p b m", b=2), HD1 ** -0.5).then_inc(c_kve, 1)
                        act.copy(VC[u][q, :, k, :], PS[q, 1, 128:384].rearrange("p (b k d) -> p b k d", b=2, k=2)[:, :, k, :]).then_inc(c_kve, 1)

            def q_copy(t, u):
                if live(t):
                    act.wait_ge(c_q, t + 1)
                    act.copy(QT[u], PS[:, 2:4, :].rearrange("p a (b c) -> p (a b) c", b=4)).then_inc(c_qe, 1)

            def exps_c(t, u):
                if live(t):
                    act.wait_ge(c_sub, t + 1)
                    act.activation(Ec[u], Ec[u], ACT.Exp).then_inc(c_exp, 1)

            def e_t_copy_c(t, u):
                if live(t):
                    act.wait_ge(c_te, t + 1)
                    act.copy(ETc[u], PS[:, 6:8, :].rearrange("p a (b c) -> p (a b) c", b=4)).then_inc(c_et, 1)

            def tanh_c(t, u):
                if live(t):
                    act.wait_ge(c_h, t + 1)
                    act.activation(tg[u], PS[:, 3, :].rearrange("p (a b) -> p a b", a=MC), ACT.Tanh, scale=0.5).then_inc(c_t, 1)

            def o_t_copy(t, u):
                if live(t):
                    act.wait_ge(c_o, t + 1)
                    act.copy(OTc[u].rearrange("p t (b l) -> p b t l", b=2),
                             PS[:, 6:8, :].rearrange("p b (t l) -> p b t l", t=HP)).then_inc(c_ot, 1)

            def step_c(s, u):
                e_t_copy_c(s - 1, 1 - u)
                in_copy_c(s + 1, 1 - u)
                tanh_c(s, u)
                exps_c(s, u)
                o_t_copy(s - 1, 1 - u)
                kv_copy(s + 1, 1 - u)
                q_copy(s + 1, 1 - u)

            act.wait_ge(kb_zero, 4)
            pipelined(act, step_c, 1, 1)

            act.wait_ge(c_res, T)
            with act.Fori(0, T // 2) as i:
                for u in range(2):
                    t = i * 2 + u
                    act.wait_ge(d_tz, t + 1)
                    act.copy(ZT[:, bass.ts(t, 128)], PS[:, 6 + u, 0:128]).then_inc(d_zt, 1)
            for j in range(E1 * 3):
                n = F1C[j % 3][1]
                act.wait_ge(d_h, j + 1)
                after(act, d_u, j - 1)
                act.activation(Td[j % 2][0:n, :], PS[0:n, 2 * (j % 2), :], ACT.Tanh, scale=0.5).then_inc(d_t, 1)

        @block.vector
        def _(dve):
            for p in range(2):
                dve.memset(VB[p], 0.0).then_inc(vb_zero, 1)
            dve.wait_ge(vb_zero, 2)
            for p in range(2):
                dve.memset(VB[p][0:64, :, :, HD0:HD0 + 1], 1.0).then_inc(vb_zero, 1)
                dve.memset(VB[p][64:128, :, :, VW - 1:VW], 1.0).then_inc(vb_zero, 1)
            dve.wait_ge(small_loaded, 16 * N_SMALL)
            dve.tensor_scalar(bk_scaled[:, :], bias0[:, 1:2], HD0 ** -0.5, None, ALU.mult).then_inc(const_ready, 1)
            dve.wait_ge(gates_ready, 1)
            dve.tensor_scalar(gbo[:, :], gbo[:, :], gates[:, 0:1], None, ALU.mult).then_inc(const_ready, 1)
            dve.tensor_scalar(w2m_sb[:, :, :], w2m_sb[:, :, :], 0.5, None, ALU.mult).then_inc(const_ready, 1)
            dve.tensor_scalar(escale_sb[:, :], escale_sb[:, :], gates[:, 2:3], 0.5, ALU.mult, ALU.mult).then_inc(const_ready, 1)
            dve.tensor_scalar(gates[:, 3:4], gates[:, 3:4], 0.5, None, ALU.mult).then_inc(const_ready, 1)
            dve.wait_ge(consts_loaded, 32)
            dve.tensor_copy(before_bf[:, :], wide[:, 0:128]).then_inc(route_const, 1)
            dve.memset(ones_bf[:, :], 1.0).then_inc(route_const, 1)
            dve.tensor_copy(rows_used[:, :], consts[:, 0:E0]).then_inc(route_const, 1)
            dve.wait_ge(const_ready, 5)
            dve.wait_ge(route_const, 3)
            dve.wait_ge(ident_ready, 2)

            def xtile(t):
                return X[:, bass.ts(t, 1), :].squeeze(1)

            def stats(t, ty, u):
                if live(t):
                    dve.bn_stats(stat[1 - u][:, 0:6], xtile(t)).then_inc(a_st, 1)
                if live(ty):
                    dve.wait_ge(a_res, ty + 1)
                    after(dve, y_saved, ty - 1)
                    dve.memset(spare[:, 1:2], 0.0)
                    dve.bn_stats(ystat[u][:, 0:6], xtile(ty)).then_inc(y_st, 1)
                if live(t):
                    dve.wait_ge(a_st, t + 1)
                    dve.memset(spare[:, 0:1], 0.0)
                    dve.bn_aggr(stat[1 - u][:, 6:8], stat[1 - u][:, 0:6]).then_inc(a_mv, 1)
                if live(ty):
                    dve.wait_ge(y_st, ty + 1)
                    dve.memset(spare[:, 2:3], 0.0)
                    dve.bn_aggr(ystat[u][:, 6:8], ystat[u][:, 0:6]).then_inc(y_mv, 1)

            def normalise_y(t, u):
                if live(t):
                    dve.wait_ge(y_rstd, t + 1)
                    after(dve, y_tin, t - 1)
                    dve.tensor_scalar(yn[u], xtile(t), ystat[u][:, 6:7], ystat[u][:, 7:8], ALU.subtract, ALU.mult).then_inc(y_n, 1)

            def rows_for_scatter(t, u):
                if live(t):
                    dve.wait_ge(y_saved, t + 1)
                    after(dve, scattered[u], t * 16 - 16 * u)
                    dve.tensor_scalar(yst[u], xtile(t), MR[:, bass.ts(t, 1), 0:1].squeeze(1), MR[:, bass.ts(t, 1), 1:2].squeeze(1),
                                      ALU.subtract, ALU.mult).then_inc(yst_ready, 1)

            v3 = [128, 2, E0]
            v4 = [128, 2, E0, E0]

            def pair(buf, t):
                return buf[:, bass.ds(t, 2), :]

            def ranked(t, k):
                dve.wait_ge(r_rank, t * LINKS + 2 * k)

            def route(t, k):
                if not live(t):
                    return
                L = PS[:, 6, 256:272].rearrange("p (k e) -> p k e", k=2)
                P = PS[:, 6, 272:288].rearrange("p (k e) -> p k e", k=2)
                if k == 1:
                    dve.wait_ge(r_logits, t + 2)
                    dve.reduce_max(lmx, L, AX.X).then_inc(r_max, 2)
                    dve.wait_ge(r_max, t + 2)
                    after(dve, r_exp, t)
                    dve.tensor_tensor(lg, L, lmx.unsqueeze(2).to_broadcast(v3), ALU.subtract).then_inc(r_shift, 2)
                if k == 2:
                    dve.wait_ge(r_exp, t + 2)
                    dve.reduce_sum(lsum, ex, AX.X).then_inc(r_rank, 2)
                if k == 3:
                    ranked(t, 1)
                    dve.reciprocal(lsum, lsum).then_inc(r_rank, 2)
                if k == 4:
                    ranked(t, 2)
                    dve.tensor_tensor(pair(PR, t), ex, lsum.unsqueeze(2).to_broadcast(v3), ALU.mult).then_inc(r_rank, 2)
                if k == 5:
                    ranked(t, 3)
                    dve.tensor_tensor(dif, pair(PR, t).unsqueeze(2).to_broadcast(v4), pair(PR, t).unsqueeze(3).to_broadcast(v4), ALU.subtract).then_inc(r_rank, 2)
                if k == 6:
                    ranked(t, 4)
                    dve.scalar_tensor_tensor(tie, dif, 0.0, tri[:, :, :].unsqueeze(1).to_broadcast(v4), ALU.is_equal, ALU.mult).then_inc(r_rank, 2)
                if k == 7:
                    ranked(t, 5)
                    dve.scalar_tensor_tensor(dif, dif, 0.0, tie, ALU.is_gt, ALU.add).then_inc(r_rank, 2)
                if k == 8:
                    ranked(t, 6)
                    dve.reduce_sum(pair(RK, t), dif, AX.X).then_inc(r_rank, 2)
                if k == 9:
                    ranked(t, 7)
                    after(dve, r_count, t)
                    dve.tensor_scalar(ohb[:, :, :], pair(RK, t), 2.0, None, ALU.is_lt).then_inc(r_two, 2)
                if k == 10:
                    dve.wait_ge(r_count, t + 2)
                    after(dve, r_counted, t)
                    dve.tensor_tensor(slot, P, rows_used[:, :].unsqueeze(1).to_broadcast(v3), ALU.add).then_inc(r_slot, 2)
                if k == 11:
                    dve.wait_ge(r_slot, t * 3 + 2)
                    dve.tensor_tensor(rows_used[:, :], rows_used[:, :], PS[:, 6, 288:296], ALU.add).then_inc(r_counted, 2)
                    for r in range(2):
                        dve.scalar_tensor_tensor(picked[:, :, r, :], pair(RK, t), float(r), slot, ALU.is_equal, ALU.mult).then_inc(r_slot, 2)
                if k == 12:
                    dve.wait_ge(r_slot, t * 3 + 6)
                    dve.reduce_sum(pair(POS, t), picked, AX.X).then_inc(r_pos, 2)

            def normalise(t, u):
                if live(t):
                    dve.wait_ge(a_rstd, t + 1)
                    after(dve, a_tin, t - 1)
                    dve.tensor_scalar(xn[u], xtile(t), stat[u][:, 6:7], stat[u][:, 9:10], ALU.subtract, ALU.mult).then_inc(a_xn, 1)

            def softmax(t, u):
                if live(t):
                    S = PS[:, 2:4, :].rearrange("p a (g m) -> p (a g) m", g=8)
                    dve.wait_ge(a_s, t + 1)
                    dve.reduce_max(mx[u], S, AX.X).then_inc(a_mx, 1)
                    dve.wait_ge(a_mx, t + 1)
                    after(dve, a_te, t - 1)
                    dve.tensor_tensor(Ea[u], S, mx[u].unsqueeze(2).to_broadcast([128, H, SEQ]), ALU.subtract).then_inc(a_sub, 1)

            def scale_k(t, u):
                if live(t):
                    dve.wait_ge(a_k, t + 1)
                    for g in range(HP - KA):
                        m = dve.tensor_scalar(KE[u][:, g, :], kT[u], Pc[:, g:g + 1], None, ALU.mult)
                    m.then_inc(a_ked, 1)

            def normalise_out(t, u):
                if live(t):
                    O = PS[:, 6, 0:HP * VW].rearrange("p (g d) -> p g d", g=H)
                    dve.wait_ge(a_av, t + 1)
                    dve.reciprocal(rs[u], O[:, :, HD0]).then_inc(a_rc, 1)
                    dve.wait_ge(a_rc, t + 1)
                    after(dve, a_to, t - 1)
                    dve.tensor_tensor(On[u], O[:, :, 0:HD0], rs[u].unsqueeze(2).to_broadcast([128, H, HD0]), ALU.mult).then_inc(a_on, 1)

            def residual(t):
                if live(t):
                    dve.wait_ge(a_pr, t + 1)
                    dve.wait_ge(a_xb, t + 1)
                    dve.scalar_tensor_tensor(xtile(t), PS[:, 7, 128:256], gates[:, 0:1], xtile(t), ALU.mult, ALU.add).then_inc(a_res, 1)

            def step(s, u):
                softmax(s, u)
                if u == 1:
                    route(s - 7, 2)
                normalise(s + 2, u)
                if u == 1:
                    route(s - 7, 3)
                normalise_y(s - 3, 1 - u)
                if u == 1:
                    route(s - 7, 4)
                if known(s) and s == 0:
                    for q in x_loaded[1:]:
                        dve.wait_ge(q, 16)
                scale_k(s + 1, 1 - u)
                if u == 1:
                    route(s - 7, 5)
                residual(s - 2)
                if u == 1:
                    route(s - 7, 6)
                stats(s + 3, s - 2, u)
                if u == 1:
                    route(s - 7, 7)
                normalise_out(s - 1, 1 - u)
                if u == 1:
                    route(s - 7, 8)
                if u == 0:
                    route(s - 8, 10)
                    route(s - 6, 1)
                    route(s - 8, 11)
                    route(s - 8, 12)
                rows_for_scatter(s - 8, u)
                if u == 1:
                    route(s - 7, 9)

            dve.wait_ge(x_loaded[0], 16)
            pipelined(dve, step, 3, 10, lo=10)
            dve.wait_ge(a_res, T)
            dve.wait_ge(r_counted, T)
            dve.tensor_scalar(ixp[:, :], rows_used[:, :], wide[:, 128:129], None, ALU.add).then_inc(pad_ix, 1)

            links = {"n": 0}

            def link(ins, sem_):
                links["n"] += 1
                ins.then_inc(sem_, 1)
                dve.wait_ge(sem_, links["n"])

            tile_no = consts[:, E0 + T:E0 + T + NS]
            e8 = [128, E0, E0]
            link(dve.tensor_tensor(cnt, rows_used[:, :], consts[:, 0:E0], ALU.subtract), m_link)
            link(dve.tensor_tensor(cmpj, cnt.unsqueeze(2).to_broadcast([128, E0, T]),
                                   consts[:, E0:E0 + T].unsqueeze(1).to_broadcast([128, E0, T]), ALU.is_gt), m_link)
            link(dve.reduce_sum(ntl, cmpj, AX.X), m_link)
            link(dve.tensor_tensor(before, tri[:, :, :], ntl.unsqueeze(1).to_broadcast(e8), ALU.mult), m_link)
            link(dve.reduce_sum(ends, before, AX.X), m_link)
            link(dve.scalar_tensor_tensor(shift, ends, -128.0, consts[:, 0:E0], ALU.mult, ALU.add), m_link)
            link(dve.tensor_tensor(ends, ends, ntl, ALU.add), m_link)
            link(dve.tensor_scalar(hop, ntl, -128.0, float(REG), ALU.mult, ALU.add), m_link)
            link(dve.tensor_tensor(past, tile_no.unsqueeze(2).to_broadcast([128, NS, E0]),
                                   ends.unsqueeze(1).to_broadcast([128, NS, E0]), ALU.is_ge), m_link)
            link(dve.reduce_sum(mapf[:, 0, :], past, AX.X), m_link)
            dve.tensor_scalar(emap[:, :], mapf[:, 0, :], float(E0 - 1), None, ALU.min).then_inc(map_ready, 1)
            link(dve.tensor_tensor(past, past, hop.unsqueeze(1).to_broadcast([128, NS, E0]), ALU.mult), m_link)
            link(dve.reduce_sum(mapf[:, 1, :], past, AX.X), m_link)
            dve.scalar_tensor_tensor(rmap[:, :], tile_no, 128.0, mapf[:, 1, :], ALU.mult, ALU.add).then_inc(map_ready, 1)

            def weights(n):
                scales = escale_sb[:, :].unsqueeze(1).to_broadcast([128, T, E0])
                if n == 0:
                    links["n"] = 0
                    for r in range(2):
                        link(dve.scalar_tensor_tensor(pick, RK[:, :, :], float(r), PR[:, :, :], ALU.is_equal, ALU.mult), w_link)
                        link(dve.reduce_sum(p12[:, r, :], pick, AX.X), w_link)
                    dve.tensor_tensor(cw[:, 0, :], p12[:, 1, :], p12[:, 0, :], ALU.subtract).then_inc(w_dif, 1)
                if n == 1:
                    for r in range(2):
                        link(dve.scalar_tensor_tensor(pick, RK[:, :, :], float(r), scales, ALU.is_equal, ALU.mult), w_link)
                        link(dve.reduce_sum(p12[:, r, :], pick, AX.X), w_link)
                if n == 2:
                    dve.wait_ge(w_exp, 1)
                    link(dve.tensor_scalar(cw[:, 2, :], cw[:, 1, :], 1.0, None, ALU.add), w_link)
                    link(dve.reciprocal(cw[:, 0, :], cw[:, 2, :]), w_link)
                    link(dve.tensor_tensor(cw[:, 2, :], cw[:, 1, :], cw[:, 0, :], ALU.mult), w_link)
                    link(dve.tensor_tensor(CF[:, 0, :], p12[:, 0, :], cw[:, 0, :], ALU.mult), w_link)
                    link(dve.tensor_tensor(CF[:, 1, :], p12[:, 1, :], cw[:, 2, :], ALU.mult), w_link)
                if n == 3:
                    dve.wait_ge(ix_ready, T)
                    for r in range(2):
                        link(dve.scalar_tensor_tensor(pick, RK[:, :, :], float(r), shift.unsqueeze(1).to_broadcast([128, T, E0]), ALU.is_equal, ALU.mult), w_link)
                        link(dve.reduce_sum(p12[:, r, :], pick, AX.X), w_link)
                        link(dve.tensor_tensor(POS[:, :, r], POS[:, :, r], p12[:, r, :], ALU.subtract), w_link)
                    assert links["n"] == W_LINKS

            def y_t_copy(i, u):
                if live(i, NS):
                    dve.wait_ge(b_ty, i + 1)
                    after(dve, b_h, i - 1)
                    dve.tensor_copy(yTs[u], PS[:, 0, 0:128]).then_inc(b_yT, 1)

            def silu(i, u):
                if live(i, NS):
                    dve.wait_ge(b_t, i + 1)
                    after(dve, b_tu, i - 1)
                    dve.scalar_tensor_tensor(U[u], Th[u], 1.0, PS[:, 1 + u, :], ALU.add, ALU.mult).then_inc(b_u, 1)

            def slot_out(i, u):
                if live(i, NS):
                    dve.wait_ge(b_y, i + 1)
                    after(dve, o_stored[u], i * 8 - 8 * u)
                    dve.tensor_copy(OT[u], PS[:, 5 + u, 0:D]).then_inc(b_o, 1)

            def step_b(s, u):
                y_t_copy(s + 1, 1 - u)
                slot_out(s - 3, 1 - u)
                silu(s, u)
                if known(s) and 0 <= s < 4:
                    weights(s)

            pipelined(dve, step_b, 1, 3, n=NS)
            for p in range(2):
                dve.memset(KB[p], 0.0).then_inc(kb_zero, 1)
                dve.memset(VC[p], 0.0).then_inc(kb_zero, 1)

            def add_experts(t, u):
                if live(t):
                    dve.wait_ge(gathered[u], t * 16 + (32 - 16 * u))
                    dve.scalar_tensor_tensor(xtile(t), Gt[u][:, 0, :], CF[:, 0, bass.ts(t, 1)], xtile(t), ALU.mult, ALU.add).then_inc(g_add, 1)
                    dve.wait_ge(g_add, t + 1)
                    dve.scalar_tensor_tensor(xtile(t), Gt[u][:, 1, :], CF[:, 1, bass.ts(t, 1)], xtile(t), ALU.mult, ALU.add).then_inc(g_sum, 1)

            def stats_c(t, u):
                if live(t):
                    s = cst[u]
                    dve.wait_ge(ctx_loaded[u], t * 8 + (8 * T + 16 - 8 * u))
                    dve.wait_ge(g_sum, t + 1)
                    dve.memset(spare[:, 1:2], 0.0)
                    dve.bn_stats(s[:, 0:6], xtile(t)).then_inc(c_ch, 1)
                    dve.bn_stats(s[:, 6:12], cxb[u][:, :]).then_inc(c_ch, 1)
                    dve.wait_ge(c_ch, t * 2 + 2)
                    dve.memset(spare[:, 0:1], 0.0)
                    dve.bn_aggr(s[:, 12:14], s[:, 0:6])
                    dve.bn_aggr(s[:, 14:16], s[:, 6:12]).then_inc(c_mv, 1)

            def normalise_c(t, u):
                if live(t):
                    s = cst[u]
                    dve.wait_ge(c_rstd, t * 2 + 1)
                    after(dve, c_tin, t - 1)
                    dve.tensor_scalar(xn2[u][:, 0, :], xtile(t), s[:, 12:13], s[:, 18:19], ALU.subtract, ALU.mult).then_inc(c_ch2, 1)
                    dve.tensor_scalar(xn2[u][:, 1, :], cxb[u][:, :], s[:, 14:15], s[:, 19:20], ALU.subtract, ALU.mult)
                    dve.wait_ge(c_ch2, t * 2 + 1)
                    dve.bn_stats(s[:, 20:26], xn2[u][:, 0, :]).then_inc(c_ch2, 1)
                    dve.wait_ge(c_ch2, t * 2 + 2)
                    dve.memset(spare[:, 0:1], 0.0)
                    dve.bn_aggr(s[:, 28:30], s[:, 20:26]).then_inc(c_mv, 1)

            def normalise_again(t, u):
                if live(t):
                    s = cst[u]
                    dve.wait_ge(c_rstd, t * 2 + 2)
                    dve.tensor_scalar(xn2[u][:, 0, :], xn2[u][:, 0, :], s[:, 28:29], s[:, 34:35], ALU.subtract, ALU.mult).then_inc(c_xn, 1)

            def softmax_c(t, u):
                if live(t):
                    S = PS[:, 4:6, :].rearrange("p a (g m) -> p (a g) m", g=8)
                    dve.wait_ge(c_s, t + 1)
                    after(dve, c_te, t - 1)
                    dve.tensor_tensor(Ec[u], S, MK[:, bass.ts(t, 1), :].to_broadcast([128, H, SEQ]), ALU.add).then_inc(c_add, 1)
                    dve.wait_ge(c_add, t + 1)
                    dve.reduce_max(cmx[u], Ec[u], AX.X).then_inc(c_mx, 1)
                    dve.wait_ge(c_mx, t + 1)
                    dve.tensor_tensor(Ec[u], Ec[u], cmx[u].unsqueeze(2).to_broadcast([128, H, SEQ]), ALU.subtract).then_inc(c_sub, 1)

            def sums_c(t, u):
                if live(t):
                    dve.wait_ge(c_exp, t + 1)
                    dve.reduce_sum(csum[u], Ec[u], AX.X).then_inc(c_sum, 1)
                    dve.wait_ge(c_sum, t + 1)
                    dve.reciprocal(cinv[u], csum[u]).then_inc(c_inv, 1)

            def mlp_c(t, u):
                if live(t):
                    dve.wait_ge(c_t, t + 1)
                    dve.scalar_tensor_tensor(tg[u].rearrange("p a b -> p (a b)"), tg[u].rearrange("p a b -> p (a b)"), 1.0, PS[:, 3, :],
                                             ALU.add, ALU.mult).then_inc(c_g, 1)
                    dve.wait_ge(c_g, t + 1)
                    after(dve, c_out, t - 1)
                    dve.tensor_tensor(Uc[u].rearrange("p a b -> p (a b)"), tg[u].rearrange("p a b -> p (a b)"), PS[:, 2, :], ALU.mult).then_inc(c_u, 1)

            def residual_c(t):
                if live(t):
                    dve.wait_ge(c_out, t + 1)
                    dve.scalar_tensor_tensor(xtile(t), PS[:, 0, 256:384], gates[:, 1:2], xtile(t), ALU.mult, ALU.add).then_inc(c_res, 1)

            def step_c(s, u):
                residual_c(s - 2)
                normalise_again(s + 1, 1 - u)
                softmax_c(s, u)
                mlp_c(s, u)
                sums_c(s, u)
                stats_c(s + 2, u)
                add_experts(s + 3, 1 - u)
                normalise_c(s + 2, u)

            pipelined(dve, step_c, 3, 2)

            dve.wait_ge(c_res, T)
            dve.wait_ge(c_tin, T)

            def stats_d(t, u):
                if live(t):
                    dve.bn_stats(dst_[u][:, 0:6], xtile(t)).then_inc(d_st, 1)
                    dve.wait_ge(d_st, t + 1)
                    dve.memset(spare[:, 0:1], 0.0)
                    dve.bn_aggr(dst_[u][:, 6:8], dst_[u][:, 0:6]).then_inc(d_mv, 1)

            def normalise_d(t, u):
                if live(t):
                    dve.wait_ge(d_rstd, t + 1)
                    after(dve, d_tz, t - 1)
                    dve.tensor_scalar(zn[u], xtile(t), dst_[u][:, 6:7], dst_[u][:, 9:10], ALU.subtract, ALU.mult).then_inc(d_zn, 1)

            def step_d(s, u):
                stats_d(s + 1, 1 - u)
                normalise_d(s, u)

            pipelined(dve, step_d, 1, 1)

            ZR = RT.rearrange("p (b s) -> p b s", s=SEQ)

            def expert_out(e):
                dve.wait_ge(d_yu, 3 * (e + 1))
                dve.tensor_scalar(ZR[:, :, e * CT:(e + 1) * CT], PS[:, 4 + e % 2, :].rearrange("p (b s) -> p b s", s=CT),
                                  gates[:, 3:4], None, ALU.mult).then_inc(d_r, 1)

            for j in range(E1 * 3):
                n = F1C[j % 3][1]
                dve.wait_ge(d_t, j + 1)
                dve.scalar_tensor_tensor(Td[j % 2][0:n, :], Td[j % 2][0:n, :], 1.0, PS[0:n, 2 * (j % 2), :], ALU.add, ALU.mult).then_inc(d_g, 1)
                dve.wait_ge(d_g, j + 1)
                after(dve, d_yu, j - 2)
                dve.tensor_tensor(Ud[j % 3][0:n, :], Td[j % 2][0:n, :], PS[0:n, 2 * (j % 2) + 1, :], ALU.mult).then_inc(d_u, 1)
                if j % 3 == 1 and j >= 3:
                    expert_out(j // 3 - 1)
            expert_out(E1 - 1)
            for g in range(G):
                dve.wait_ge(d_tr, g + 1)
                dve.tensor_tensor(X[:, g * GT:(g + 1) * GT, :], PS[:, 6 + g % 2, :].rearrange("p (k d) -> p k d", k=GT),
                                  X[:, g * GT:(g + 1) * GT, :], ALU.add).then_inc(d_x, 1)

        @block.tensor
        def _(pe):
            def scores(t, u):
                if live(t):
                    pe.wait_ge(a_q, t + 1)
                    pe.wait_ge(a_ked, t + 1)
                    pe.wait_ge(a_kep, t + 1)
                    pe.wait_ge(a_kea, t + 1)
                    after(pe, a_sub, t)
                    for h in range(2):
                        for b in range(2):
                            m = pe.matmul(PS[64 * b:64 * b + 64, 2 + h, :].rearrange("p (g m) -> p g m", m=SEQ),
                                          qT[u][:, 64 * b:64 * b + 64],
                                          KE[u][:, 8 * h:8 * h + 8, 64 * b:64 * b + 64], start=True, stop=True)
                    m.then_inc(a_s, 1)

            def turn_out(t, u):
                if live(t):
                    pe.wait_ge(a_on, t + 1)
                    after(pe, a_res, t)
                    pe.transpose(PS[:, 7, 0:128], On[u].rearrange("p g d -> p (g d)"), ident[:, :]).then_inc(a_to, 1)

            def turn_y(t, u):
                if live(t):
                    pe.wait_ge(y_n, t + 1)
                    after(pe, a_xc, t * 2 + 12 if not known(t) else min(2 * T, t * 2 + 12))
                    after(pe, y_t, t)
                    pe.transpose(PS[:, 0, 256:384], yn[u], ident[:, :]).then_inc(y_tin, 1)

            def turn_in(t, u):
                if live(t):
                    pe.wait_ge(a_xn, t + 1)
                    after(pe, a_xc, t * 2)
                    after(pe, y_t, t - 6)
                    pe.wait_ge(ctx_loaded[u], t * 8 + (16 - 8 * u))
                    pe.transpose(PS[:, 0, 0:128], xn[u], ident[:, :])
                    pe.transpose(PS[:, 0, 128:256], cxb[u][:, :], ident[:, :]).then_inc(a_tin, 1)

            def turn_e(t, u):
                if live(t):
                    pe.wait_ge(a_exp, t + 1)
                    after(pe, a_et, t)
                    for k in range(HP):
                        m = pe.transpose(PS[:, 4 + k // 4, 128 * (k % 4):128 * (k % 4) + 128],
                                         Ea[u][:, 2 * k:2 * k + 2, :].rearrange("p g m -> p (g m)"), ident[:, :])
                    m.then_inc(a_te, 1)

            def project(t, u):
                if live(t):
                    pe.wait_ge(a_xc, t * 2 + 2)
                    after(pe, a_v, t * 2)
                    pe.matmul(PS[:, 1, 128:256], wk0_sb[:, :], xcT[u][:, 1, :], start=True, stop=True)
                    pe.matmul(PS[:, 1, 0:128], wq0_sb[:, :], xcT[u][:, 0, :], start=True, stop=True).then_inc(a_qk, 1)

            def project_v(t, u):
                if live(t):
                    pe.wait_ge(a_q, t + 1)
                    for b in range(2):
                        m = pe.matmul(PS[:, 1, 256 + 128 * b:384 + 128 * b], xcT[u][:, 2 + b, :], wv0_sb[:, :], start=True, stop=True)
                    m.then_inc(a_qkv, 1)

            def project_out(t, u):
                if live(t):
                    pe.wait_ge(a_ot, t + 1)
                    pe.matmul(PS[:, 7, 128:256], OTa[u], wo0_sb[:, :], start=True, stop=True).then_inc(a_pr, 1)

            def values(t, u):
                if live(t):
                    pe.wait_ge(a_et, t + 1)
                    pe.wait_ge(a_v, t * 2 + 2)
                    for k in range(HP):
                        for b in range(2):
                            m = pe.matmul(PS[64 * b:64 * b + 64, 6, VW * k:VW * k + VW], ETa[u][:, k, 64 * b:64 * b + 64],
                                          VB[u][:, b, k, :], start=True, stop=True)
                    m.then_inc(a_av, 1)

            def bank6_free(s, u):
                def upto(n):
                    return max(0, min(T, n)) if known(s) else n
                after(pe, a_on, upto(s - 1))
                after(pe, r_shift, upto(s - 6 + u))
                after(pe, r_counted, upto(s - 8 + u))

            def router(t, u):
                if live(t):
                    pe.wait_ge(y_t, t + 1)
                    pe.matmul(PS[:, 6, 256 + E0 * u:256 + E0 * u + E0], yt[u], router_sb[:, :], start=True, stop=True).then_inc(r_logits, 1)

            def count(t):
                if live(t):
                    pe.wait_ge(r_two, t + 2)
                    pe.matmul(PS[:, 6, 272:280], before_bf[:, :], ohb[:, 0, :], start=True, stop=True)
                    pe.matmul(PS[:, 6, 280:288], before_bf[:, :], ohb[:, 1, :], start=True, stop=False)
                    pe.matmul(PS[:, 6, 280:288], ones_bf[:, :], ohb[:, 0, :], start=False, stop=True)
                    pe.matmul(PS[:, 6, 288:296], ones_bf[:, :], ohb[:, 0, :], start=True, stop=False)
                    pe.matmul(PS[:, 6, 288:296], ones_bf[:, :], ohb[:, 1, :], start=False, stop=True).then_inc(r_count, 2)

            def step(s, u):
                scores(s, u)
                turn_out(s - 2, u)
                project(s + 1, 1 - u)
                turn_e(s - 1, 1 - u)
                project_out(s - 2, u)
                project_v(s + 1, 1 - u)
                bank6_free(s, u)
                router(s - 5, 1 - u)
                if u == 0:
                    count(s - 8)
                turn_y(s - 4, u)
                turn_in(s + 2, u)
                values(s - 1, 1 - u)

            pe.wait_ge(small_loaded, 16 * N_SMALL)
            pe.wait_ge(ident_ready, 2)
            pe.wait_ge(route_const, 3)
            pipelined(pe, step, 2, 10, lo=10)

            def turn_slot(i, u):
                if live(i, NS):
                    pe.wait_ge(st_loaded[u], i * 8 + (16 - 8 * u))
                    after(pe, b_yT, i)
                    pe.transpose(PS[:, 0, 0:128], ST[u], ident[:, :]).then_inc(b_ty, 1)

            def expert_of(i):
                if live(i, NS):
                    return pe.value_load(emap[0:1, bass.ds(i, 1)], min_val=0, max_val=E0 - 1)

            def up(i, u, e):
                if live(i, NS):
                    pe.wait_ge(b_yT, i + 1)
                    after(pe, b_u, i - 1)
                    pe.matmul(PS[:, 1 + u, :], yTs[u], w1_sb[:, bass.ds(e, 1), :].squeeze(1), start=True, stop=True).then_inc(b_h, 1)

            def turn_u(i, u):
                if live(i, NS):
                    pe.wait_ge(b_u, i + 1)
                    after(pe, b_uT, i - 1)
                    for c in range(FC0):
                        m = pe.transpose(PS[:, 3 + u, 128 * c:128 * c + 128], U[u][:, 128 * c:128 * c + 128], ident[:, :])
                    m.then_inc(b_tu, 1)

            def down(i, u, e):
                if live(i, NS):
                    pe.wait_ge(b_uT, i + 1)
                    after(pe, b_o, i - 1)
                    for c in range(FC0):
                        m = pe.matmul(PS[:, 5 + u, 0:D], UT[u][:, c, :], w2_sb[:, bass.ds(e, 1), c, :].squeeze(1), start=(c == 0), stop=(c == FC0 - 1))
                    m.then_inc(b_y, 1)

            def step_b(s, u):
                turn_slot(s + 1, 1 - u)
                turn_u(s - 2, u)
                e_down = expert_of(s - 3)
                down(s - 3, 1 - u, e_down)
                e_up = expert_of(s)
                up(s, u, e_up)

            pe.wait_ge(w0_loaded, 32)
            pe.wait_ge(map_ready, 2)
            pe.wait_ge(r_counted, T)
            pipelined(pe, step_b, 1, 3, n=NS)

            def turn_in_c(t, u):
                if live(t):
                    pe.wait_ge(c_xn, t + 1)
                    after(pe, c_xc, t * 3)
                    after(pe, c_res, t - 2)
                    pe.transpose(PS[:, 0, 0:128], xn2[u][:, 0, :], ident[:, :])
                    pe.transpose(PS[:, 0, 128:256], xn2[u][:, 1, :], ident[:, :]).then_inc(c_tin, 1)

            def keys_values(t, u):
                if live(t):
                    pe.wait_ge(c_xc, t * 3 + 3)
                    after(pe, c_kve, t * 4)
                    pe.matmul(PS[:, 1, 0:128], wkv_sb[:, 0:128], xcT2[u][:, 1, :], start=True, stop=True)
                    for b in range(2):
                        m = pe.matmul(PS[:, 1, 128 + 128 * b:256 + 128 * b], xcT2[u][:, 2 + b, :], wkv_sb[:, 128:256], start=True, stop=True)
                    m.then_inc(c_kv, 1)

            def queries(t, u):
                if live(t):
                    after(pe, c_u, t)
                    for k in range(HP):
                        m = pe.matmul(PS[:, 2 + k // 4, 128 * (k % 4):128 * (k % 4) + 128], wq1_sb[:, 128 * k:128 * k + 128],
                                      xcT2[u][:, 0, :], start=True, stop=True)
                    m.then_inc(c_q, 1)

            def scores_c(t, u):
                if live(t):
                    pe.wait_ge(c_qe, t + 1)
                    pe.wait_ge(c_kve, t * 4 + 4)
                    after(pe, c_sub, t)
                    for k in range(HP):
                        for b in range(2):
                            m = pe.matmul(PS[64 * b:64 * b + 64, 4 + k // 4, 128 * (k % 4):128 * (k % 4) + 128],
                                          QT[u][:, k, 64 * b:64 * b + 64], KB[u][:, b, :, :].rearrange("p k m -> p (k m)"),
                                          start=True, stop=True)
                    m.then_inc(c_s, 1)

            def turn_e_c(t, u):
                if live(t):
                    pe.wait_ge(c_nrm, t + 1)
                    after(pe, c_ot, t)
                    for k in range(HP):
                        m = pe.transpose(PS[:, 6 + k // 4, 128 * (k % 4):128 * (k % 4) + 128],
                                         Ec[u][:, 2 * k:2 * k + 2, :].rearrange("p g m -> p (g m)"), ident[:, :])
                    m.then_inc(c_te, 1)

            def mlp_up(t, u):
                if live(t):
                    pe.wait_ge(c_qe, t + 1)
                    for k in range(2 * MC):
                        m = pe.matmul(PS[:, 2 + k // 4, 128 * (k % 4):128 * (k % 4) + 128], w1m_sb[:, 128 * k:128 * k + 128],
                                      xcT2[u][:, 0, :], start=True, stop=True)
                    m.then_inc(c_h, 1)

            def values_c(t, u):
                if live(t):
                    pe.wait_ge(c_et, t + 1)
                    for b in range(2):
                        m = pe.matmul(PS[:, 6 + b, :].rearrange("p (t l) -> p t l", t=HP), VC[u][:, b, :, :].rearrange("p k d -> p (k d)"),
                                      ETc[u][:, :, 64 * b:64 * b + 64], start=True, stop=True)
                    m.then_inc(c_o, 1)

            def project_c(t, u, first):
                if live(t):
                    if first:
                        pe.wait_ge(c_u, t + 1)
                        after(pe, c_res, t)
                        for k in range(MC):
                            pe.matmul(PS[:, 0, 256:384], Uc[u][:, k, :], w2m_sb[:, k, :], start=(k == 0), stop=False)
                        pe.wait_ge(c_ot, t + 1)
                    for k in range(0, OUT1) if first else range(OUT1, HP):
                        m = pe.matmul(PS[:, 0, 256:384], OTc[u][:, k, :], wout_sb[:, k, :], start=False, stop=(k == HP - 1))
                    if not first:
                        m.then_inc(c_out, 1)

            def step_c(s, u):
                scores_c(s, u)
                turn_e_c(s - 1, 1 - u)
                turn_in_c(s + 1, 1 - u)
                mlp_up(s, u)
                values_c(s - 1, 1 - u)
                keys_values(s + 1, 1 - u)
                project_c(s - 1, 1 - u, True)
                queries(s + 1, 1 - u)
                project_c(s - 1, 1 - u, False)

            pe.wait_ge(w1l_loaded, 64)
            pe.wait_ge(b_o, NS)
            pe.wait_ge(const_ready, 5)
            pipelined(pe, step_c, 1, 1)

            def turn_z(t, u):
                if live(t):
                    pe.wait_ge(d_zn, t + 1)
                    after(pe, d_zt, t - 1)
                    pe.transpose(PS[:, 6 + u, 0:128], zn[u], ident[:, :]).then_inc(d_tz, 1)

            pe.wait_ge(c_ot, T)
            pipelined(pe, turn_z, 0, 1)
            Z = ZT.rearrange("p (b s) -> p b s", s=SEQ)

            def up_d(j):
                e, (f, n) = j // 3, F1C[j % 3]
                after(pe, d_u, j - 1)
                z = Z[:, :, e * CT:(e + 1) * CT]
                for i, w in enumerate((w1e_sb, w3e_sb)):
                    m = pe.matmul(PS[0:n, 2 * (j % 2) + i, :].rearrange("p (b s) -> p b s", s=CT), w[:, e, f:f + n], z, start=True, stop=True)
                m.then_inc(d_h, 1)

            def down_d(j):
                e, c = j // 3, j % 3
                n = F1C[c][1]
                pe.wait_ge(d_u, j + 1)
                if c == 0:
                    after(pe, d_r, e - 1)
                pe.matmul(PS[:, 4 + e % 2, :], w2e_sb[0:n, e, c, :], Ud[j % 3][0:n, :], start=(c == 0), stop=(c == 2)).then_inc(d_yu, 1)

            pe.wait_ge(wd_loaded, 80)
            pe.wait_ge(d_zt, T)
            up_d(0)
            for j in range(E1 * 3):
                if j + 1 < E1 * 3:
                    up_d(j + 1)
                down_d(j)
            pe.wait_ge(d_r, E1)
            for g in range(G):
                after(pe, d_x, g - 1)
                for k in range(GT):
                    t = g * GT + k
                    m = pe.transpose(PS[:, 6 + g % 2, 128 * k:128 * k + 128], RT[:, 128 * t:128 * t + 128], ident[:, :])
                m.then_inc(d_tr, 1)


def kernel(**inputs):
    import numpy as np
    import concourse.bacc as bacc
    from concourse.bass_utils import run_bass_kernel_spmd

    a = {k: np.asarray(v) for k, v in inputs.items()}
    wk, wv = np.split(a["L1_xattn_Wkv"], 2, axis=1)
    laid = [
        ("x", a["x"]), ("ctx_in", a["ctx_1024"]), ("mask", a["mask_BxSxS2_ff0"]), ("g_xattn", a["g_xattn"]), ("g_ffn", a["g_ffn"]),
        ("wqT0", a["L0_xattn_Wq"].T), ("bq0", a["L0_xattn_bq"]), ("wkT0", a["L0_xattn_Wk"].T), ("bk0", a["L0_xattn_bk"]),
        ("wvT0", a["L0_xattn_Wv"].T), ("bv0", a["L0_xattn_bv"]), ("woT0", a["L0_xattn_Wo"].T), ("bo0", a["L0_xattn_bo"]),
        ("P0", np.repeat(a["L0_xattn_P"], HD0, axis=0)), ("routerT", a["L0_ffn_router_w"].T),
        ("w1T0", a["L0_ffn_w1"].transpose(2, 0, 1)),
        ("w2T0", a["L0_ffn_w2"].reshape(E0, D, FC0, 128).transpose(3, 0, 2, 1)),
        ("escale", a["L0_ffn_expert_scale"]),
        ("ln_g", a["L1_xattn_ln_g"]), ("ln_b", a["L1_xattn_ln_b"]), ("cln_g", a["L1_xattn_cln_g"]), ("cln_b", a["L1_xattn_cln_b"]),
        ("wq1", a["L1_xattn_Wq"]), ("wkv1", np.concatenate([wk, wk, wv, wv], axis=1)), ("wout1", a["L1_xattn_Wout"]),
        ("w1m", a["L1_xattn_W1"]), ("w2m", a["L1_xattn_W2"]),
        ("w1e", a["L1_ffn_w1"].transpose(1, 0, 2)), ("w3e", a["L1_ffn_w3"].transpose(1, 0, 2)), ("w2e", a["L1_ffn_w2"]),
    ]
    consts = np.zeros((129, 129), np.float32)
    consts[0, 0:E0] = np.arange(E0) * REG
    consts[0, E0:E0 + T] = np.arange(T) * 128
    consts[0, E0 + T:E0 + T + NS] = np.arange(NS)
    consts[1:, 0:128] = np.triu(np.ones((128, 128)), 1)
    consts[1:, 128] = np.arange(128)
    laid.append(("shape_consts", consts))
    nc = bacc.Bacc("TRN2", target_bir_lowering=False, num_devices=1)
    arrays, args = {}, []
    for name, v in laid:
        v = np.ascontiguousarray(v)
        arrays[name] = v
        args.append(nc.dram_tensor(name, v.shape, mybir.dt.from_np(v.dtype), kind="ExternalInput").ap())
    args.append(nc.dram_tensor("out", a["x"].shape, F32, kind="ExternalOutput").ap())
    for name, rows in (("y_rows", ROWS), ("o_rows", NS * 128)):
        args.append(nc.dram_tensor(name, [rows, D], F32).ap())
    build(nc, *args)
    r = run_bass_kernel_spmd(nc, [arrays], core_ids=[0])
    return r.results[0]["out"]
```

```python
from contextlib import ExitStack

import concourse.bass as bass
from concourse import mybir

F32 = mybir.dt.float32
ALU = mybir.AluOpType
ACT = mybir.ActivationFunctionType
AX = mybir.AxisListType

D = 128
SEQ = 64
NSEQ = 64
TOK = 128
T = NSEQ * SEQ // TOK
H = 16
HP = H // 2
HD0 = D // H
HD1 = 64
E0 = 8
F0 = 512
FC0 = F0 // 128
REG = NSEQ * SEQ + 128
NS = (2 * NSEQ * SEQ + E0 * 127) // 128 + 1
SPARE = NS - 2 * NSEQ * SEQ // 128
ROWS = E0 * REG + SPARE * 128
GT = 4
G = T // GT
E1 = 8
F1 = 352
F1C = [(0, 128), (128, 128), (256, 96)]
CT = SEQ // E1
MLP = 512
MC = MLP // 128
EPS = 1e-5
assert NS % 2 == 0
KA = 7
OUT1 = 3
LINKS = 7
W_LINKS = 19
VW = 2 * (HD0 + 1)


def known(n):
    return isinstance(n, int)


def after(eng, sem, n):
    if not known(n) or n > 0:
        eng.wait_ge(sem, n)


def live(t, n=T):
    return not known(t) or 0 <= t < n


def pipelined(eng, step, lead, trail, n=T, lo=4):
    hi = n - lead - (n - lead) % 2
    for s in range(-lead, lo):
        step(s, s % 2)
    with eng.Fori(0, (hi - lo) // 2) as i:
        for u in range(2):
            step(i * 2 + (lo + u), u)
    for s in range(hi, n + trail):
        step(s, s % 2)


def build(nc, x, ctx_in, mask, g_xattn, g_ffn, wqT0, bq0, wkT0, bk0, wvT0, bv0, woT0, bo0, P0,
          routerT, w1T0, w2T0, escale, ln_g, ln_b, cln_g, cln_b, wq1, wkv1, wout1, w1m, w2m,
          w1e, w3e, w2e, shape_consts, out, y_rows, o_rows):
    with ExitStack() as ctx:
        def sb(name, *shape, dtype=F32):
            return ctx.enter_context(nc.sbuf_tensor(name, [128, *shape], dtype))

        def sem(name):
            return ctx.enter_context(nc.semaphore(name))

        X = sb("X", T, D)
        MK = sb("MK", T, SEQ)
        ident = sb("ident", 128)
        minus_half = sb("minus_half", GT)
        eps = sb("eps", GT)
        gates = sb("gates", 4)
        rawg = sb("rawg", 4)
        spare = sb("spare", 5)

        wq0_sb = sb("wq0_sb", D)
        wk0_sb = sb("wk0_sb", D)
        wv0_sb = sb("wv0_sb", D)
        wo0_sb = sb("wo0_sb", D)
        bias0 = sb("bias0", 3)
        bk_scaled = sb("bk_scaled", 1)
        Pc = sb("Pc", H)
        gbo = sb("gbo", D)
        router_sb = sb("router_sb", E0)
        escale_sb = sb("escale_sb", E0)
        tri = sb("tri", E0, E0)
        lnv = sb("lnv", 4)
        wkv_sb = sb("wkv_sb", 256)
        wq1_sb = sb("wq1_sb", H * HD1)
        wout_sb = sb("wout_sb", HP, D)
        w1m_sb = sb("w1m_sb", 2 * MLP)
        w2m_sb = sb("w2m_sb", MC, D)

        w1_sb = sb("w1_sb", E0, F0)
        w2_sb = sb("w2_sb", E0, FC0, D)
        w1e_sb = sb("w1e_sb", E1, F1)
        w3e_sb = sb("w3e_sb", E1, F1)
        w2e_sb = sb("w2e_sb", E1, len(F1C), D)
        consts = sb("consts", E0 + T + NS)
        wide = sb("wide", 129)
        PR = sb("PR", T, E0)
        RK = sb("RK", T, E0)
        POS = sb("POS", T, 2)
        MR = sb("MR", T, 2)
        CF = sb("CF", 2, T)
        rows_used = sb("rows_used", E0)
        pool_spare = sb("pool_spare", 1)
        zeros = sb("zeros", D)
        BF = mybir.dt.bfloat16
        before_bf = sb("before_bf", 128, dtype=BF)
        ones_bf = sb("ones_bf", 128, dtype=BF)
        ohb = sb("ohb", 2, E0, dtype=BF)
        ixs = [sb(f"ixs{u}", 2, dtype=mybir.dt.uint32) for u in range(2)]
        ixp = sb("ixp", E0, dtype=mybir.dt.uint32)
        emap = sb("emap", 2 * (NS + 2), dtype=mybir.dt.int32)
        rmap = sb("rmap", NS, dtype=mybir.dt.int32)
        cxb = [sb(f"cxb{u}", D) for u in range(2)]

        SIZES = {"ac": 13 * 1024 + 512, "bd": 7 * 1024 + 256}
        arenas = {k: sb(f"arena_{k}", n) for k, n in SIZES.items()}
        at = {}

        def part(which, *shape):
            n = 1
            for d in shape:
                n *= d
            lo = at.get(which, 0)
            at[which] = lo + n
            assert at[which] <= SIZES[which], (which, at)
            a = arenas[which][:, lo:lo + n]
            if len(shape) == 1:
                return a
            names = "abcd"[:len(shape)]
            return a.rearrange(f"p ({' '.join(names)}) -> p {' '.join(names)}",
                               **dict(zip(names[1:], shape[1:])))

        xn = [part("ac", D) for _ in range(2)]
        xcT = [part("ac", 4, 128) for _ in range(2)]
        qT = [part("ac", TOK) for _ in range(2)]
        kT = [part("ac", TOK) for _ in range(2)]
        KE = [part("ac", H, TOK) for _ in range(2)]
        VB = [part("ac", 2, HP, VW) for _ in range(2)]
        Ea = [part("ac", H, SEQ) for _ in range(2)]
        ETa = [part("ac", HP, TOK) for _ in range(2)]
        On = [part("ac", H, HD0) for _ in range(2)]
        OTa = [part("ac", TOK) for _ in range(2)]
        stat = [part("ac", 16) for _ in range(2)]
        mx = [part("ac", H) for _ in range(2)]
        rs = [part("ac", H) for _ in range(2)]
        ystat = [part("bd", 16) for _ in range(2)]
        yn = [part("bd", D) for _ in range(2)]
        yt = [part("bd", TOK) for _ in range(2)]
        yst = [part("bd", D) for _ in range(2)]
        lmx = part("bd", 2)
        lsum = part("bd", 2)
        lg = part("bd", 2, E0)
        ex = part("bd", 2, E0)
        dif = part("bd", 2, E0, E0)
        tie = part("bd", 2, E0, E0)
        slot = part("bd", 2, E0)
        picked = part("bd", 2, 2, E0)
        cnt = part("bd", E0)
        cmpj = part("bd", E0, T)
        ntl = part("bd", E0)
        before = part("bd", E0, E0)
        ends = part("bd", E0)
        hop = part("bd", E0)
        past = part("bd", NS, E0)
        mapf = part("bd", 2, NS)
        at["bd"] = 0
        ST = [part("bd", D) for _ in range(2)]
        yTs = [part("bd", TOK) for _ in range(2)]
        Th = [part("bd", F0) for _ in range(2)]
        U = [part("bd", F0) for _ in range(2)]
        UT = [part("bd", FC0, TOK) for _ in range(2)]
        OT = [part("bd", D) for _ in range(2)]
        shift = part("bd", E0)
        pick = part("bd", T, E0)
        p12 = part("bd", 2, T)
        cw = part("bd", 3, T)
        at["ac"] = 0
        xn2 = [part("ac", 2, D) for _ in range(2)]
        xcT2 = [part("ac", 4, 128) for _ in range(2)]
        QT = [part("ac", HP, TOK) for _ in range(2)]
        KB = [part("ac", 2, 2, SEQ) for _ in range(2)]
        VC = [part("ac", 2, 2, HD1) for _ in range(2)]
        Ec = [part("ac", H, SEQ) for _ in range(2)]
        ETc = [part("ac", HP, TOK) for _ in range(2)]
        OTc = [part("ac", HP, TOK) for _ in range(2)]
        tg = [part("ac", MC, TOK) for _ in range(2)]
        Uc = [part("ac", MC, TOK) for _ in range(2)]
        cst = [part("ac", 40) for _ in range(2)]
        cmx = [part("ac", H) for _ in range(2)]
        csum = [part("ac", H) for _ in range(2)]
        cinv = [part("ac", H) for _ in range(2)]
        at["bd"] = 0
        zn = [part("bd", D) for _ in range(2)]
        dst_ = [part("bd", 16) for _ in range(2)]
        ZT = part("bd", T * TOK)
        zt_end = at["bd"]
        Gt = [part("bd", 2, D) for _ in range(2)]
        at["bd"] = zt_end
        Td = [part("bd", 512) for _ in range(2)]
        Ud = [part("bd", 512) for _ in range(3)]
        at["ac"] = 0
        RT = part("ac", T * TOK)
        PS = ctx.enter_context(nc.psum_tensor("PS", [128, 8, 512], F32))

        first_loaded = sem("first_loaded")
        small_loaded = sem("small_loaded")
        x_loaded = [sem(f"x_loaded{i}") for i in range(4)]
        w0_loaded = sem("w0_loaded")
        ctx_loaded = [sem(f"ctx_loaded{u}") for u in range(2)]
        w1l_loaded = sem("w1l_loaded")
        wd_loaded = sem("wd_loaded")
        ident_zero = sem("ident_zero")
        ident_ready = sem("ident_ready")
        half_ready = sem("half_ready")
        gates_ready = sem("gates_ready")
        const_ready = sem("const_ready")
        vb_zero = sem("vb_zero")
        a_st = sem("a_st"); a_mv = sem("a_mv"); a_eps = sem("a_eps"); a_rstd = sem("a_rstd"); a_xn = sem("a_xn"); a_xb = sem("a_xb")
        a_tin = sem("a_tin"); a_xc = sem("a_xc"); a_qk = sem("a_qk"); a_qkv = sem("a_qkv"); a_k = sem("a_k"); a_q = sem("a_q"); a_v = sem("a_v")
        a_ked = sem("a_ked"); a_kep = sem("a_kep"); a_kea = sem("a_kea"); a_s = sem("a_s"); a_mx = sem("a_mx"); a_sub = sem("a_sub"); a_exp = sem("a_exp")
        a_te = sem("a_te"); a_et = sem("a_et"); a_av = sem("a_av"); a_rc = sem("a_rc"); a_on = sem("a_on"); a_to = sem("a_to")
        a_ot = sem("a_ot"); a_pr = sem("a_pr"); a_res = sem("a_res")
        y_st = sem("y_st"); y_mv = sem("y_mv"); y_eps = sem("y_eps"); y_rstd = sem("y_rstd"); y_saved = sem("y_saved")
        y_n = sem("y_n"); y_tin = sem("y_tin"); y_t = sem("y_t"); r_logits = sem("r_logits"); r_rank = sem("r_rank"); r_max = sem("r_max"); r_slot = sem("r_slot")
        r_shift = sem("r_shift"); r_exp = sem("r_exp"); r_two = sem("r_two"); r_count = sem("r_count"); r_counted = sem("r_counted"); r_pos = sem("r_pos")
        yst_ready = sem("yst_ready"); ix_ready = sem("ix_ready"); pad_ix = sem("pad_ix")
        scattered = [sem(f"scattered{u}") for u in range(2)]
        padded = [sem(f"padded{e}") for e in range(E0)]; trash_zero = sem("trash_zero"); zeros_ready = sem("zeros_ready")
        route_const = sem("route_const")
        m_link = sem("m_link"); map_ready = sem("map_ready"); w_link = sem("w_link"); w_dif = sem("w_dif"); w_exp = sem("w_exp")
        st_loaded = [sem(f"st_loaded{u}") for u in range(2)]
        o_stored = [sem(f"o_stored{u}") for u in range(2)]
        b_ty = sem("b_ty"); b_yT = sem("b_yT"); b_h = sem("b_h"); b_t = sem("b_t"); b_u = sem("b_u"); b_tu = sem("b_tu"); b_uT = sem("b_uT")
        b_y = sem("b_y"); b_o = sem("b_o")
        g_ix = sem("g_ix"); g_sum = sem("g_sum"); g_add = sem("g_add")
        gathered = [sem(f"gathered{u}") for u in range(2)]
        c_ch = sem("c_ch"); c_ch2 = sem("c_ch2"); c_add = sem("c_add"); c_mv = sem("c_mv"); c_eps = sem("c_eps"); c_rstd = sem("c_rstd"); c_xn = sem("c_xn"); c_tin = sem("c_tin"); c_xc = sem("c_xc")
        c_kv = sem("c_kv"); c_kve = sem("c_kve"); c_q = sem("c_q"); c_qe = sem("c_qe"); c_s = sem("c_s"); c_mx = sem("c_mx")
        c_sub = sem("c_sub"); c_exp = sem("c_exp"); c_sum = sem("c_sum"); c_inv = sem("c_inv"); c_nrm = sem("c_nrm"); c_te = sem("c_te"); c_et = sem("c_et")
        c_o = sem("c_o"); c_ot = sem("c_ot"); c_h = sem("c_h"); c_t = sem("c_t"); c_g = sem("c_g"); c_u = sem("c_u"); c_out = sem("c_out"); c_res = sem("c_res")
        kb_zero = sem("kb_zero")
        d_st = sem("d_st"); d_mv = sem("d_mv"); d_eps = sem("d_eps"); d_rstd = sem("d_rstd"); d_zn = sem("d_zn"); d_tz = sem("d_tz"); d_zt = sem("d_zt")
        d_h = sem("d_h"); d_t = sem("d_t"); d_g = sem("d_g"); d_u = sem("d_u"); d_yu = sem("d_yu"); d_r = sem("d_r"); d_tr = sem("d_tr"); d_x = sem("d_x")
        stored = sem("stored")

        block = ctx.enter_context(nc.Block())

        x_t = x.rearrange("(t b) s d -> (b s) t d", b=2)
        c_t_in = ctx_in.rearrange("(t b) s d -> (b s) t d", b=2)
        out_t = out.rearrange("(t b) s d -> (b s) t d", b=2)
        XC = ((0, 2), (2, 8), (8, 16), (16, T))
        N_FIRST, N_SMALL = 6, 15
        assert T == 32 and E0 == E1 == 8

        @block.sync
        def _(sp):
            def load_x(i):
                sl = slice(*XC[i])
                sp.dma_start(X[:, sl, :], x_t[:, sl, :]).then_inc(x_loaded[i], 16)

            def load_ctx(t, u, sem_free, free):
                after(sp, sem_free, free)
                sp.dma_start(cxb[u][:, :], c_t_in[:, bass.ts(t, 1), :].squeeze(1)).then_inc(ctx_loaded[u], 16)

            load_x(0)
            firsts = ((wk0_sb[:, :], wkT0), (wq0_sb[:, :], wqT0), (bias0[:, 0:1], bq0.unsqueeze(1)),
                      (bias0[:, 1:2], bk0.unsqueeze(1)), (Pc[:, :], P0), (wv0_sb[:, :], wvT0))
            assert len(firsts) == N_FIRST
            for dst, src in firsts:
                sp.dma_start(dst, src).then_inc(first_loaded, 16)
            load_ctx(0, 0, a_tin, 0)
            load_x(1)
            load_ctx(1, 1, a_tin, 0)
            smalls = ((bias0[:, 2:3], bv0.unsqueeze(1)), (wo0_sb[:, :], woT0),
                      (gbo[:, :], bo0.unsqueeze(0).broadcast_to([128, D])),
                      (rawg[:, 0:2], g_xattn.unsqueeze(0).broadcast_to([128, 2])),
                      (rawg[:, 2:4], g_ffn.unsqueeze(0).broadcast_to([128, 2])),
                      (escale_sb[:, :], escale.unsqueeze(0).broadcast_to([128, E0])),
                      (router_sb[:, :], routerT),
                      (lnv[:, 0:1], ln_g.unsqueeze(1)), (lnv[:, 1:2], ln_b.unsqueeze(1)),
                      (lnv[:, 2:3], cln_g.unsqueeze(1)), (lnv[:, 3:4], cln_b.unsqueeze(1)),
                      (wkv_sb[:, :], wkv1), (w2m_sb[:, :, :], w2m.rearrange("(c p) d -> p c d", p=128)),
                      (consts[:, :], shape_consts[0:1, 0:E0 + T + NS].broadcast_to([128, E0 + T + NS])),
                      (wide[:, :], shape_consts[1:129, :]))
            assert len(smalls) == N_SMALL
            for dst, src in smalls:
                sp.dma_start(dst, src).then_inc(small_loaded, 16)
            load_x(2)
            load_x(3)

            def load_expert(e):
                sp.dma_start(w1_sb[:, bass.ds(e, 1), :], w1T0[:, bass.ds(e, 1), :]).then_inc(w0_loaded, 16)
                sp.dma_start(w2_sb[:, bass.ds(e, 1), :, :], w2T0[:, bass.ds(e, 1), :, :]).then_inc(w0_loaded, 16)

            def load_eighth(k):
                sp.dma_start(MK[:, bass.ts(k, T // 8), :], mask.rearrange("(t b) s m -> (b s) t m", b=2)[:, bass.ts(k, T // 8), :]).then_inc(w1l_loaded, 16)
                sp.dma_start(wq1_sb[:, bass.ts(k, 128)], wq1[:, bass.ts(k, 128)]).then_inc(w1l_loaded, 16)
                sp.dma_start(wout_sb[:, bass.ds(k, 1), :], wout1.rearrange("(t p) d -> p t d", p=128)[:, bass.ds(k, 1), :]).then_inc(w1l_loaded, 16)
                sp.dma_start(w1m_sb[:, bass.ts(k, 128)], w1m[:, bass.ts(k, 128)]).then_inc(w1l_loaded, 16)

            def load_expert1(e):
                sp.dma_start(w1e_sb[:, bass.ds(e, 1), :], w1e[:, bass.ds(e, 1), :]).then_inc(wd_loaded, 16)
                sp.dma_start(w3e_sb[:, bass.ds(e, 1), :], w3e[:, bass.ds(e, 1), :]).then_inc(wd_loaded, 16)
                for c, (f, n) in enumerate(F1C):
                    sp.dma_start(w2e_sb[0:n, bass.ds(e, 1), c, :], w2e[bass.ds(e, 1), f:f + n, :].rearrange("e f d -> f e d")).then_inc(wd_loaded, 16)

            load_expert(0)
            with sp.Fori(1, 8) as i:
                for u in range(2):
                    load_ctx(i * 2 + u, u, a_tin, i * 2 + (u - 1))
                load_expert(i)
            with sp.Fori(0, 8) as i:
                for u in range(2):
                    load_ctx(i * 2 + (16 + u), u, a_tin, i * 2 + (15 + u))
                load_eighth(i)
            def load_slot(i, u):
                if live(i, NS):
                    after(sp, b_ty, i - 1)
                    if known(i) and i < E0:
                        sp.wait_ge(padded[i], 16)
                    row = sp.value_load(rmap[0:1, bass.ds(i, 1)], min_val=0, max_val=ROWS - 128)
                    sp.dma_start(ST[u], y_rows[bass.ds(row, 128), :]).then_inc(st_loaded[u], 16)

            def store_slot(i, u):
                if live(i, NS):
                    sp.wait_ge(b_o, i + 1)
                    sp.dma_start(o_rows[bass.ts(i, 128), :], OT[u]).then_inc(o_stored[u], 16)

            def step_b(s, u):
                load_slot(s + 3, 1 - u)
                store_slot(s - 2, u)

            sp.wait_ge(map_ready, 3)
            sp.wait_ge(trash_zero, 16)
            for u in range(2):
                sp.wait_ge(scattered[u], 16 * T)
            pipelined(sp, step_b, 3, 2, n=NS, lo=6)
            load_ctx(0, 0, a_tin, T)
            load_ctx(1, 1, a_tin, T)
            load_expert1(0)
            with sp.Fori(1, 8) as i:
                for u in range(2):
                    load_ctx(i * 2 + u, u, c_mv, i * 4 + (2 * u - 2))
                load_expert1(i)
            with sp.Fori(8, T // 2) as i:
                for u in range(2):
                    load_ctx(i * 2 + u, u, c_mv, i * 4 + (2 * u - 2))
            for g in range(G):
                sp.wait_ge(d_x, g + 1)
                sl = slice(g * GT, (g + 1) * GT)
                sp.dma_start(out_t[:, sl, :], X[:, sl, :]).then_inc(stored, 16)
            sp.wait_ge(stored, 16 * G)

        @block.gpsimd
        def _(pool):
            pool.memset(ident[:, :], 0.0).then_inc(ident_zero, 1)
            pool.memset(minus_half[:, :], -0.5).then_inc(half_ready, 1)
            pool.memset(eps[:, :], EPS).then_inc(half_ready, 1)
            pool.memset(tri[:, :, :], 0.0).then_inc(ident_zero, 1)
            pool.wait_ge(ident_zero, 2)
            pool.affine_select(out=ident[:, :], in_=ident[:, :], compare_op=ALU.not_equal, fill=1.0, base=0,
                               pattern=[[-1, 128]], channel_multiplier=1).then_inc(ident_ready, 1)
            pool.affine_select(out=tri[:, :, :], in_=tri[:, :, :], compare_op=ALU.is_ge, fill=1.0, base=0,
                               pattern=[[-1, E0], [1, E0]], channel_multiplier=0).then_inc(ident_ready, 1)
            pool.memset(zeros[:, :], 0.0).then_inc(zeros_ready, 1)
            pool.wait_ge(zeros_ready, 1)
            pool.dma_start(y_rows[E0 * REG:ROWS, :].rearrange("(k p) d -> p k d", p=128),
                           zeros[:, :].unsqueeze(1).to_broadcast([128, SPARE, D])).then_inc(trash_zero, 16)
            pool.wait_ge(half_ready, 2)

            def rstd(t, u):
                if live(t):
                    pool.wait_ge(a_mv, t + 1)
                    pool.tensor_tensor(stat[u][:, 8:9], stat[u][:, 7:8], eps[:, 0:1], ALU.add).then_inc(a_eps, 1)
                    pool.wait_ge(a_eps, t + 1)
                    pool.tensor_tensor(stat[u][:, 9:10], stat[u][:, 8:9], minus_half[:, 0:1], ALU.pow).then_inc(a_rstd, 1)

            def scale_k(t, u):
                if live(t):
                    pool.wait_ge(a_k, t + 1)
                    pool.tensor_tensor(KE[u][:, HP:H, :], kT[u].unsqueeze(1).to_broadcast([128, HP, TOK]),
                                       Pc[:, HP:H].unsqueeze(2).to_broadcast([128, HP, TOK]), ALU.mult).then_inc(a_kep, 1)

            def add_bias(t):
                if live(t):
                    if known(t) and t == 0:
                        pool.wait_ge(const_ready, 2)
                    pool.wait_ge(a_xn, t + 1)
                    pool.tensor_tensor(X[:, bass.ts(t, 1), :].squeeze(1), X[:, bass.ts(t, 1), :].squeeze(1), gbo[:, :], ALU.add).then_inc(a_xb, 1)

            def rstd_y(t, u):
                if live(t):
                    pool.wait_ge(y_mv, t + 1)
                    pool.tensor_tensor(ystat[u][:, 8:9], ystat[u][:, 7:8], eps[:, 0:1], ALU.add).then_inc(y_eps, 1)
                    pool.wait_ge(y_eps, t + 1)
                    pool.tensor_tensor(ystat[u][:, 7:8], ystat[u][:, 8:9], minus_half[:, 0:1], ALU.pow).then_inc(y_rstd, 1)
                    pool.wait_ge(y_rstd, t + 1)
                    pool.tensor_copy(MR[:, bass.ts(t, 1), :].squeeze(1), ystat[u][:, 6:8]).then_inc(y_saved, 1)

            def scatter(t, u):
                if live(t):
                    pool.wait_ge(r_pos, t + 1)
                    after(pool, scattered[u], t * 16 - 16 * u)
                    pool.tensor_copy(ixs[u][:, :], POS[:, bass.ts(t, 1), :].squeeze(1)).then_inc(ix_ready, 1)
                    pool.wait_ge(ix_ready, t + 1)
                    pool.wait_ge(yst_ready, t + 1)
                    pool.tensor_tensor(pool_spare[:, :], eps[:, 0:1], eps[:, 0:1], ALU.add)
                    for r in range(2):
                        pool.indirect_dma_start(y_rows, bass.IndirectOffsetOnAxis(ap=ixs[u][:, r:r + 1], axis=0), yst[u], None).then_inc(scattered[u], 16)

            def step(s, u):
                scale_k(s + 1, 1 - u)
                add_bias(s)
                scatter(s - 8, u)
                rstd(s + 3, 1 - u)
                rstd_y(s - 2, u)

            pipelined(pool, step, 3, 9, lo=10)

            pool.wait_ge(pad_ix, 1)
            for e in range(E0):
                pool.indirect_dma_start(y_rows, bass.IndirectOffsetOnAxis(ap=ixp[:, e:e + 1], axis=0), zeros[:, :], None).then_inc(padded[e], 16)


            def rstd_c(t, u, k):
                if live(t):
                    pool.wait_ge(c_mv, t * 2 + (k + 1))
                    a = 12 if k == 0 else 28
                    n = 2 if k == 0 else 1
                    pool.tensor_tensor(cst[u][:, a + 4:a + 4 + n], cst[u][:, a + 1:a + 2 * n:2], eps[:, 0:n], ALU.add).then_inc(c_eps, 1)
                    pool.wait_ge(c_eps, t * 2 + (k + 1))
                    pool.tensor_tensor(cst[u][:, a + 6:a + 6 + n], cst[u][:, a + 4:a + 4 + n], minus_half[:, 0:n], ALU.pow).then_inc(c_rstd, 1)

            def rstd_z(t, u):
                if live(t):
                    pool.wait_ge(d_mv, t + 1)
                    pool.tensor_tensor(dst_[u][:, 8:9], dst_[u][:, 7:8], eps[:, 0:1], ALU.add).then_inc(d_eps, 1)
                    pool.wait_ge(d_eps, t + 1)
                    pool.tensor_tensor(dst_[u][:, 9:10], dst_[u][:, 8:9], minus_half[:, 0:1], ALU.pow).then_inc(d_rstd, 1)

            def divide(t, u):
                if live(t):
                    pool.wait_ge(c_inv, t + 1)
                    pool.tensor_tensor(Ec[u], Ec[u], cinv[u].unsqueeze(2).to_broadcast([128, H, SEQ]), ALU.mult).then_inc(c_nrm, 1)

            def gather(t, u):
                if live(t):
                    after(pool, gathered[u], t * 16 - 16 * u)
                    pool.tensor_copy(ixs[u][:, :], POS[:, bass.ts(t, 1), :].squeeze(1)).then_inc(g_ix, 1)
                    pool.wait_ge(g_ix, t + 1)
                    after(pool, g_sum, t - 1)
                    pool.tensor_tensor(pool_spare[:, :], eps[:, 0:1], eps[:, 0:1], ALU.add)
                    for r in range(2):
                        pool.indirect_dma_start(Gt[u][:, r, :], None, o_rows, bass.IndirectOffsetOnAxis(ap=ixs[u][:, r:r + 1], axis=0)).then_inc(gathered[u], 16)

            def step_c(s, u):
                divide(s, u)
                rstd_c(s + 2, u, 0)
                rstd_c(s + 2, u, 1)
                rstd_z(s - 2, u)
                gather(s + 4, u)

            for u in range(2):
                pool.wait_ge(scattered[u], 16 * T)
                pool.wait_ge(w_link, W_LINKS)
                pool.wait_ge(o_stored[u], 8 * NS)
            pipelined(pool, step_c, 4, 2, lo=6)

        @block.scalar
        def _(act):
            act.wait_ge(const_ready, 1)

            def out_t_copy(t, u):
                if live(t):
                    act.wait_ge(a_to, t + 1)
                    act.activation(OTa[u], PS[:, 7, 0:128], ACT.Identity, bias=bias0[:, 2:3]).then_inc(a_ot, 1)

            def in_copy(t, u):
                if live(t):
                    act.wait_ge(a_tin, t + 1)
                    after(act, a_qkv, t - 1)
                    act.copy(xcT[u][:, 0:2, :], PS[:, 0, 0:256].rearrange("p (a b) -> p a b", a=2)).then_inc(a_xc, 1)
                    act.copy(xcT[u][:, 2:4, :].rearrange("p b (k m) -> p b k m", k=2),
                             PS[:, 0, 128:256].rearrange("p (b m) -> p b m", b=2).unsqueeze(2).to_broadcast([128, 2, 2, SEQ])).then_inc(a_xc, 1)

            def e_t_copy(t, u):
                if live(t):
                    for h in range(2):
                        act.wait_ge(a_te, t * 2 + (h + 1))
                        act.copy(ETa[u][:, 4 * h:4 * h + 4, :], PS[:, 4 + h, :].rearrange("p (b c) -> p b c", b=4)).then_inc(a_et, 1)

            def qk_copy(t, u):
                if live(t):
                    act.wait_ge(a_qk, t + 1)
                    after(act, a_ked, t - 1)
                    after(act, a_kep, t - 1)
                    after(act, a_kea, t - 1)
                    act.activation(kT[u], PS[:, 1, 128:256], ACT.Identity, bias=bk_scaled[:, 0:1], scale=HD0 ** -0.5).then_inc(a_k, 1)
                    act.activation(qT[u], PS[:, 1, 0:128], ACT.Identity, bias=bias0[:, 0:1]).then_inc(a_q, 1)

            def scale_k(t, u):
                if live(t):
                    act.wait_ge(a_k, t + 1)
                    for g in range(HP - KA, HP):
                        m = act.activation(KE[u][:, g, :], kT[u], ACT.Identity, scale=Pc[:, g:g + 1])
                    m.then_inc(a_kea, 1)

            def v_copy(t, u):
                if live(t):
                    act.wait_ge(a_qkv, t + 1)
                    after(act, a_av, t - 1)
                    v = PS[:, 1, 256:512].rearrange("p (b t k d) -> p b t k d", b=2, t=HP, k=2)
                    vb = VB[u].rearrange("p b t (k d) -> p b t k d", k=2)
                    for k in range(2):
                        act.copy(vb[64 * k:64 * k + 64, :, :, k, 0:HD0], v[64 * k:64 * k + 64, :, :, k, :]).then_inc(a_v, 1)

            def exps(t, u):
                if live(t):
                    act.wait_ge(a_sub, t + 1)
                    act.activation(Ea[u], Ea[u], ACT.Exp).then_inc(a_exp, 1)

            def y_copy(t, u):
                if live(t):
                    act.wait_ge(y_tin, t + 1)
                    after(act, r_logits, t - 1)
                    act.copy(yt[u], PS[:, 0, 256:384]).then_inc(y_t, 1)

            def router_exp(t):
                if live(t):
                    act.wait_ge(r_shift, t + 2)
                    after(act, r_rank, t * LINKS - (2 * LINKS - 6))
                    act.activation(ex, lg, ACT.Exp).then_inc(r_exp, 2)

            def step(s, u):
                if known(s) and s == 0:
                    act.wait_ge(small_loaded, 16 * N_SMALL)
                    act.activation(gates[:, :], rawg[:, :], ACT.Tanh).then_inc(gates_ready, 1)
                if u == 0:
                    router_exp(s - 6)
                out_t_copy(s - 2, u)
                qk_copy(s + 1, 1 - u)
                e_t_copy(s - 1, 1 - u)
                scale_k(s + 1, 1 - u)
                in_copy(s + 2, u)
                y_copy(s - 3, 1 - u)
                v_copy(s + 1, 1 - u)
                exps(s, u)

            act.wait_ge(vb_zero, 6)
            pipelined(act, step, 2, 9, lo=10)

            def tanh_b(i, u):
                if live(i, NS):
                    act.wait_ge(b_h, i + 1)
                    after(act, b_u, i - 1)
                    act.activation(Th[u], PS[:, 1 + u, :], ACT.Tanh, scale=0.5).then_inc(b_t, 1)

            def u_t_copy(i, u):
                if live(i, NS):
                    act.wait_ge(b_tu, i + 1)
                    after(act, b_y, i - 1)
                    act.copy(UT[u], PS[:, 3 + u, :].rearrange("p (c t) -> p c t", c=FC0)).then_inc(b_uT, 1)

            def step_b(s, u):
                tanh_b(s, u)
                u_t_copy(s - 1, 1 - u)
                if known(s) and s == 1:
                    act.wait_ge(w_dif, 1)
                    act.activation(cw[:, 1, :], cw[:, 0, :], ACT.Exp).then_inc(w_exp, 1)

            act.wait_ge(map_ready, 3)
            pipelined(act, step_b, 0, 1, n=NS)

            def in_copy_c(t, u):
                if live(t):
                    act.wait_ge(c_tin, t + 1)
                    after(act, c_h, t - 1)
                    act.activation(xcT2[u][:, 0, :], PS[:, 0, 0:128], ACT.Identity, bias=lnv[:, 1:2], scale=lnv[:, 0:1]).then_inc(c_xc, 1)
                    act.activation(xcT2[u][:, 1, :], PS[:, 0, 128:256], ACT.Identity, bias=lnv[:, 3:4], scale=lnv[:, 2:3]).then_inc(c_xc, 1)
                    act.activation(xcT2[u][:, 2:4, :].rearrange("p b (k m) -> p b k m", k=2),
                                   PS[:, 0, 128:256].rearrange("p (b m) -> p b m", b=2).unsqueeze(2).to_broadcast([128, 2, 2, SEQ]),
                                   ACT.Identity, bias=lnv[:, 3:4], scale=lnv[:, 2:3]).then_inc(c_xc, 1)

            def kv_copy(t, u):
                if live(t):
                    act.wait_ge(c_kv, t + 1)
                    after(act, c_o, t - 1)
                    for k in range(2):
                        q = slice(64 * k, 64 * k + 64)
                        act.mul(KB[u][q, :, k, :], PS[q, 1, 0:128].rearrange("p (b m) -> p b m", b=2), HD1 ** -0.5).then_inc(c_kve, 1)
                        act.copy(VC[u][q, :, k, :], PS[q, 1, 128:384].rearrange("p (b k d) -> p b k d", b=2, k=2)[:, :, k, :]).then_inc(c_kve, 1)

            def z_copy(t, u):
                if live(t):
                    act.wait_ge(d_tz, t + 1)
                    act.copy(ZT[:, bass.ts(t, 128)], PS[:, 1, 384:512]).then_inc(d_zt, 1)

            def q_copy(t, u):
                if live(t):
                    for h in range(2):
                        act.wait_ge(c_q, t * 2 + (h + 1))
                        act.copy(QT[u][:, 4 * h:4 * h + 4, :], PS[:, 2 + h, :].rearrange("p (b c) -> p b c", b=4)).then_inc(c_qe, 1)

            def exps_c(t, u):
                if live(t):
                    act.wait_ge(c_sub, t + 1)
                    act.activation(Ec[u], Ec[u], ACT.Exp).then_inc(c_exp, 1)

            def e_t_copy_c(t, u):
                if live(t):
                    act.wait_ge(c_te, t + 1)
                    act.copy(ETc[u], PS[:, 6:8, :].rearrange("p a (b c) -> p (a b) c", b=4)).then_inc(c_et, 1)

            def tanh_c(t, u):
                if live(t):
                    act.wait_ge(c_h, t + 1)
                    act.activation(tg[u], PS[:, 3, :].rearrange("p (a b) -> p a b", a=MC), ACT.Tanh, scale=0.5).then_inc(c_t, 1)

            def o_t_copy(t, u):
                if live(t):
                    act.wait_ge(c_o, t + 1)
                    act.copy(OTc[u].rearrange("p t (b l) -> p b t l", b=2),
                             PS[:, 6:8, :].rearrange("p b (t l) -> p b t l", t=HP)).then_inc(c_ot, 1)

            def step_c(s, u):
                e_t_copy_c(s - 1, 1 - u)
                in_copy_c(s + 1, 1 - u)
                tanh_c(s, u)
                exps_c(s, u)
                o_t_copy(s - 1, 1 - u)
                kv_copy(s + 1, 1 - u)
                z_copy(s - 3, 1 - u)
                q_copy(s + 1, 1 - u)

            act.wait_ge(kb_zero, 4)
            pipelined(act, step_c, 1, 3, lo=6)

            for j in range(E1 * 3):
                n = F1C[j % 3][1]
                act.wait_ge(d_h, j + 1)
                after(act, d_u, j - 1)
                act.activation(Td[j % 2][0:n, :], PS[0:n, 2 * (j % 2), :], ACT.Tanh, scale=0.5).then_inc(d_t, 1)

        @block.vector
        def _(dve):
            for p in range(2):
                dve.memset(VB[p], 0.0).then_inc(vb_zero, 1)
            dve.wait_ge(vb_zero, 2)
            for p in range(2):
                dve.memset(VB[p][0:64, :, :, HD0:HD0 + 1], 1.0).then_inc(vb_zero, 1)
                dve.memset(VB[p][64:128, :, :, VW - 1:VW], 1.0).then_inc(vb_zero, 1)
            dve.wait_ge(first_loaded, 16 * N_FIRST)
            dve.tensor_scalar(bk_scaled[:, :], bias0[:, 1:2], HD0 ** -0.5, None, ALU.mult).then_inc(const_ready, 1)

            def late_constants():
                dve.wait_ge(small_loaded, 16 * N_SMALL)
                dve.wait_ge(gates_ready, 1)
                dve.tensor_scalar(gbo[:, :], gbo[:, :], gates[:, 0:1], None, ALU.mult).then_inc(const_ready, 1)
                dve.tensor_scalar(w2m_sb[:, :, :], w2m_sb[:, :, :], 0.5, None, ALU.mult).then_inc(const_ready, 1)
                dve.tensor_scalar(escale_sb[:, :], escale_sb[:, :], gates[:, 2:3], 0.5, ALU.mult, ALU.mult).then_inc(const_ready, 1)
                dve.tensor_scalar(gates[:, 3:4], gates[:, 3:4], 0.5, None, ALU.mult).then_inc(const_ready, 1)
                dve.tensor_copy(before_bf[:, :], wide[:, 0:128]).then_inc(route_const, 1)
                dve.memset(ones_bf[:, :], 1.0).then_inc(route_const, 1)
                dve.tensor_copy(rows_used[:, :], consts[:, 0:E0]).then_inc(route_const, 1)
                dve.memset(emap[:, :], 0).then_inc(route_const, 1)
                dve.wait_ge(const_ready, 5)
                dve.wait_ge(route_const, 4)
                dve.wait_ge(ident_ready, 2)

            def xtile(t):
                return X[:, bass.ts(t, 1), :].squeeze(1)

            def stats(t, ty, u):
                if live(t):
                    dve.bn_stats(stat[1 - u][:, 0:6], xtile(t)).then_inc(a_st, 1)
                if live(ty):
                    dve.wait_ge(a_res, ty + 1)
                    after(dve, y_saved, ty - 1)
                    dve.memset(spare[:, 1:2], 0.0)
                    dve.bn_stats(ystat[u][:, 0:6], xtile(ty)).then_inc(y_st, 1)
                if live(t):
                    dve.wait_ge(a_st, t + 1)
                    dve.memset(spare[:, 0:1], 0.0)
                    dve.bn_aggr(stat[1 - u][:, 6:8], stat[1 - u][:, 0:6]).then_inc(a_mv, 1)
                if live(ty):
                    dve.wait_ge(y_st, ty + 1)
                    dve.memset(spare[:, 2:3], 0.0)
                    dve.bn_aggr(ystat[u][:, 6:8], ystat[u][:, 0:6]).then_inc(y_mv, 1)

            def normalise_y(t, u):
                if live(t):
                    dve.wait_ge(y_rstd, t + 1)
                    after(dve, y_tin, t - 1)
                    dve.tensor_scalar(yn[u], xtile(t), ystat[u][:, 6:7], ystat[u][:, 7:8], ALU.subtract, ALU.mult).then_inc(y_n, 1)

            def rows_for_scatter(t, u):
                if live(t):
                    dve.wait_ge(y_saved, t + 1)
                    after(dve, scattered[u], t * 16 - 16 * u)
                    dve.tensor_scalar(yst[u], xtile(t), MR[:, bass.ts(t, 1), 0:1].squeeze(1), MR[:, bass.ts(t, 1), 1:2].squeeze(1),
                                      ALU.subtract, ALU.mult).then_inc(yst_ready, 1)

            v3 = [128, 2, E0]
            v4 = [128, 2, E0, E0]

            def pair(buf, t):
                return buf[:, bass.ds(t, 2), :]

            def ranked(t, k):
                dve.wait_ge(r_rank, t * LINKS + 2 * k)

            def route(t, k):
                if not live(t):
                    return
                L = PS[:, 6, 256:272].rearrange("p (k e) -> p k e", k=2)
                P = PS[:, 6, 272:288].rearrange("p (k e) -> p k e", k=2)
                if k == 1:
                    dve.wait_ge(r_logits, t + 2)
                    dve.reduce_max(lmx, L, AX.X).then_inc(r_max, 2)
                    dve.wait_ge(r_max, t + 2)
                    after(dve, r_exp, t)
                    dve.tensor_tensor(lg, L, lmx.unsqueeze(2).to_broadcast(v3), ALU.subtract).then_inc(r_shift, 2)
                if k == 2:
                    dve.wait_ge(r_exp, t + 2)
                    dve.reduce_sum(lsum, ex, AX.X).then_inc(r_rank, 2)
                if k == 3:
                    ranked(t, 1)
                    dve.reciprocal(lsum, lsum).then_inc(r_rank, 2)
                if k == 4:
                    ranked(t, 2)
                    dve.tensor_tensor(pair(PR, t), ex, lsum.unsqueeze(2).to_broadcast(v3), ALU.mult).then_inc(r_rank, 2)
                if k == 5:
                    ranked(t, 3)
                    dve.tensor_tensor(dif, pair(PR, t).unsqueeze(2).to_broadcast(v4), pair(PR, t).unsqueeze(3).to_broadcast(v4), ALU.subtract).then_inc(r_rank, 2)
                if k == 6:
                    ranked(t, 4)
                    dve.scalar_tensor_tensor(tie, dif, 0.0, tri[:, :, :].unsqueeze(1).to_broadcast(v4), ALU.is_equal, ALU.mult).then_inc(r_rank, 2)
                if k == 7:
                    ranked(t, 5)
                    dve.scalar_tensor_tensor(dif, dif, 0.0, tie, ALU.is_gt, ALU.add).then_inc(r_rank, 2)
                if k == 8:
                    ranked(t, 6)
                    dve.reduce_sum(pair(RK, t), dif, AX.X).then_inc(r_rank, 2)
                if k == 9:
                    ranked(t, 7)
                    after(dve, r_count, t)
                    dve.tensor_scalar(ohb[:, :, :], pair(RK, t), 2.0, None, ALU.is_lt).then_inc(r_two, 2)
                if k == 10:
                    dve.wait_ge(r_count, t + 2)
                    after(dve, r_counted, t)
                    dve.tensor_tensor(slot, P, rows_used[:, :].unsqueeze(1).to_broadcast(v3), ALU.add).then_inc(r_slot, 2)
                if k == 11:
                    dve.wait_ge(r_slot, t * 3 + 2)
                    dve.tensor_tensor(rows_used[:, :], rows_used[:, :], PS[:, 6, 288:296], ALU.add).then_inc(r_counted, 2)
                    for r in range(2):
                        dve.scalar_tensor_tensor(picked[:, :, r, :], pair(RK, t), float(r), slot, ALU.is_equal, ALU.mult).then_inc(r_slot, 2)
                if k == 12:
                    dve.wait_ge(r_slot, t * 3 + 6)
                    dve.reduce_sum(pair(POS, t), picked, AX.X).then_inc(r_pos, 2)

            def normalise(t, u):
                if live(t):
                    dve.wait_ge(a_rstd, t + 1)
                    after(dve, a_tin, t - 1)
                    dve.tensor_scalar(xn[u], xtile(t), stat[u][:, 6:7], stat[u][:, 9:10], ALU.subtract, ALU.mult).then_inc(a_xn, 1)

            def maximum(t, u):
                if live(t):
                    S = PS[:, 2:4, :].rearrange("p a (g m) -> p (a g) m", g=8)
                    dve.wait_ge(a_s, t + 1)
                    dve.reduce_max(mx[u], S, AX.X).then_inc(a_mx, 1)

            def shift_scores(t, u):
                if live(t):
                    S = PS[:, 2:4, :].rearrange("p a (g m) -> p (a g) m", g=8)
                    dve.wait_ge(a_mx, t + 1)
                    after(dve, a_te, t * 2 - 2)
                    dve.tensor_tensor(Ea[u], S, mx[u].unsqueeze(2).to_broadcast([128, H, SEQ]), ALU.subtract).then_inc(a_sub, 1)

            def scale_k(t, u):
                if live(t):
                    dve.wait_ge(a_k, t + 1)
                    for g in range(HP - KA):
                        m = dve.tensor_scalar(KE[u][:, g, :], kT[u], Pc[:, g:g + 1], None, ALU.mult)
                    m.then_inc(a_ked, 1)

            def normalise_out(t, u):
                if live(t):
                    O = PS[:, 6, 0:HP * VW].rearrange("p (g d) -> p g d", g=H)
                    dve.wait_ge(a_av, t + 1)
                    dve.reciprocal(rs[u], O[:, :, HD0]).then_inc(a_rc, 1)
                    dve.wait_ge(a_rc, t + 1)
                    after(dve, a_to, t - 1)
                    dve.tensor_tensor(On[u], O[:, :, 0:HD0], rs[u].unsqueeze(2).to_broadcast([128, H, HD0]), ALU.mult).then_inc(a_on, 1)

            def residual(t):
                if live(t):
                    dve.wait_ge(a_pr, t + 1)
                    dve.wait_ge(a_xb, t + 1)
                    dve.scalar_tensor_tensor(xtile(t), PS[:, 7, 128:256], gates[:, 0:1], xtile(t), ALU.mult, ALU.add).then_inc(a_res, 1)

            def step(s, u):
                for i, first in enumerate((-1, 4, 9), 1):
                    if known(s) and s == first:
                        dve.wait_ge(x_loaded[i], 16)
                maximum(s, u)
                normalise_y(s - 3, 1 - u)
                normalise(s + 2, u)
                if u == 0:
                    route(s - 6, 2)
                shift_scores(s, u)
                if u == 0:
                    route(s - 6, 3)
                scale_k(s + 1, 1 - u)
                if u == 0:
                    route(s - 6, 4)
                if known(s) and s == 0:
                    late_constants()
                residual(s - 2)
                if u == 0:
                    route(s - 6, 5)
                stats(s + 3, s - 2, u)
                if u == 0:
                    route(s - 6, 6)
                normalise_out(s - 1, 1 - u)
                if u == 0:
                    route(s - 6, 7)
                if u == 1:
                    route(s - 7, 10)
                    route(s - 5, 1)
                    route(s - 7, 11)
                    route(s - 7, 12)
                rows_for_scatter(s - 7, 1 - u)
                if u == 0:
                    route(s - 6, 8)
                    route(s - 6, 9)

            dve.wait_ge(x_loaded[0], 16)
            pipelined(dve, step, 3, 9, lo=10)
            dve.wait_ge(a_res, T)
            dve.wait_ge(r_counted, T)
            dve.tensor_scalar(ixp[:, :], rows_used[:, :], wide[:, 128:129], None, ALU.add).then_inc(pad_ix, 1)

            links = {"n": 0}

            def link(ins, sem_):
                links["n"] += 1
                ins.then_inc(sem_, 1)
                dve.wait_ge(sem_, links["n"])

            tile_no = consts[:, E0 + T:E0 + T + NS]
            e8 = [128, E0, E0]
            link(dve.tensor_tensor(cnt, rows_used[:, :], consts[:, 0:E0], ALU.subtract), m_link)
            link(dve.tensor_tensor(cmpj, cnt.unsqueeze(2).to_broadcast([128, E0, T]),
                                   consts[:, E0:E0 + T].unsqueeze(1).to_broadcast([128, E0, T]), ALU.is_gt), m_link)
            link(dve.reduce_sum(ntl, cmpj, AX.X), m_link)
            link(dve.tensor_tensor(before, tri[:, :, :], ntl.unsqueeze(1).to_broadcast(e8), ALU.mult), m_link)
            link(dve.reduce_sum(ends, before, AX.X), m_link)
            link(dve.scalar_tensor_tensor(shift, ends, -128.0, consts[:, 0:E0], ALU.mult, ALU.add), m_link)
            link(dve.tensor_tensor(ends, ends, ntl, ALU.add), m_link)
            link(dve.tensor_scalar(hop, ntl, -128.0, float(REG), ALU.mult, ALU.add), m_link)
            link(dve.tensor_tensor(past, tile_no.unsqueeze(2).to_broadcast([128, NS, E0]),
                                   ends.unsqueeze(1).to_broadcast([128, NS, E0]), ALU.is_ge), m_link)
            link(dve.reduce_sum(mapf[:, 0, :], past, AX.X), m_link)
            quads = emap[:, :].rearrange("p (i k) -> p i k", k=4)
            ef = mapf[:, 0, :].rearrange("p (i k) -> p i k", k=2)
            dve.tensor_scalar(quads[:, 0:NS // 2, 2:4], ef, float(E0 - 1), None, ALU.min).then_inc(map_ready, 1)
            dve.tensor_scalar(quads[:, 1:NS // 2 + 1, 0:2], ef, float(E0 - 1), None, ALU.min).then_inc(map_ready, 1)
            link(dve.tensor_tensor(past, past, hop.unsqueeze(1).to_broadcast([128, NS, E0]), ALU.mult), m_link)
            link(dve.reduce_sum(mapf[:, 1, :], past, AX.X), m_link)
            dve.scalar_tensor_tensor(rmap[:, :], tile_no, 128.0, mapf[:, 1, :], ALU.mult, ALU.add).then_inc(map_ready, 1)

            def weights(n):
                scales = escale_sb[:, :].unsqueeze(1).to_broadcast([128, T, E0])
                if n == 0:
                    links["n"] = 0
                    for r in range(2):
                        link(dve.scalar_tensor_tensor(pick, RK[:, :, :], float(r), PR[:, :, :], ALU.is_equal, ALU.mult), w_link)
                        link(dve.reduce_sum(p12[:, r, :], pick, AX.X), w_link)
                    dve.tensor_tensor(cw[:, 0, :], p12[:, 1, :], p12[:, 0, :], ALU.subtract).then_inc(w_dif, 1)
                if n == 1:
                    for r in range(2):
                        link(dve.scalar_tensor_tensor(pick, RK[:, :, :], float(r), scales, ALU.is_equal, ALU.mult), w_link)
                        link(dve.reduce_sum(p12[:, r, :], pick, AX.X), w_link)
                if n == 2:
                    dve.wait_ge(w_exp, 1)
                    link(dve.tensor_scalar(cw[:, 2, :], cw[:, 1, :], 1.0, None, ALU.add), w_link)
                    link(dve.reciprocal(cw[:, 0, :], cw[:, 2, :]), w_link)
                    link(dve.tensor_tensor(cw[:, 2, :], cw[:, 1, :], cw[:, 0, :], ALU.mult), w_link)
                    link(dve.tensor_tensor(CF[:, 0, :], p12[:, 0, :], cw[:, 0, :], ALU.mult), w_link)
                    link(dve.tensor_tensor(CF[:, 1, :], p12[:, 1, :], cw[:, 2, :], ALU.mult), w_link)
                if n == 3:
                    dve.wait_ge(ix_ready, T)
                    for r in range(2):
                        link(dve.scalar_tensor_tensor(pick, RK[:, :, :], float(r), shift.unsqueeze(1).to_broadcast([128, T, E0]), ALU.is_equal, ALU.mult), w_link)
                        link(dve.reduce_sum(p12[:, r, :], pick, AX.X), w_link)
                        link(dve.tensor_tensor(POS[:, :, r], POS[:, :, r], p12[:, r, :], ALU.subtract), w_link)
                    assert links["n"] == W_LINKS

            def y_t_copy(i, u):
                if live(i, NS):
                    dve.wait_ge(b_ty, i + 1)
                    after(dve, b_h, i - 1)
                    dve.tensor_copy(yTs[u], PS[:, 0, 0:128]).then_inc(b_yT, 1)

            def silu(i, u):
                if live(i, NS):
                    dve.wait_ge(b_t, i + 1)
                    after(dve, b_tu, i - 1)
                    dve.scalar_tensor_tensor(U[u], Th[u], 1.0, PS[:, 1 + u, :], ALU.add, ALU.mult).then_inc(b_u, 1)

            def slot_out(i, u):
                if live(i, NS):
                    dve.wait_ge(b_y, i + 1)
                    after(dve, o_stored[u], i * 8 - 8 * u)
                    dve.tensor_copy(OT[u], PS[:, 5 + u, 0:D]).then_inc(b_o, 1)

            def step_b(s, u):
                y_t_copy(s + 1, 1 - u)
                silu(s, u)
                slot_out(s - 2, u)
                if known(s) and 0 <= s < 4:
                    weights(s)

            pipelined(dve, step_b, 1, 2, n=NS)
            for p in range(2):
                dve.memset(KB[p], 0.0).then_inc(kb_zero, 1)
                dve.memset(VC[p], 0.0).then_inc(kb_zero, 1)

            def add_experts(t, u):
                if live(t):
                    dve.wait_ge(gathered[u], t * 16 + (32 - 16 * u))
                    dve.scalar_tensor_tensor(xtile(t), Gt[u][:, 0, :], CF[:, 0, bass.ts(t, 1)], xtile(t), ALU.mult, ALU.add).then_inc(g_add, 1)
                    dve.wait_ge(g_add, t + 1)
                    dve.scalar_tensor_tensor(xtile(t), Gt[u][:, 1, :], CF[:, 1, bass.ts(t, 1)], xtile(t), ALU.mult, ALU.add).then_inc(g_sum, 1)

            def stats_c(t, u):
                if live(t):
                    s = cst[u]
                    dve.wait_ge(ctx_loaded[u], t * 8 + (8 * T + 16 - 8 * u))
                    dve.wait_ge(g_sum, t + 1)
                    dve.memset(spare[:, 1:2], 0.0)
                    dve.bn_stats(s[:, 0:6], xtile(t)).then_inc(c_ch, 1)
                    dve.bn_stats(s[:, 6:12], cxb[u][:, :]).then_inc(c_ch, 1)
                    dve.wait_ge(c_ch, t * 2 + 2)
                    dve.memset(spare[:, 0:1], 0.0)
                    dve.bn_aggr(s[:, 12:14], s[:, 0:6])
                    dve.bn_aggr(s[:, 14:16], s[:, 6:12]).then_inc(c_mv, 1)

            def normalise_c(t, u):
                if live(t):
                    s = cst[u]
                    dve.wait_ge(c_rstd, t * 2 + 1)
                    after(dve, c_tin, t - 1)
                    dve.tensor_scalar(xn2[u][:, 0, :], xtile(t), s[:, 12:13], s[:, 18:19], ALU.subtract, ALU.mult).then_inc(c_ch2, 1)
                    dve.tensor_scalar(xn2[u][:, 1, :], cxb[u][:, :], s[:, 14:15], s[:, 19:20], ALU.subtract, ALU.mult)
                    dve.wait_ge(c_ch2, t * 2 + 1)
                    dve.bn_stats(s[:, 20:26], xn2[u][:, 0, :]).then_inc(c_ch2, 1)
                    dve.wait_ge(c_ch2, t * 2 + 2)
                    dve.memset(spare[:, 0:1], 0.0)
                    dve.bn_aggr(s[:, 28:30], s[:, 20:26]).then_inc(c_mv, 1)

            def normalise_again(t, u):
                if live(t):
                    s = cst[u]
                    dve.wait_ge(c_rstd, t * 2 + 2)
                    dve.tensor_scalar(xn2[u][:, 0, :], xn2[u][:, 0, :], s[:, 28:29], s[:, 34:35], ALU.subtract, ALU.mult).then_inc(c_xn, 1)

            def softmax_c(t, u):
                if live(t):
                    S = PS[:, 4:6, :].rearrange("p a (g m) -> p (a g) m", g=8)
                    dve.wait_ge(c_s, t + 1)
                    after(dve, c_te, t - 1)
                    dve.tensor_tensor(Ec[u], S, MK[:, bass.ts(t, 1), :].to_broadcast([128, H, SEQ]), ALU.add).then_inc(c_add, 1)
                    dve.wait_ge(c_add, t + 1)
                    dve.reduce_max(cmx[u], Ec[u], AX.X).then_inc(c_mx, 1)
                    dve.wait_ge(c_mx, t + 1)
                    dve.tensor_tensor(Ec[u], Ec[u], cmx[u].unsqueeze(2).to_broadcast([128, H, SEQ]), ALU.subtract).then_inc(c_sub, 1)

            def sums_c(t, u):
                if live(t):
                    dve.wait_ge(c_exp, t + 1)
                    dve.reduce_sum(csum[u], Ec[u], AX.X).then_inc(c_sum, 1)
                    dve.wait_ge(c_sum, t + 1)
                    dve.reciprocal(cinv[u], csum[u]).then_inc(c_inv, 1)

            def mlp_c(t, u):
                if live(t):
                    dve.wait_ge(c_t, t + 1)
                    dve.scalar_tensor_tensor(tg[u].rearrange("p a b -> p (a b)"), tg[u].rearrange("p a b -> p (a b)"), 1.0, PS[:, 3, :],
                                             ALU.add, ALU.mult).then_inc(c_g, 1)
                    dve.wait_ge(c_g, t + 1)
                    after(dve, c_out, t - 1)
                    dve.tensor_tensor(Uc[u].rearrange("p a b -> p (a b)"), tg[u].rearrange("p a b -> p (a b)"), PS[:, 2, :], ALU.mult).then_inc(c_u, 1)

            def residual_c(t):
                if live(t):
                    dve.wait_ge(c_out, t + 1)
                    dve.scalar_tensor_tensor(xtile(t), PS[:, 0, 256:384], gates[:, 1:2], xtile(t), ALU.mult, ALU.add).then_inc(c_res, 1)

            def stats_z(t, u):
                if live(t):
                    dve.wait_ge(c_res, t + 1)
                    dve.memset(spare[:, 3:4], 0.0)
                    dve.bn_stats(dst_[u][:, 0:6], xtile(t)).then_inc(d_st, 1)
                    dve.wait_ge(d_st, t + 1)
                    dve.memset(spare[:, 4:5], 0.0)
                    dve.bn_aggr(dst_[u][:, 6:8], dst_[u][:, 0:6]).then_inc(d_mv, 1)

            def normalise_z(t, u):
                if live(t):
                    dve.wait_ge(d_rstd, t + 1)
                    after(dve, d_tz, t - 1)
                    dve.tensor_scalar(zn[u], xtile(t), dst_[u][:, 6:7], dst_[u][:, 9:10], ALU.subtract, ALU.mult).then_inc(d_zn, 1)

            def step_c(s, u):
                residual_c(s - 2)
                normalise_again(s + 1, 1 - u)
                normalise_z(s - 3, 1 - u)
                softmax_c(s, u)
                mlp_c(s, u)
                sums_c(s, u)
                stats_c(s + 2, u)
                add_experts(s + 3, 1 - u)
                normalise_c(s + 2, u)
                stats_z(s - 2, u)

            pipelined(dve, step_c, 3, 3, lo=6)

            dve.wait_ge(c_res, T)
            dve.wait_ge(c_tin, T)
            ZR = RT.rearrange("p (b s) -> p b s", s=SEQ)

            def expert_out(e):
                dve.wait_ge(d_yu, 3 * (e + 1))
                dve.tensor_scalar(ZR[:, :, e * CT:(e + 1) * CT], PS[:, 4 + e % 2, :].rearrange("p (b s) -> p b s", s=CT),
                                  gates[:, 3:4], None, ALU.mult).then_inc(d_r, 1)

            for j in range(E1 * 3):
                n = F1C[j % 3][1]
                dve.wait_ge(d_t, j + 1)
                dve.scalar_tensor_tensor(Td[j % 2][0:n, :], Td[j % 2][0:n, :], 1.0, PS[0:n, 2 * (j % 2), :], ALU.add, ALU.mult).then_inc(d_g, 1)
                dve.wait_ge(d_g, j + 1)
                after(dve, d_yu, j - 2)
                dve.tensor_tensor(Ud[j % 3][0:n, :], Td[j % 2][0:n, :], PS[0:n, 2 * (j % 2) + 1, :], ALU.mult).then_inc(d_u, 1)
                if j % 3 == 1 and j >= 3:
                    expert_out(j // 3 - 1)
            expert_out(E1 - 1)
            for g in range(G):
                dve.wait_ge(d_tr, g + 1)
                dve.tensor_tensor(X[:, g * GT:(g + 1) * GT, :], PS[:, 6 + g % 2, :].rearrange("p (k d) -> p k d", k=GT),
                                  X[:, g * GT:(g + 1) * GT, :], ALU.add).then_inc(d_x, 1)

        @block.tensor
        def _(pe):
            def scores(t, u):
                if live(t):
                    pe.wait_ge(a_q, t + 1)
                    pe.wait_ge(a_ked, t + 1)
                    pe.wait_ge(a_kep, t + 1)
                    pe.wait_ge(a_kea, t + 1)
                    after(pe, a_sub, t)
                    for h in range(2):
                        for b in range(2):
                            m = pe.matmul(PS[64 * b:64 * b + 64, 2 + h, :].rearrange("p (g m) -> p g m", m=SEQ),
                                          qT[u][:, 64 * b:64 * b + 64],
                                          KE[u][:, 8 * h:8 * h + 8, 64 * b:64 * b + 64], start=True, stop=True)
                    m.then_inc(a_s, 1)

            def turn_out(t, u):
                if live(t):
                    pe.wait_ge(a_on, t + 1)
                    after(pe, a_res, t)
                    pe.transpose(PS[:, 7, 0:128], On[u].rearrange("p g d -> p (g d)"), ident[:, :]).then_inc(a_to, 1)

            def turn_y(t, u):
                if live(t):
                    pe.wait_ge(y_n, t + 1)
                    after(pe, a_xc, t * 2 + 10 if not known(t) else min(2 * T, t * 2 + 10))
                    after(pe, y_t, t)
                    pe.transpose(PS[:, 0, 256:384], yn[u], ident[:, :]).then_inc(y_tin, 1)

            def turn_in(t, u):
                if live(t):
                    pe.wait_ge(a_xn, t + 1)
                    after(pe, a_xc, t * 2)
                    after(pe, y_t, t - 5)
                    pe.wait_ge(ctx_loaded[u], t * 8 + (16 - 8 * u))
                    pe.transpose(PS[:, 0, 0:128], xn[u], ident[:, :])
                    pe.transpose(PS[:, 0, 128:256], cxb[u][:, :], ident[:, :]).then_inc(a_tin, 1)

            def turn_e(t, u):
                if live(t):
                    pe.wait_ge(a_exp, t + 1)
                    after(pe, a_et, t * 2)
                    for k in range(HP):
                        m = pe.transpose(PS[:, 4 + k // 4, 128 * (k % 4):128 * (k % 4) + 128],
                                         Ea[u][:, 2 * k:2 * k + 2, :].rearrange("p g m -> p (g m)"), ident[:, :])
                        if k % 4 == 3:
                            m.then_inc(a_te, 1)

            def project(t, u):
                if live(t):
                    pe.wait_ge(a_xc, t * 2 + 2)
                    after(pe, a_v, t * 2)
                    pe.matmul(PS[:, 1, 128:256], wk0_sb[:, :], xcT[u][:, 1, :], start=True, stop=True)
                    pe.matmul(PS[:, 1, 0:128], wq0_sb[:, :], xcT[u][:, 0, :], start=True, stop=True).then_inc(a_qk, 1)

            def project_v(t, u):
                if live(t):
                    pe.wait_ge(a_q, t + 1)
                    for b in range(2):
                        m = pe.matmul(PS[:, 1, 256 + 128 * b:384 + 128 * b], xcT[u][:, 2 + b, :], wv0_sb[:, :], start=True, stop=True)
                    m.then_inc(a_qkv, 1)

            def project_out(t, u):
                if live(t):
                    pe.wait_ge(a_ot, t + 1)
                    pe.matmul(PS[:, 7, 128:256], OTa[u], wo0_sb[:, :], start=True, stop=True).then_inc(a_pr, 1)

            def values(t, u):
                if live(t):
                    pe.wait_ge(a_v, t * 2 + 2)
                    for k in range(HP):
                        if k % 4 == 0:
                            pe.wait_ge(a_et, t * 2 + (k // 4 + 1))
                        for b in range(2):
                            m = pe.matmul(PS[64 * b:64 * b + 64, 6, VW * k:VW * k + VW], ETa[u][:, k, 64 * b:64 * b + 64],
                                          VB[u][:, b, k, :], start=True, stop=True)
                    m.then_inc(a_av, 1)

            def bank6_free(s, u):
                def upto(n):
                    return max(0, min(T, n)) if known(s) else n
                after(pe, a_on, upto(s - 1))
                after(pe, r_shift, upto(s - 4 - u))
                after(pe, r_counted, upto(s - 6 - u))

            def router(t, u):
                if live(t):
                    pe.wait_ge(y_t, t + 1)
                    pe.matmul(PS[:, 6, 256 + E0 * u:256 + E0 * u + E0], yt[u], router_sb[:, :], start=True, stop=True).then_inc(r_logits, 1)

            def count(t):
                if live(t):
                    pe.wait_ge(r_two, t + 2)
                    pe.matmul(PS[:, 6, 272:280], before_bf[:, :], ohb[:, 0, :], start=True, stop=True)
                    pe.matmul(PS[:, 6, 280:288], before_bf[:, :], ohb[:, 1, :], start=True, stop=False)
                    pe.matmul(PS[:, 6, 280:288], ones_bf[:, :], ohb[:, 0, :], start=False, stop=True)
                    pe.matmul(PS[:, 6, 288:296], ones_bf[:, :], ohb[:, 0, :], start=True, stop=False)
                    pe.matmul(PS[:, 6, 288:296], ones_bf[:, :], ohb[:, 1, :], start=False, stop=True).then_inc(r_count, 2)

            def step(s, u):
                if known(s) and s == 1:
                    pe.wait_ge(small_loaded, 16 * N_SMALL)
                    pe.wait_ge(route_const, 4)
                scores(s, u)
                turn_out(s - 2, u)
                project(s + 1, 1 - u)
                turn_e(s - 1, 1 - u)
                project_out(s - 2, u)
                project_v(s + 1, 1 - u)
                bank6_free(s, u)
                router(s - 4, u)
                if u == 1:
                    count(s - 7)
                values(s - 1, 1 - u)
                turn_y(s - 3, 1 - u)
                turn_in(s + 2, u)

            pe.wait_ge(first_loaded, 16 * N_FIRST)
            pe.wait_ge(ident_ready, 2)
            pipelined(pe, step, 2, 9, lo=10)

            def turn_slot(i, u):
                if live(i, NS):
                    pe.wait_ge(st_loaded[u], i * 8 + (16 - 8 * u))
                    after(pe, b_yT, i)
                    pe.transpose(PS[:, 0, 0:128], ST[u], ident[:, :]).then_inc(b_ty, 1)

            expert_regs = [pe.alloc_register(f"expert{k}") for k in range(4)]
            experts = [None] * 4

            def load_experts(s):
                pe.load(expert_regs, emap[0:1, bass.ds(s * 2, 4)])
                for k in range(4):
                    experts[k] = pe.snap(expert_regs[k], min_val=0, max_val=E0 - 1)

            def up(i, u, e):
                if live(i, NS):
                    pe.wait_ge(b_yT, i + 1)
                    after(pe, b_u, i - 1)
                    pe.matmul(PS[:, 1 + u, :], yTs[u], w1_sb[:, bass.ds(e, 1), :].squeeze(1), start=True, stop=True).then_inc(b_h, 1)

            def turn_u(i, u):
                if live(i, NS):
                    pe.wait_ge(b_u, i + 1)
                    after(pe, b_uT, i - 1)
                    for c in range(FC0):
                        m = pe.transpose(PS[:, 3 + u, 128 * c:128 * c + 128], U[u][:, 128 * c:128 * c + 128], ident[:, :])
                    m.then_inc(b_tu, 1)

            def down(i, u, e):
                if live(i, NS):
                    pe.wait_ge(b_uT, i + 1)
                    after(pe, b_o, i - 1)
                    for c in range(FC0):
                        m = pe.matmul(PS[:, 5 + u, 0:D], UT[u][:, c, :], w2_sb[:, bass.ds(e, 1), c, :].squeeze(1), start=(c == 0), stop=(c == FC0 - 1))
                    m.then_inc(b_y, 1)

            def step_b(s, u):
                if u == 0:
                    load_experts(s)
                up(s, u, experts[2 + u])
                turn_slot(s + 1, 1 - u)
                turn_u(s - 1, 1 - u)
                down(s - 2, u, experts[u])

            pe.wait_ge(w0_loaded, 16 * 2 * E0)
            pe.wait_ge(map_ready, 3)
            pe.wait_ge(r_counted, T)
            pipelined(pe, step_b, 1, 2, n=NS)

            def turn_in_c(t, u):
                if live(t):
                    pe.wait_ge(c_xn, t + 1)
                    after(pe, c_xc, t * 3)
                    after(pe, c_res, t - 2)
                    pe.transpose(PS[:, 0, 0:128], xn2[u][:, 0, :], ident[:, :])
                    pe.transpose(PS[:, 0, 128:256], xn2[u][:, 1, :], ident[:, :]).then_inc(c_tin, 1)

            def turn_z(t, u):
                if live(t):
                    pe.wait_ge(d_zn, t + 1)
                    after(pe, c_kve, t * 4 + 16 if not known(t) else min(4 * T, t * 4 + 16))
                    after(pe, d_zt, t)
                    pe.transpose(PS[:, 1, 384:512], zn[u], ident[:, :]).then_inc(d_tz, 1)

            def keys_values(t, u):
                if live(t):
                    pe.wait_ge(c_xc, t * 3 + 3)
                    after(pe, c_kve, t * 4)
                    after(pe, d_zt, t - 4)
                    pe.matmul(PS[:, 1, 0:128], wkv_sb[:, 0:128], xcT2[u][:, 1, :], start=True, stop=True)
                    for b in range(2):
                        m = pe.matmul(PS[:, 1, 128 + 128 * b:256 + 128 * b], xcT2[u][:, 2 + b, :], wkv_sb[:, 128:256], start=True, stop=True)
                    m.then_inc(c_kv, 1)

            def queries(t, u):
                if live(t):
                    after(pe, c_u, t)
                    for k in range(HP):
                        m = pe.matmul(PS[:, 2 + k // 4, 128 * (k % 4):128 * (k % 4) + 128], wq1_sb[:, 128 * k:128 * k + 128],
                                      xcT2[u][:, 0, :], start=True, stop=True)
                        if k % 4 == 3:
                            m.then_inc(c_q, 1)

            def scores_c(t, u):
                if live(t):
                    pe.wait_ge(c_kve, t * 4 + 4)
                    after(pe, c_sub, t)
                    for k in range(HP):
                        if k % 4 == 0:
                            pe.wait_ge(c_qe, t * 2 + (k // 4 + 1))
                        for b in range(2):
                            m = pe.matmul(PS[64 * b:64 * b + 64, 4 + k // 4, 128 * (k % 4):128 * (k % 4) + 128],
                                          QT[u][:, k, 64 * b:64 * b + 64], KB[u][:, b, :, :].rearrange("p k m -> p (k m)"),
                                          start=True, stop=True)
                    m.then_inc(c_s, 1)

            def turn_e_c(t, u):
                if live(t):
                    pe.wait_ge(c_nrm, t + 1)
                    after(pe, c_ot, t)
                    for k in range(HP):
                        m = pe.transpose(PS[:, 6 + k // 4, 128 * (k % 4):128 * (k % 4) + 128],
                                         Ec[u][:, 2 * k:2 * k + 2, :].rearrange("p g m -> p (g m)"), ident[:, :])
                    m.then_inc(c_te, 1)

            def mlp_up(t, u):
                if live(t):
                    pe.wait_ge(c_qe, t * 2 + 2)
                    for k in range(2 * MC):
                        m = pe.matmul(PS[:, 2 + k // 4, 128 * (k % 4):128 * (k % 4) + 128], w1m_sb[:, 128 * k:128 * k + 128],
                                      xcT2[u][:, 0, :], start=True, stop=True)
                    m.then_inc(c_h, 1)

            def values_c(t, u):
                if live(t):
                    pe.wait_ge(c_et, t + 1)
                    for b in range(2):
                        m = pe.matmul(PS[:, 6 + b, :].rearrange("p (t l) -> p t l", t=HP), VC[u][:, b, :, :].rearrange("p k d -> p (k d)"),
                                      ETc[u][:, :, 64 * b:64 * b + 64], start=True, stop=True)
                    m.then_inc(c_o, 1)

            def project_c(t, u, first):
                if live(t):
                    if first:
                        pe.wait_ge(c_u, t + 1)
                        after(pe, c_res, t)
                        for k in range(MC):
                            pe.matmul(PS[:, 0, 256:384], Uc[u][:, k, :], w2m_sb[:, k, :], start=(k == 0), stop=False)
                        pe.wait_ge(c_ot, t + 1)
                    for k in range(0, OUT1) if first else range(OUT1, HP):
                        m = pe.matmul(PS[:, 0, 256:384], OTc[u][:, k, :], wout_sb[:, k, :], start=False, stop=(k == HP - 1))
                    if not first:
                        m.then_inc(c_out, 1)

            def step_c(s, u):
                scores_c(s, u)
                turn_e_c(s - 1, 1 - u)
                turn_in_c(s + 1, 1 - u)
                mlp_up(s, u)
                values_c(s - 1, 1 - u)
                turn_z(s - 3, 1 - u)
                keys_values(s + 1, 1 - u)
                project_c(s - 1, 1 - u, True)
                queries(s + 1, 1 - u)
                project_c(s - 1, 1 - u, False)

            pe.wait_ge(w1l_loaded, 16 * 4 * 8)
            pe.wait_ge(b_o, NS)
            pe.wait_ge(const_ready, 5)
            pipelined(pe, step_c, 1, 3, lo=6)

            Z = ZT.rearrange("p (b s) -> p b s", s=SEQ)

            def up_d(j):
                e, (f, n) = j // 3, F1C[j % 3]
                after(pe, d_u, j - 1)
                z = Z[:, :, e * CT:(e + 1) * CT]
                for i, w in enumerate((w1e_sb, w3e_sb)):
                    m = pe.matmul(PS[0:n, 2 * (j % 2) + i, :].rearrange("p (b s) -> p b s", s=CT), w[:, e, f:f + n], z, start=True, stop=True)
                m.then_inc(d_h, 1)

            def down_d(j):
                e, c = j // 3, j % 3
                n = F1C[c][1]
                pe.wait_ge(d_u, j + 1)
                if c == 0:
                    after(pe, d_r, e - 1)
                pe.matmul(PS[:, 4 + e % 2, :], w2e_sb[0:n, e, c, :], Ud[j % 3][0:n, :], start=(c == 0), stop=(c == 2)).then_inc(d_yu, 1)

            pe.wait_ge(wd_loaded, 16 * 5 * E1)
            pe.wait_ge(d_zt, T)
            up_d(0)
            for j in range(E1 * 3):
                if j + 1 < E1 * 3:
                    up_d(j + 1)
                down_d(j)
            pe.wait_ge(d_r, E1)
            for g in range(G):
                after(pe, d_x, g - 1)
                for k in range(GT):
                    t = g * GT + k
                    m = pe.transpose(PS[:, 6 + g % 2, 128 * k:128 * k + 128], RT[:, 128 * t:128 * t + 128], ident[:, :])
                m.then_inc(d_tr, 1)


def kernel(**inputs):
    import numpy as np
    import concourse.bacc as bacc
    from concourse.bass_utils import run_bass_kernel_spmd

    a = {k: np.asarray(v) for k, v in inputs.items()}
    wk, wv = np.split(a["L1_xattn_Wkv"], 2, axis=1)
    laid = [
        ("x", a["x"]), ("ctx_in", a["ctx_1024"]), ("mask", a["mask_BxSxS2_ff0"]), ("g_xattn", a["g_xattn"]), ("g_ffn", a["g_ffn"]),
        ("wqT0", a["L0_xattn_Wq"].T), ("bq0", a["L0_xattn_bq"]), ("wkT0", a["L0_xattn_Wk"].T), ("bk0", a["L0_xattn_bk"]),
        ("wvT0", a["L0_xattn_Wv"].T), ("bv0", a["L0_xattn_bv"]), ("woT0", a["L0_xattn_Wo"].T), ("bo0", a["L0_xattn_bo"]),
        ("P0", np.repeat(a["L0_xattn_P"], HD0, axis=0)), ("routerT", a["L0_ffn_router_w"].T),
        ("w1T0", a["L0_ffn_w1"].transpose(2, 0, 1)),
        ("w2T0", a["L0_ffn_w2"].reshape(E0, D, FC0, 128).transpose(3, 0, 2, 1)),
        ("escale", a["L0_ffn_expert_scale"]),
        ("ln_g", a["L1_xattn_ln_g"]), ("ln_b", a["L1_xattn_ln_b"]), ("cln_g", a["L1_xattn_cln_g"]), ("cln_b", a["L1_xattn_cln_b"]),
        ("wq1", a["L1_xattn_Wq"]), ("wkv1", np.concatenate([wk, wk, wv, wv], axis=1)), ("wout1", a["L1_xattn_Wout"]),
        ("w1m", a["L1_xattn_W1"]), ("w2m", a["L1_xattn_W2"]),
        ("w1e", a["L1_ffn_w1"].transpose(1, 0, 2)), ("w3e", a["L1_ffn_w3"].transpose(1, 0, 2)), ("w2e", a["L1_ffn_w2"]),
    ]
    consts = np.zeros((129, 129), np.float32)
    consts[0, 0:E0] = np.arange(E0) * REG
    consts[0, E0:E0 + T] = np.arange(T) * 128
    consts[0, E0 + T:E0 + T + NS] = np.arange(NS)
    consts[1:, 0:128] = np.triu(np.ones((128, 128)), 1)
    consts[1:, 128] = np.arange(128)
    laid.append(("shape_consts", consts))
    nc = bacc.Bacc("TRN2", target_bir_lowering=False, num_devices=1)
    arrays, args = {}, []
    for name, v in laid:
        v = np.ascontiguousarray(v)
        arrays[name] = v
        args.append(nc.dram_tensor(name, v.shape, mybir.dt.from_np(v.dtype), kind="ExternalInput").ap())
    args.append(nc.dram_tensor("out", a["x"].shape, F32, kind="ExternalOutput").ap())
    for name, rows in (("y_rows", ROWS), ("o_rows", NS * 128)):
        args.append(nc.dram_tensor(name, [rows, D], F32).ap())
    build(nc, *args)
    r = run_bass_kernel_spmd(nc, [arrays], core_ids=[0])
    return r.results[0]["out"]
```
